# Optimizing a Trainium2 kernel written in Bass

```python
import numpy as np
import jax
import jax.numpy as jnp

def _softmax(x, axis=-1):
    return jax.nn.softmax(x, axis=axis)

def _gelu(x):
    return jax.nn.gelu(x, approximate=True)

def _silu(x):
    return jax.nn.silu(x)

def _sigmoid(x):
    return jax.nn.sigmoid(x)

def _layernorm(x, axis=-1, eps=1e-05):
    m = jnp.mean(x, axis=axis, keepdims=True)
    v = jnp.var(x, axis=axis, keepdims=True)
    return (x - m) / jnp.sqrt(v + eps)

def _scatter_add(tgt, idx, src, axis=0):
    return tgt.at[idx].add(src)

def _segment_sum(src, seg, n):
    return jax.ops.segment_sum(src, seg, n)
kernel_name = 'mk_cond_seq_d4_seqx_r4_b946c6'

def setup_inputs(seed: int=0):
    np.random.seed(seed)
    _w = jnp.asarray

    def _rec_inputs():
        import jax
        import jax.numpy as jnp
        _rk = jax.random.key(seed)
        x = 7.22e-05 + 1 * jax.random.normal(jax.random.fold_in(_rk, 1), (4, 512, 256), jnp.float32)
        _lenS = 512 - jax.random.randint(jax.random.fold_in(_rk, 7), (4,), 0, max(1, 512 // 4) + 1, jnp.int32)
        _lenS2 = 512 - jax.random.randint(jax.random.fold_in(_rk, 8), (4,), 0, max(1, 512 // 4) + 1, jnp.int32)
        cond_1024 = 0.0061147 + 1.02565 * jax.random.normal(jax.random.fold_in(_rk, 11), (4, 256), jnp.float32)
        return (x, cond_1024)
    x, cond_1024 = _rec_inputs()

    def _L0_cond_setup():
        import jax, jax.numpy as jnp
        import numpy as np
        DIM = 256
        MLP_RATIO = 4
        EPS = 1e-06

        def rmsnorm(x, w):
            return x * jax.lax.rsqrt(jnp.mean(x * x, axis=-1, keepdims=True) + EPS) * w

        def film(x, cond, w, b):
            ss = cond @ w + b
            scale, shift = jnp.split(ss, 2, axis=-1)
            return x * (1.0 + scale[:, None, :]) + shift[:, None, :]
        key = jax.random.key(seed)
        ks = jax.random.split(key, 16)
        B, N, D = (4, 512, DIM)
        H = D * MLP_RATIO
        s = lambda fan_in: 1.0 / np.sqrt(fan_in)
        return {'x': jax.random.normal(ks[0], (B, N, D), jnp.float32), 'cond': jax.random.normal(ks[1], (B, D), jnp.float32), 'norm1_w': jnp.ones((D,), jnp.float32), 'film1_w': jax.random.normal(ks[2], (D, 2 * D), jnp.float32) * s(D), 'film1_b': jnp.zeros((2 * D,), jnp.float32), 'q_w': jax.random.normal(ks[3], (D, D), jnp.float32) * s(D), 'q_b': jnp.zeros((D,), jnp.float32), 'k_w': jax.random.normal(ks[4], (D, D), jnp.float32) * s(D), 'k_b': jnp.zeros((D,), jnp.float32), 'v_w': jax.random.normal(ks[5], (D, D), jnp.float32) * s(D), 'v_b': jnp.zeros((D,), jnp.float32), 'proj_w': jax.random.normal(ks[6], (D, D), jnp.float32) * s(D), 'proj_b': jnp.zeros((D,), jnp.float32), 'norm2_w': jnp.ones((D,), jnp.float32), 'film2_w': jax.random.normal(ks[7], (D, 2 * D), jnp.float32) * s(D), 'film2_b': jnp.zeros((2 * D,), jnp.float32), 'mlp_w1': jax.random.normal(ks[8], (D, H), jnp.float32) * s(D), 'mlp_b1': jnp.zeros((H,), jnp.float32), 'mlp_w2': jax.random.normal(ks[9], (H, D), jnp.float32) * s(H), 'mlp_b2': jnp.zeros((D,), jnp.float32)}
    _L0_cond_all = _L0_cond_setup()
    _L0_cond_in = {k: v for k, v in _L0_cond_all.items() if k in ('norm1_w', 'film1_w', 'film1_b', 'q_w', 'q_b', 'k_w', 'k_b', 'v_w', 'v_b', 'proj_w', 'proj_b', 'norm2_w', 'film2_w', 'film2_b', 'mlp_w1', 'mlp_b1', 'mlp_w2', 'mlp_b2')}
    del _L0_cond_all

    def _L1_cond_setup():
        import jax, jax.numpy as jnp
        import numpy as np
        EPS_LN = 1e-06
        EPS_NORM = 1e-12
        MAX_SCALE_MUL = float(np.log(100.0))
        H = 16

        def _ln(x):
            mu = jnp.mean(x, axis=-1, keepdims=True)
            var = jnp.mean((x - mu) ** 2, axis=-1, keepdims=True)
            return (x - mu) / jnp.sqrt(var + EPS_LN)

        def _l2norm(x):
            n = jnp.sqrt(jnp.sum(x * x, axis=-1, keepdims=True))
            return x / jnp.maximum(n, EPS_NORM)
        key = jax.random.key(seed)
        ks = jax.random.split(key, 12)
        B, L, C = (4, 256, 256)
        Ccond, Dff = (256, 1024)
        s = lambda fan: 1.0 / np.sqrt(fan)
        return {'x': jax.random.normal(ks[0], (B, L, C), jnp.float32), 'cond': jax.random.normal(ks[1], (B, Ccond), jnp.float32), 'mat_qkv_w': jax.random.normal(ks[2], (3 * C, C), jnp.float32) * s(C), 'q_bias': jnp.zeros((C,), jnp.float32), 'v_bias': jnp.zeros((C,), jnp.float32), 'scale_mul': jnp.full((1, H, 1, 1), np.log(4.0), jnp.float32), 'proj_w': jax.random.normal(ks[3], (C, C), jnp.float32) * s(C), 'proj_b': jnp.zeros((C,), jnp.float32), 'ada_w': jax.random.normal(ks[4], (6 * C, Ccond), jnp.float32) * s(Ccond), 'ada_b': jnp.zeros((6 * C,), jnp.float32), 'fc1_w': jax.random.normal(ks[5], (Dff, C), jnp.float32) * s(C), 'fc1_b': jnp.zeros((Dff,), jnp.float32), 'fc2_w': jax.random.normal(ks[6], (C, Dff), jnp.float32) * s(Dff), 'fc2_b': jnp.zeros((C,), jnp.float32)}
    _L1_cond_all = _L1_cond_setup()
    _L1_cond_in = {k: v for k, v in _L1_cond_all.items() if k in ('mat_qkv_w', 'q_bias', 'v_bias', 'scale_mul', 'proj_w', 'proj_b', 'ada_w', 'ada_b', 'fc1_w', 'fc1_b', 'fc2_w', 'fc2_b')}
    del _L1_cond_all

    def _L2_cond_setup():
        import jax, jax.numpy as jnp
        import numpy as np
        D = 256
        H = 16
        HD = D // H
        MLP = 4 * D

        def _lin(key, fin, fout):
            k1, k2 = jax.random.split(key)
            lim = 1.0 / np.sqrt(fin)
            W = jax.random.uniform(k1, (fin, fout), minval=-lim, maxval=lim, dtype=jnp.float32)
            b = jax.random.uniform(k2, (fout,), minval=-lim, maxval=lim, dtype=jnp.float32)
            return (W, b)

        def layernorm(x, g, b, eps=1e-05):
            mu = jnp.mean(x, axis=-1, keepdims=True)
            var = jnp.var(x, axis=-1, keepdims=True)
            return (x - mu) * jax.lax.rsqrt(var + eps) * g + b

        def attention(h, Wqkv, bqkv, Wproj, bproj):
            B, L, _ = h.shape
            qkv = (h @ Wqkv + bqkv).reshape(B, L, 3, H, HD)
            q, k, v = jnp.moveaxis(qkv, 2, 0)
            scale = HD ** (-0.5)
            attn = jnp.einsum('blhd,bmhd->bhlm', q, k) * scale
            attn = jax.nn.softmax(attn, axis=-1)
            out = jnp.einsum('bhlm,bmhd->blhd', attn, v).reshape(B, L, D)
            return out @ Wproj + bproj
        key = jax.random.key(seed)
        ks = jax.random.split(key, 10)
        x = jax.random.normal(ks[0], (4, 512, D), dtype=jnp.float32)
        time_emb = jax.random.normal(ks[1], (4, D), dtype=jnp.float32)
        Wqkv, bqkv = _lin(ks[2], D, 3 * D)
        Wproj, bproj = _lin(ks[3], D, D)
        W1, b1 = _lin(ks[4], D, MLP)
        W2, b2 = _lin(ks[5], MLP, D)
        Wt, bt = _lin(ks[6], D, 6 * D)
        g1 = jnp.ones((D,), jnp.float32)
        be1 = jnp.zeros((D,), jnp.float32)
        g2 = jnp.ones((D,), jnp.float32)
        be2 = jnp.zeros((D,), jnp.float32)
        return {'x': x, 'time_emb': time_emb, 'Wqkv': Wqkv, 'bqkv': bqkv, 'Wproj': Wproj, 'bproj': bproj, 'W1': W1, 'b1': b1, 'W2': W2, 'b2': b2, 'Wt': Wt, 'bt': bt, 'g1': g1, 'be1': be1, 'g2': g2, 'be2': be2}
    _L2_cond_all = _L2_cond_setup()
    _L2_cond_in = {k: v for k, v in _L2_cond_all.items() if k in ('Wqkv', 'bqkv', 'Wproj', 'bproj', 'W1', 'b1', 'W2', 'b2', 'Wt', 'bt', 'g1', 'be1', 'g2', 'be2')}
    del _L2_cond_all

    def _L3_cond_setup():
        import jax, jax.numpy as jnp
        import numpy as np
        EPS = 1e-05

        def _sln(h, w, ln_g, ln_b, Wg, bg, Wb, bb):
            mu = jnp.mean(h, axis=-1, keepdims=True)
            var = jnp.mean((h - mu) ** 2, axis=-1, keepdims=True)
            ln = (h - mu) / jnp.sqrt(var + EPS) * ln_g + ln_b
            gamma = (w @ Wg.T + bg)[:, None, :]
            beta = (w @ Wb.T + bb)[:, None, :]
            return gamma * ln + beta
        key = jax.random.key(seed)
        ks = jax.random.split(key, 20)
        B, N, D = (4, 256, 256)
        F = 4 * D
        s = lambda fan: 1.0 / np.sqrt(fan)
        inp = {'hidden': jax.random.normal(ks[0], (B, N, D), jnp.float32), 'w': jax.random.normal(ks[1], (B, D), jnp.float32), 'ln_g': jnp.ones((D,), jnp.float32), 'ln_b': jnp.zeros((D,), jnp.float32), 'Wg': jax.random.normal(ks[2], (D, D), jnp.float32) * s(D), 'bg': jnp.zeros((D,), jnp.float32), 'Wb': jax.random.normal(ks[3], (D, D), jnp.float32) * s(D), 'bb': jnp.zeros((D,), jnp.float32), 'Wqkv': jax.random.normal(ks[4], (3 * D, D), jnp.float32) * s(D), 'bqkv': jnp.zeros((3 * D,), jnp.float32), 'Wp': jax.random.normal(ks[5], (D, D), jnp.float32) * s(D), 'bp': jnp.zeros((D,), jnp.float32), 'W1': jax.random.normal(ks[6], (F, D), jnp.float32) * s(D), 'b1': jnp.zeros((F,), jnp.float32), 'W2': jax.random.normal(ks[7], (D, F), jnp.float32) * s(F), 'b2': jnp.zeros((D,), jnp.float32), 'num_heads': 16}
        return inp
    _L3_cond_all = _L3_cond_setup()
    _L3_cond_in = {k: v for k, v in _L3_cond_all.items() if k in ('ln_g', 'ln_b', 'Wg', 'bg', 'Wb', 'bb', 'Wqkv', 'bqkv', 'Wp', 'bp', 'W1', 'b1', 'W2', 'b2')}
    del _L3_cond_all
    return {'x': x, 'cond_1024': cond_1024, 'L0_cond_norm1_w': _L0_cond_in['norm1_w'], 'L0_cond_film1_w': _L0_cond_in['film1_w'], 'L0_cond_film1_b': _L0_cond_in['film1_b'], 'L0_cond_q_w': _L0_cond_in['q_w'], 'L0_cond_q_b': _L0_cond_in['q_b'], 'L0_cond_k_w': _L0_cond_in['k_w'], 'L0_cond_k_b': _L0_cond_in['k_b'], 'L0_cond_v_w': _L0_cond_in['v_w'], 'L0_cond_v_b': _L0_cond_in['v_b'], 'L0_cond_proj_w': _L0_cond_in['proj_w'], 'L0_cond_proj_b': _L0_cond_in['proj_b'], 'L0_cond_norm2_w': _L0_cond_in['norm2_w'], 'L0_cond_film2_w': _L0_cond_in['film2_w'], 'L0_cond_film2_b': _L0_cond_in['film2_b'], 'L0_cond_mlp_w1': _L0_cond_in['mlp_w1'], 'L0_cond_mlp_b1': _L0_cond_in['mlp_b1'], 'L0_cond_mlp_w2': _L0_cond_in['mlp_w2'], 'L0_cond_mlp_b2': _L0_cond_in['mlp_b2'], 'L1_cond_mat_qkv_w': _L1_cond_in['mat_qkv_w'], 'L1_cond_q_bias': _L1_cond_in['q_bias'], 'L1_cond_v_bias': _L1_cond_in['v_bias'], 'L1_cond_scale_mul': _L1_cond_in['scale_mul'], 'L1_cond_proj_w': _L1_cond_in['proj_w'], 'L1_cond_proj_b': _L1_cond_in['proj_b'], 'L1_cond_ada_w': _L1_cond_in['ada_w'], 'L1_cond_ada_b': _L1_cond_in['ada_b'], 'L1_cond_fc1_w': _L1_cond_in['fc1_w'], 'L1_cond_fc1_b': _L1_cond_in['fc1_b'], 'L1_cond_fc2_w': _L1_cond_in['fc2_w'], 'L1_cond_fc2_b': _L1_cond_in['fc2_b'], 'L2_cond_Wqkv': _L2_cond_in['Wqkv'], 'L2_cond_bqkv': _L2_cond_in['bqkv'], 'L2_cond_Wproj': _L2_cond_in['Wproj'], 'L2_cond_bproj': _L2_cond_in['bproj'], 'L2_cond_W1': _L2_cond_in['W1'], 'L2_cond_b1': _L2_cond_in['b1'], 'L2_cond_W2': _L2_cond_in['W2'], 'L2_cond_b2': _L2_cond_in['b2'], 'L2_cond_Wt': _L2_cond_in['Wt'], 'L2_cond_bt': _L2_cond_in['bt'], 'L2_cond_g1': _L2_cond_in['g1'], 'L2_cond_be1': _L2_cond_in['be1'], 'L2_cond_g2': _L2_cond_in['g2'], 'L2_cond_be2': _L2_cond_in['be2'], 'L3_cond_ln_g': _L3_cond_in['ln_g'], 'L3_cond_ln_b': _L3_cond_in['ln_b'], 'L3_cond_Wg': _L3_cond_in['Wg'], 'L3_cond_bg': _L3_cond_in['bg'], 'L3_cond_Wb': _L3_cond_in['Wb'], 'L3_cond_bb': _L3_cond_in['bb'], 'L3_cond_Wqkv': _L3_cond_in['Wqkv'], 'L3_cond_bqkv': _L3_cond_in['bqkv'], 'L3_cond_Wp': _L3_cond_in['Wp'], 'L3_cond_bp': _L3_cond_in['bp'], 'L3_cond_W1': _L3_cond_in['W1'], 'L3_cond_b1': _L3_cond_in['b1'], 'L3_cond_W2': _L3_cond_in['W2'], 'L3_cond_b2': _L3_cond_in['b2']}

def reference(x, cond_1024, L0_cond_norm1_w, L0_cond_film1_w, L0_cond_film1_b, L0_cond_q_w, L0_cond_q_b, L0_cond_k_w, L0_cond_k_b, L0_cond_v_w, L0_cond_v_b, L0_cond_proj_w, L0_cond_proj_b, L0_cond_norm2_w, L0_cond_film2_w, L0_cond_film2_b, L0_cond_mlp_w1, L0_cond_mlp_b1, L0_cond_mlp_w2, L0_cond_mlp_b2, L1_cond_mat_qkv_w, L1_cond_q_bias, L1_cond_v_bias, L1_cond_scale_mul, L1_cond_proj_w, L1_cond_proj_b, L1_cond_ada_w, L1_cond_ada_b, L1_cond_fc1_w, L1_cond_fc1_b, L1_cond_fc2_w, L1_cond_fc2_b, L2_cond_Wqkv, L2_cond_bqkv, L2_cond_Wproj, L2_cond_bproj, L2_cond_W1, L2_cond_b1, L2_cond_W2, L2_cond_b2, L2_cond_Wt, L2_cond_bt, L2_cond_g1, L2_cond_be1, L2_cond_g2, L2_cond_be2, L3_cond_ln_g, L3_cond_ln_b, L3_cond_Wg, L3_cond_bg, L3_cond_Wb, L3_cond_bb, L3_cond_Wqkv, L3_cond_bqkv, L3_cond_Wp, L3_cond_bp, L3_cond_W1, L3_cond_b1, L3_cond_W2, L3_cond_b2):
    import jax
    import jax.numpy as jnp

    def _L0_cond_ref(x, cond, norm1_w, film1_w, film1_b, q_w, q_b, k_w, k_b, v_w, v_b, proj_w, proj_b, norm2_w, film2_w, film2_b, mlp_w1, mlp_b1, mlp_w2, mlp_b2):
        import jax, jax.numpy as jnp
        import numpy as np
        DIM = 256
        MLP_RATIO = 4
        EPS = 1e-06

        def rmsnorm(x, w):
            return x * jax.lax.rsqrt(jnp.mean(x * x, axis=-1, keepdims=True) + EPS) * w

        def film(x, cond, w, b):
            ss = cond @ w + b
            scale, shift = jnp.split(ss, 2, axis=-1)
            return x * (1.0 + scale[:, None, :]) + shift[:, None, :]
        B, N, D = x.shape
        x_in = x
        h = film(rmsnorm(x, norm1_w), cond, film1_w, film1_b)
        Q = h @ q_w + q_b
        K = h @ k_w + k_b
        V = h @ v_w + v_b
        scores = jnp.einsum('bnd,bmd->bnm', Q, K) * D ** (-0.5)
        attn = jax.nn.softmax(scores, axis=-1)
        out = jnp.einsum('bnm,bmd->bnd', attn, V)
        x = x_in + (out @ proj_w + proj_b)
        x_in = x
        h = film(rmsnorm(x, norm2_w), cond, film2_w, film2_b)
        h = jax.nn.gelu(h @ mlp_w1 + mlp_b1, approximate=False) @ mlp_w2 + mlp_b2
        return x_in + h

    def _L1_cond_ref(x, cond, mat_qkv_w, q_bias, v_bias, scale_mul, proj_w, proj_b, ada_w, ada_b, fc1_w, fc1_b, fc2_w, fc2_b):
        import jax, jax.numpy as jnp
        import numpy as np
        EPS_LN = 1e-06
        EPS_NORM = 1e-12
        MAX_SCALE_MUL = float(np.log(100.0))
        H = 16

        def _ln(x):
            mu = jnp.mean(x, axis=-1, keepdims=True)
            var = jnp.mean((x - mu) ** 2, axis=-1, keepdims=True)
            return (x - mu) / jnp.sqrt(var + EPS_LN)

        def _l2norm(x):
            n = jnp.sqrt(jnp.sum(x * x, axis=-1, keepdims=True))
            return x / jnp.maximum(n, EPS_NORM)
        B, L, C = x.shape
        hd = C // H
        ada = jax.nn.silu(cond) @ ada_w.T + ada_b
        ada = ada.reshape(B, 1, 6, C)
        gamma1, gamma2, scale1, scale2, shift1, shift2 = [ada[:, :, i] for i in range(6)]
        x1 = _ln(x) * (scale1 + 1.0) + shift1
        qkv_bias = jnp.concatenate([q_bias, jnp.zeros_like(q_bias), v_bias])
        qkv = (x1 @ mat_qkv_w.T + qkv_bias).reshape(B, L, 3, H, hd)
        q, k, v = [jnp.transpose(qkv[:, :, i], (0, 2, 1, 3)) for i in range(3)]
        sm = jnp.exp(jnp.minimum(scale_mul, MAX_SCALE_MUL))
        q = _l2norm(q) * sm
        k = _l2norm(k)
        scores = jnp.einsum('bhqd,bhkd->bhqk', q, k)
        probs = jax.nn.softmax(scores, axis=-1)
        o = jnp.einsum('bhqk,bhkd->bhqd', probs, v)
        o = jnp.transpose(o, (0, 2, 1, 3)).reshape(B, L, C)
        attn_out = o @ proj_w.T + proj_b
        x = x + attn_out * gamma1
        x2 = _ln(x) * (scale2 + 1.0) + shift2
        h = jax.nn.gelu(x2 @ fc1_w.T + fc1_b, approximate=False)
        ffn_out = h @ fc2_w.T + fc2_b
        x = x + ffn_out * gamma2
        return x

    def _L2_cond_ref(x, time_emb, Wqkv, bqkv, Wproj, bproj, W1, b1, W2, b2, Wt, bt, g1, be1, g2, be2):
        import jax, jax.numpy as jnp
        import numpy as np
        D = 256
        H = 16
        HD = D // H
        MLP = 4 * D

        def _lin(key, fin, fout):
            k1, k2 = jax.random.split(key)
            lim = 1.0 / np.sqrt(fin)
            W = jax.random.uniform(k1, (fin, fout), minval=-lim, maxval=lim, dtype=jnp.float32)
            b = jax.random.uniform(k2, (fout,), minval=-lim, maxval=lim, dtype=jnp.float32)
            return (W, b)

        def layernorm(x, g, b, eps=1e-05):
            mu = jnp.mean(x, axis=-1, keepdims=True)
            var = jnp.var(x, axis=-1, keepdims=True)
            return (x - mu) * jax.lax.rsqrt(var + eps) * g + b

        def attention(h, Wqkv, bqkv, Wproj, bproj):
            B, L, _ = h.shape
            qkv = (h @ Wqkv + bqkv).reshape(B, L, 3, H, HD)
            q, k, v = jnp.moveaxis(qkv, 2, 0)
            scale = HD ** (-0.5)
            attn = jnp.einsum('blhd,bmhd->bhlm', q, k) * scale
            attn = jax.nn.softmax(attn, axis=-1)
            out = jnp.einsum('bhlm,bmhd->blhd', attn, v).reshape(B, L, D)
            return out @ Wproj + bproj
        tp = (jax.nn.silu(time_emb) @ Wt + bt)[:, None, :]
        shift_msa, scale_msa, gate_msa, shift_mlp, scale_mlp, gate_mlp = jnp.split(tp, 6, axis=-1)
        h = layernorm(x, g1, be1)
        h = h * (1.0 + scale_msa) + shift_msa
        h = attention(h, Wqkv, bqkv, Wproj, bproj)
        x = x + gate_msa * h
        h = layernorm(x, g2, be2)
        h = h * (1.0 + scale_mlp) + shift_mlp
        h = jax.nn.gelu(h @ W1 + b1, approximate=False) @ W2 + b2
        x = x + gate_mlp * h
        return x

    def _L3_cond_ref(hidden, w, ln_g, ln_b, Wg, bg, Wb, bb, Wqkv, bqkv, Wp, bp, W1, b1, W2, b2, num_heads):
        import jax, jax.numpy as jnp
        import numpy as np
        EPS = 1e-05

        def _sln(h, w, ln_g, ln_b, Wg, bg, Wb, bb):
            mu = jnp.mean(h, axis=-1, keepdims=True)
            var = jnp.mean((h - mu) ** 2, axis=-1, keepdims=True)
            ln = (h - mu) / jnp.sqrt(var + EPS) * ln_g + ln_b
            gamma = (w @ Wg.T + bg)[:, None, :]
            beta = (w @ Wb.T + bb)[:, None, :]
            return gamma * ln + beta
        B, N, D = hidden.shape
        hd = D // num_heads
        h = _sln(hidden, w, ln_g, ln_b, Wg, bg, Wb, bb)
        qkv = (h @ Wqkv.T + bqkv).reshape(B, N, num_heads, hd, 3)
        q = jnp.moveaxis(qkv[..., 0], 2, 1)
        k = jnp.moveaxis(qkv[..., 1], 2, 1)
        v = jnp.moveaxis(qkv[..., 2], 2, 1)
        energy = jnp.einsum('bhqd,bhkd->bhqk', q, k)
        att = jax.nn.softmax(energy, axis=-1) / D ** 0.5
        out = jnp.einsum('bhqk,bhkd->bhqd', att, v)
        out = jnp.moveaxis(out, 1, 2).reshape(B, N, D)
        out = out @ Wp.T + bp
        h1 = out + hidden
        h2 = _sln(h1, w, ln_g, ln_b, Wg, bg, Wb, bb)
        return h2 + h1
    x = _L0_cond_ref(x, cond_1024, L0_cond_norm1_w, L0_cond_film1_w, L0_cond_film1_b, L0_cond_q_w, L0_cond_q_b, L0_cond_k_w, L0_cond_k_b, L0_cond_v_w, L0_cond_v_b, L0_cond_proj_w, L0_cond_proj_b, L0_cond_norm2_w, L0_cond_film2_w, L0_cond_film2_b, L0_cond_mlp_w1, L0_cond_mlp_b1, L0_cond_mlp_w2, L0_cond_mlp_b2)
    x = _L1_cond_ref(x, cond_1024, L1_cond_mat_qkv_w, L1_cond_q_bias, L1_cond_v_bias, L1_cond_scale_mul, L1_cond_proj_w, L1_cond_proj_b, L1_cond_ada_w, L1_cond_ada_b, L1_cond_fc1_w, L1_cond_fc1_b, L1_cond_fc2_w, L1_cond_fc2_b)
    x = _L2_cond_ref(x, cond_1024, L2_cond_Wqkv, L2_cond_bqkv, L2_cond_Wproj, L2_cond_bproj, L2_cond_W1, L2_cond_b1, L2_cond_W2, L2_cond_b2, L2_cond_Wt, L2_cond_bt, L2_cond_g1, L2_cond_be1, L2_cond_g2, L2_cond_be2)
    x = _L3_cond_ref(x, cond_1024, L3_cond_ln_g, L3_cond_ln_b, L3_cond_Wg, L3_cond_bg, L3_cond_Wb, L3_cond_bb, L3_cond_Wqkv, L3_cond_bqkv, L3_cond_Wp, L3_cond_bp, L3_cond_W1, L3_cond_b1, L3_cond_W2, L3_cond_b2, 16)
    return x

_drawn_inputs = setup_inputs


def setup_inputs(seed=0):
    import zlib

    import numpy as np

    out = dict(_drawn_inputs(seed))
    spreads = {'L0_cond_norm1_w': (1.0, 0.2),
     'L0_cond_film1_b': (0.0, 0.1),
     'L0_cond_q_b': (0.0, 0.314),
     'L0_cond_k_b': (0.0, 2.0),
     'L0_cond_v_b': (0.0, 0.1),
     'L0_cond_proj_b': (0.0, 0.1),
     'L0_cond_norm2_w': (1.0, 0.2),
     'L0_cond_film2_b': (0.0, 0.1),
     'L0_cond_mlp_b1': (0.0, 0.1),
     'L0_cond_mlp_b2': (0.0, 0.1),
     'L1_cond_q_bias': (0.0, 0.8),
     'L1_cond_v_bias': (0.0, 0.1),
     'L1_cond_scale_mul': (1.3862943649291992, 0.6),
     'L1_cond_proj_b': (0.0, 0.314),
     'L1_cond_ada_b': (0.0, 0.1),
     'L1_cond_fc1_b': (0.0, 0.467),
     'L1_cond_fc2_b': (0.0, 0.323),
     'L2_cond_g1': (1.0, 0.6),
     'L2_cond_be1': (0.0, 0.8),
     'L2_cond_g2': (1.0, 0.6),
     'L2_cond_be2': (0.0, 0.8),
     'L3_cond_ln_g': (1.0, 0.2),
     'L3_cond_ln_b': (0.0, 0.1),
     'L3_cond_bg': (0.0, 0.1),
     'L3_cond_bb': (0.0, 0.1),
     'L3_cond_bqkv': (0.0, 2.0),
     'L3_cond_bp': (0.0, 0.1),
     'L3_cond_b1': (0.0, 0.1),
     'L3_cond_b2': (0.0, 0.1)}
    factors = {'L2_cond_bqkv': 8.0,
     'L2_cond_bproj': 8.0,
     'L2_cond_b1': 25.128,
     'L2_cond_b2': 8.0,
     'L2_cond_bt': 8.0}
    for name, (base, spread) in spreads.items():
        noise = np.random.default_rng([zlib.crc32(name.encode()), seed]).standard_normal(out[name].shape)
        drawn = base * np.exp(spread * noise) if base else spread * noise
        out[name] = jnp.asarray(drawn.astype(out[name].dtype))
    for name, factor in factors.items():
        out[name] = (out[name] * factor).astype(out[name].dtype)
    return out
```

```python
from contextlib import ExitStack

import concourse.bass as bass
from concourse import mybir

F32 = mybir.dt.float32
F32R = mybir.dt.float32r
ALU = mybir.AluOpType
ACT = mybir.ActivationFunctionType
AX_X = mybir.AxisListType.X

LAYERS, BATCH, TOK, DIM, HID = 4, 4, 512, 256, 1024
HEADS, HD = 16, 16
P = 128
CH = DIM // P
TT = TOK // P
MT = HID // P
UNITS = HEADS // 4
JOBS = LAYERS * BATCH
TICKS = UNITS * TT
RING = 3
BLK = 64
KS = 3 * HD
EPS = (1e-6, 1e-6, 1e-5, 1e-5)
SCALE = (DIM ** -0.5, 1.0, HD ** -0.5, 1.0)
C_Q, C_K, C_V, C_B1, C_MB, C_G, C_BE, N_COL = 0, 2, 4, 6, 14, 22, 26, 30
R_PB, R_FB, R_GB, R_QK, R_SM, R_LG, R_LB = 0, 1024, 1792, 3328, 3840, 3856, 4112
N_ROW = 4368


def layer(j):
    return j // BATCH


def batch(j):
    return j % BATCH


def multi(j):
    return layer(j) > 0


def plan_steps():
    plan = []

    def add(kind, a, i=0):
        plan.append((kind, a, i))

    def prep(j):
        at = {t: [] for t in range(TICKS)}
        if j >= JOBS:
            return at
        at[0] += [("stat1", j, 0)]
        at[1] += [("norm1", j, 0)]
        at[2] += [("hT1", j, c) for c in range(CH)]
        if layer(j) == 1:
            at[3] += [("qktok", j, t) for t in range(TT)] + [("qkss", j, t) for t in range(TT)]
            at[4] += [("qknorm", j, t) for t in range(TT)]
            at[5] += [(x, j, i) for i in range(2) for x in "qk"]
        else:
            at[3] += [("q", j, 0), ("k", j, 0)]
            at[4] += [("q", j, 1), ("k", j, 1)]
        at[6] += [("v", j, i) for i in range(2)]
        if multi(j):
            at[5] += [("stack", UNITS * j, 0)]
            at[8] += [("stack", UNITS * j + 1, 0)]
            at[12] += [("stack", UNITS * j + 2, 0)]
        return at

    def post(j):
        at = {t: [] for t in range(TICKS)}
        if j < 0:
            return at
        if multi(j):
            at[1] += [("oT1", j, c) for c in range(TT)]
            at[2] += [("oT2", j, c) for c in range(CH)]
        at[5] += [("proj", j, i) for i in range(2)]
        at[6] += [("stat2", j, 0)]
        at[7] += [("norm2", j, 0)]
        if layer(j) < LAYERS - 1:
            at[8] += [("hT2", j, c) for c in range(CH)]
            at[9] += [("fc1", j, m) for m in range(MT // 2)]
            at[10] += [("fc1", j, m) for m in range(MT // 2, MT)]
            at[12] += [("fc2", j, 0)]
            at[13] += [("fc2", j, 1)]
        else:
            at[8] += [("final", j, t) for t in range(TT)]
        return at

    def weave(attention, maxima, rest):
        if not attention or not maxima:
            plan.extend(attention + maxima + rest)
            return
        cut = len(rest) // 2
        scores, av = attention[:2], attention[2:]
        parts = [scores[:1], maxima[:1], scores[1:], maxima[1:2], rest[:cut], maxima[2:3], av,
                 rest[cut:], maxima[3:]]
        for part in parts:
            plan.extend(part)

    add("load_mod", 0)
    add("load_qkv", 0)
    add("load_post", 0)
    add("mod", 0)
    add("load_mod", 1)
    first = prep(0)
    for t in range(TICKS):
        plan.extend(first[t])
    for w in range(JOBS + 1):
        before, after = post(w - 1), prep(w + 1)
        for t in range(TICKS):
            rest = before[t] + after[t]
            attention, maxima = [], []
            g, c = divmod(t, TT)
            if w < JOBS and multi(w):
                if t == 0:
                    add("stack", UNITS * w + 3)
                attention += [("scores", UNITS * w + g, 2 * c + h) for h in range(2)]
            if t > 0 and w < JOBS and multi(w):
                attention += [("av", UNITS * w + (t - 1) // TT, (t - 1) % TT)]
            if t == 0 and w > BATCH:
                attention += [("av", UNITS * w - 1, TT - 1)]
            u = UNITS * w + g + 2
            if UNITS * BATCH <= u < UNITS * JOBS:
                maxima = [("max", u, 4 * c + n) for n in range(4)]
            if c == 0 and UNITS * BATCH <= u - 1 < UNITS * JOBS:
                rest = [("shift", u - 1, 0)] + rest
            if w < BATCH:
                if t < TT:
                    rest = [("scores0", w, t)] + rest
                if 2 <= t < 2 + TT:
                    rest = [("pT0", w, t - 2)] + rest
                if t in (7, 8):
                    rest = [("av0", w, t - 7)] + rest
            if t == 3 and w in (BATCH - 1, BATCH):
                rest = [("vones", w + 1, 0)] + rest
            if w < JOBS:
                last = layer(w) == LAYERS - 1
                if t == 11 and multi(w):
                    rest += [("gate", w, 0)]
                if t == 14 and batch(w) == 2 and not last:
                    rest += [("mod", layer(w) + 1, 0)]
            weave(attention, maxima, rest)
            if w < JOBS:
                if t == 7 and batch(w) == 2 and not last:
                    add("load_qkv", layer(w) + 1)
                if t == 14 and batch(w) == 0 and multi(w):
                    add("load_post", layer(w))
                if t == 15 and batch(w) == 2 and layer(w) < LAYERS - 2:
                    add("load_mod", layer(w) + 2)
                if t == 15 and batch(w) == 3 and not last:
                    add("load_gate", layer(w) + 1)
    return plan


PLAN = plan_steps()
RINGED = ("hT1", "v", "qktok", "q", "k", "max", "shift", "oT1", "oT2", "proj", "hT2", "fc1",
          "fc2", "gate", "mod", "pT0", "av0")
NTH, USE, USES = {}, {}, []
_count = {}
for _s in PLAN:
    _count[_s[0]] = _count.get(_s[0], 0) + 1
    NTH[_s] = _count[_s[0]]
    if _s[0] in RINGED:
        USE[_s] = len(USES)
        USES.append(_s)


def nth(kind, a, i=0):
    return NTH[(kind, a, i)]


def use(kind, a, i=0):
    return USE[(kind, a, i)] + 1


def cond_blocks_kernel(nc, x, cond, cols, rows, wqkv, wp, w1, w2, wmod, wgate, out):
    x_v = x.rearrange("b (t p) d -> p b t d", p=P)
    out_v = out.rearrange("b (t p) d -> p b t d", p=P)

    with ExitStack() as ctx:
        def sb(name, shape, dt=F32):
            return ctx.enter_context(nc.sbuf_tensor(name, shape, dt))

        def sem(name):
            return ctx.enter_context(nc.semaphore(name))

        X = sb("X", [P, BATCH * TT, DIM])
        ident = sb("ident", [P, P])
        colv = sb("colv", [P, LAYERS, N_COL])
        rowv = sb("rowv", [P, N_ROW])
        condT = sb("condT", [P, CH, BATCH])
        condS = sb("condS", [P, CH, BATCH])
        condE = sb("condE", [P, CH, BATCH])
        condR = sb("condR", [P, CH, BATCH])
        smrow = sb("smrow", [P, HEADS])
        wqkv_s = sb("wqkv_s", [P, CH, 3 * DIM])
        wp_s = sb("wp_s", [P, CH, DIM])
        w1_s = sb("w1_s", [P, CH, HID])
        w2_s = sb("w2_s", [P, MT, DIM])
        wmod_s = sb("wmod_s", [P, CH, 4 * DIM])
        wgate_s = sb("wgate_s", [P, CH, 2 * DIM])
        modr = sb("modr", [P, 8, BATCH])
        mods = sb("mods", [P, 2, 4, BATCH])
        modb = sb("modb", [P, 2, 4, BATCH])
        gates = sb("gates", [P, BATCH, 2 * DIM])
        tok1 = sb("tok1", [P, TT, DIM])
        tok2 = sb("tok2", [P, TT, DIM])
        hT = sb("hT", [P, CH, TOK])
        postT = sb("postT", [P, CH, TOK])
        qk = sb("qk", [P, 4, TOK])
        sq = sb("sq", [P, TOK])
        qh = sb("qh", [P, 2, TOK], F32R)
        ql = sb("ql", [P, 2, TOK], F32R)
        kh = sb("kh", [P, 2, TOK], F32R)
        kl = sb("kl", [P, 2, TOK], F32R)
        SQ = [sb(f"SQ{i}", [P, 2, TOK], F32R) for i in range(4)]
        SK = [sb(f"SK{i}", [P, 2, TOK], F32R) for i in range(4)]
        VW = HEADS * (HD + 1)
        V = [sb(f"V{i}", [P, TT, VW + 16]) for i in range(2)]
        probs = sb("probs", [P, 4, 2 * TOK])
        oU = sb("oU", [P, UNITS, TOK])
        gT = sb("gT", [P, MT, TOK])
        tmp = sb("tmp", [P, 2, 2, DIM])
        m16 = sb("m16", [P, 2, 16])
        cT = sb("cT", [16, 2, P], F32R)
        stats = sb("stats", [P, 2, TT, 6])
        mv = sb("mv", [P, 2, TT, 2])
        var = sb("var", [P, 2, TT])
        rstd = sb("rstd", [P, 2, TT])
        mhalf = sb("mhalf", [P, 2 * HEADS])
        ss = sb("ss", [P, TT, 2 * HEADS])
        rs = sb("rs", [P, TT, 2 * HEADS])
        rcp = sb("rcp", [P, 2, HEADS])
        nm0 = sb("nm0", [P, TT])
        nb0 = sb("nb0", [P, TT])
        sum0 = sb("sum0", [P, TT])
        rc0 = sb("rc0", [P, TT])

        ST = [ctx.enter_context(nc.psum_tensor(f"ST{i}", [P, 2 * TOK], F32)) for i in range(2)]
        AVB = ctx.enter_context(nc.psum_tensor("AVB", [P, TOK], F32))
        ring = [ctx.enter_context(nc.psum_tensor(f"ring{i}", [P, TOK], F32)) for i in range(RING)]

        def bank(kind, a, i=0):
            return ring[USE[(kind, a, i)] % RING]

        kinds = sorted({s[0] for s in PLAN if not s[0].startswith("load") and s[0] != "stack"})
        done = {k: sem("done_" + k) for k in kinds}
        pe_ring = sem("pe_ring")
        pe_scores = sem("pe_scores")
        pe_av = sem("pe_av")
        pe_s0 = sem("pe_s0")
        unit_out = sem("unit_out")
        hi_ready = sem("hi_ready")
        sq_ready = sem("sq_ready")
        var1, var2 = sem("var1"), sem("var2")
        rstd1, rstd2 = sem("rstd1"), sem("rstd2")
        ss_ready = sem("ss_ready")
        nb_ready = sem("nb_ready")
        exp0 = sem("exp0")
        y1, y2 = sem("y1"), sem("y2")
        gate_ready = sem("gate_ready")
        stacked = [sem(f"stacked{i}") for i in range(4)]
        shifted = [sem(f"shifted{i}") for i in range(2)]
        x_in = [sem(f"x_in{b}") for b in range(BATCH)]
        small_in = sem("small_in")
        in_qkv, in_post, in_mod, in_gate = sem("in_qkv"), sem("in_post"), sem("in_mod"), sem("in_gate")
        out_sem = sem("out_sem")
        dve_seq, act_seq, pool_seq = sem("dve_seq"), sem("act_seq"), sem("pool_seq")
        const_ready = sem("const_ready")
        cond_ready = sem("cond_ready")
        e_ready = sem("e_ready")

        def post_loads(l):
            return 3 if l < LAYERS - 1 else 1

        POST_IN = [16 * sum(post_loads(i) for i in range(l + 1)) for l in range(LAYERS)]

        def STACK_IN(u):
            return 16 * 12 * ((u - UNITS * BATCH) // 4 + 1)

        def SHIFT_IN(u):
            return 16 * 2 * ((u - UNITS * BATCH) // 2 + 1)

        def slot_free(eng, u):
            if u - 4 >= UNITS * BATCH:
                eng.wait_ge(pe_scores, nth("scores", u - 4, 2 * TT - 1))

        def unit_job(u):
            return u // UNITS

        def wcond(l):
            return condS if l in (1, 2) else condT

        block = ctx.enter_context(nc.Block())

        @block.sync
        def _(sp):
            sp.dma_start(colv[:, :, :], cols).then_inc(small_in, 16)
            sp.dma_start(condT[:, :, :], cond.rearrange("(c p) b -> p c b", p=P)).then_inc(small_in, 16)
            sp.dma_start(rowv[:, :], rows.partition_broadcast(P)).then_inc(small_in, 16)
            for b in range(BATCH):
                sp.dma_start(X[:, b * TT:(b + 1) * TT, :], x_v[:, b]).then_inc(x_in[b], 16)
            for kind, a, i in PLAN:
                if kind == "load_qkv":
                    if a > 0:
                        j = (a - 1) * BATCH + 3
                        sp.wait_ge(pe_ring, use("v", j, 1))
                    sp.dma_start(wqkv_s[:, :, :], wqkv[a].rearrange("(c p) n -> p c n", p=P)).then_inc(in_qkv, 16)
                elif kind == "load_post":
                    if a > 0:
                        sp.wait_ge(pe_ring, use("fc2", a * BATCH - 1, 1))
                    sp.dma_start(wp_s[:, :, :], wp[a].rearrange("(c p) n -> p c n", p=P)).then_inc(in_post, 16)
                    if a < LAYERS - 1:
                        sp.dma_start(w1_s[:, :, :], w1[a].rearrange("(c p) n -> p c n", p=P)).then_inc(in_post, 16)
                        sp.dma_start(w2_s[:, :, :], w2[a].rearrange("(m p) n -> p m n", p=P)).then_inc(in_post, 16)
                elif kind == "load_mod":
                    if a > 0:
                        sp.wait_ge(pe_ring, use("mod", a - 1))
                    sp.dma_start(wmod_s[:, :, :], wmod[a].rearrange("(c p) n -> p c n", p=P)).then_inc(in_mod, 16)
                elif kind == "load_gate":
                    if a > 1:
                        sp.wait_ge(pe_ring, use("gate", a * BATCH - 1))
                    sp.dma_start(wgate_s[:, :, :], wgate[a - 1].rearrange("(c p) n -> p c n", p=P)).then_inc(in_gate, 16)
                elif kind == "stack":
                    j, g = divmod(a, UNITS)
                    sp.wait_ge(done["k"], nth("k", j, 1))
                    sp.wait_ge(done["q"], nth("q", j, 1))
                    slot_free(sp, a)
                    sp.wait_ge(const_ready, 1)
                    for stack, parts in ((SQ[a % 4], (qh, ql, qh)), (SK[a % 4], (kh, kh, kl))):
                        for r, part in enumerate(parts):
                            for par in range(2):
                                src = part[2 * HD * g + HD * par:2 * HD * g + HD * par + HD, :, :]
                                dst = stack[BLK * par + HD * r:BLK * par + HD * r + HD, :, :]
                                sp.dma_start(dst.bitcast(F32), src.bitcast(F32)).then_inc(stacked[a % 4], 16)
                elif kind == "shift":
                    sp.wait_ge(done["shift"], nth("shift", a))
                    for par in range(2):
                        d = SQ[a % 4][BLK * par + KS:BLK * par + KS + 1, :, :]
                        dst = bass.AP(d.tensor, d.offset, [[2 * TOK, 1], [P, 8], [1, P]]).bitcast(F32)
                        s = cT[8 * par:8 * par + 8, a % 2, :]
                        src = bass.AP(s.tensor, s.offset, [[2 * P, 8], [P, 1], [1, P]]).bitcast(F32)
                        sp.dma_start(dst, s.bitcast(F32)).then_inc(shifted[a % 2], 16)
                elif kind == "final":
                    sp.wait_ge(done["final"], nth("final", a, i))
                    sp.dma_start(out_v[:, batch(a), i], tok2[:, i, :]).then_inc(out_sem, 16)
            sp.wait_ge(out_sem, 16 * BATCH * TT)

        @block.tensor
        def _(pe):
            def claim(kind, a, i):
                n = USE[(kind, a, i)]
                if n >= RING:
                    k, b, m = USES[n - RING]
                    pe.wait_ge({"proj": y1, "fc2": y2}.get(k, done[k]), nth(k, b, m))
                return ring[n % RING]

            pe.wait_ge(const_ready, 1)
            pe.wait_ge(small_in, 48)
            for kind, a, i in PLAN:
                o = claim(kind, a, i) if kind in RINGED else None
                mm = None
                if kind in ("q", "k", "qktok", "v"):
                    pe.wait_ge(done["hT1"], nth("hT1", a, CH - 1))
                    pe.wait_ge(in_qkv, 16 * (layer(a) + 1))
                if kind == "mod":
                    pe.wait_ge(in_mod, 16 * (a + 1))
                    pe.wait_ge(cond_ready, 1)
                    for m in range(8 if a < LAYERS - 1 else 4):
                        for c in range(CH):
                            mm = pe.matmul(o[:, BATCH * m:BATCH * m + BATCH], wmod_s[:, c, m * P:(m + 1) * P],
                                           wcond(a)[:, c, :], start=(c == 0), stop=(c == CH - 1))
                elif kind == "gate":
                    pe.wait_ge(in_gate, 16 * layer(a))
                    for c in range(CH):
                        mm = pe.matmul(o[:, :], wcond(layer(a))[:, c, batch(a):batch(a) + 1].to_broadcast([P, P]),
                                       wgate_s[:, c, :], start=(c == 0), stop=(c == CH - 1))
                elif kind in ("hT1", "hT2"):
                    src = tok1 if kind == "hT1" else tok2
                    norm = "norm1" if kind == "hT1" else "norm2"
                    pe.wait_ge(done[norm], nth(norm, a))
                    for t in range(TT):
                        mm = pe.transpose(o[:, t * P:(t + 1) * P], src[:, t, i * P:(i + 1) * P], ident[:, :])
                elif kind == "v":
                    for t in range(2):
                        for c in range(CH):
                            tok = (2 * i + t) * P
                            mm = pe.matmul(o[:, t * DIM:(t + 1) * DIM], hT[:, c, tok:tok + P],
                                           wqkv_s[:, c, 2 * DIM:3 * DIM], start=(c == 0), stop=(c == CH - 1))
                elif kind == "qktok":
                    for c in range(CH):
                        mm = pe.matmul(o[:, :], hT[:, c, i * P:(i + 1) * P], wqkv_s[:, c, 0:2 * DIM],
                                       start=(c == 0), stop=(c == CH - 1))
                elif kind in ("q", "k"):
                    off = DIM * (kind == "k") + i * P
                    if layer(a) == 1:
                        pe.wait_ge(done["qknorm"], nth("qknorm", a, TT - 1))
                        for t in range(TT):
                            mm = pe.transpose(o[:, t * P:(t + 1) * P], qk[:, t, off:off + P], ident[:, :])
                    else:
                        for c in range(CH):
                            mm = pe.matmul(o[:, :], wqkv_s[:, c, off:off + P], hT[:, c, :],
                                           start=(c == 0), stop=(c == CH - 1))
                elif kind == "max":
                    if i == 0:
                        pe.wait_ge(stacked[a % 4], STACK_IN(a))
                    n, c = i % 4, i // 4
                    r = BLK * (n % 2)
                    mm = pe.matmul(o[:, :], SQ[a % 4][r:r + KS, n // 2, c * P:(c + 1) * P],
                                   SK[a % 4][r:r + KS, n // 2, :], start=True, stop=True)
                elif kind == "shift":
                    pe.wait_ge(done["max"], nth("max", a, 15))
                    mm = pe.transpose(o[0:16, 0:P], m16[:, a % 2, :], ident[:, :])
                elif kind == "scores":
                    n, c, h = nth("scores", a, i) - 1, i // 2, i % 2
                    if i == 0:
                        pe.wait_ge(shifted[a % 2], SHIFT_IN(a))
                    if n >= 2:
                        pe.wait_ge(done["scores"], n - 1)
                    else:
                        pe.wait_ge(done["scores0"], nth("scores0", BATCH - 1, TT - 1))
                    for par in range(2):
                        r = BLK * par
                        mm = pe.matmul(ST[h][:, par * TOK:(par + 1) * TOK],
                                       SK[a % 4][r:r + KS + 1, h, c * P:(c + 1) * P],
                                       SQ[a % 4][r:r + KS + 1, h, :], start=True, stop=True)
                    mm.then_inc(pe_scores, 1)
                    continue
                elif kind == "av":
                    j, g = divmod(a, UNITS)
                    t = nth("av", a, i) - 1
                    if i == 0:
                        pe.wait_ge(done["v"], nth("v", j, 1))
                        if t > 0:
                            pe.wait_ge(unit_out, t // TT)
                    for n in range(4):
                        if n % 2 == 0:
                            pe.wait_ge(done["scores"], 2 * t + n // 2 + 1)
                        h = 4 * g + n
                        mm = pe.matmul(AVB[32 * n:32 * n + 32, :], V[j % 2][:, i, (HD + 1) * h:(HD + 1) * h + 32],
                                       probs[:, (2 * t + n // 2) % 4, (n % 2) * TOK:(n % 2 + 1) * TOK],
                                       start=(i == 0), stop=(i == TT - 1))
                    mm.then_inc(pe_av, 1)
                    continue
                elif kind == "scores0":
                    t = nth("scores0", a, i) - 1
                    if i == 0:
                        pe.wait_ge(done["q"], nth("q", a, 1))
                        pe.wait_ge(done["k"], nth("k", a, 1))
                    if t >= 2:
                        pe.wait_ge(exp0, t - 1)
                    for c in range(CH):
                        mm = pe.matmul(ST[t % 2][:, 0:TOK], qk[:, c, i * P:(i + 1) * P], qk[:, 2 + c, :],
                                       start=(c == 0), stop=(c == CH - 1))
                    mm.then_inc(pe_s0, 1)
                    continue
                elif kind == "pT0":
                    pe.wait_ge(done["scores0"], nth("scores0", a, i))
                    for t in range(TT):
                        mm = pe.transpose(o[:, t * P:(t + 1) * P], probs[:, i, t * P:(t + 1) * P], ident[:, :])
                elif kind == "av0":
                    pe.wait_ge(done["pT0"], nth("pT0", a, TT - 1))
                    pe.wait_ge(done["v"], nth("v", a, 1))
                    for t in range(TT):
                        mm = pe.matmul(o[:, :], V[a % 2][:, t, i * P:(i + 1) * P], gT[:, t, :],
                                       start=(t == 0), stop=(t == TT - 1))
                elif kind == "oT1":
                    pe.wait_ge(unit_out, UNITS * (a + 1 - BATCH))
                    for g in range(UNITS):
                        mm = pe.transpose(o[:, g * P:(g + 1) * P], oU[:, g, i * P:(i + 1) * P], ident[:, :])
                elif kind == "oT2":
                    pe.wait_ge(done["oT1"], nth("oT1", a, TT - 1))
                    for t in range(TT):
                        mm = pe.transpose(o[:, t * P:(t + 1) * P], tok2[:, t, i * P:(i + 1) * P], ident[:, :])
                elif kind == "proj":
                    if multi(a):
                        pe.wait_ge(done["oT2"], nth("oT2", a, CH - 1))
                    else:
                        pe.wait_ge(done["av0"], nth("av0", a, 1))
                    pe.wait_ge(in_post, POST_IN[layer(a)])
                    for t in range(2):
                        tok = (2 * i + t) * P
                        for c in range(CH):
                            src = postT[:, c, tok:tok + P] if multi(a) else oU[:, 2 + c, tok:tok + P]
                            mm = pe.matmul(o[:, t * DIM:(t + 1) * DIM], src, wp_s[:, c, :],
                                           start=(c == 0), stop=(c == CH - 1))
                elif kind == "fc1":
                    pe.wait_ge(done["hT2"], nth("hT2", a, CH - 1))
                    for c in range(CH):
                        mm = pe.matmul(o[:, :], w1_s[:, c, i * P:(i + 1) * P], postT[:, c, :],
                                       start=(c == 0), stop=(c == CH - 1))
                elif kind == "fc2":
                    pe.wait_ge(done["fc1"], nth("fc1", a, MT - 1))
                    for t in range(2):
                        tok = (2 * i + t) * P
                        for m in range(MT):
                            mm = pe.matmul(o[:, t * DIM:(t + 1) * DIM], gT[:, m, tok:tok + P], w2_s[:, m, :],
                                           start=(m == 0), stop=(m == MT - 1))
                if mm is not None:
                    mm.then_inc(pe_ring, 1)

        @block.scalar
        def _(act):
            act.wait_ge(small_in, 48)
            act.activation(condE[:, :, :], condT[:, :, :], ACT.Exp, scale=-1.0).then_inc(e_ready, 1)
            act.wait_ge(cond_ready, 1)
            act.activation(smrow[:, :], smrow[:, :], ACT.Exp).then_inc(e_ready, 1)
            for kind, a, i in PLAN:
                if kind in ("hT1", "hT2"):
                    l, b, second = layer(a), batch(a), kind == "hT2"
                    act.wait_ge(pe_ring, use(kind, a, i))
                    act.wait_ge(done["mod"], nth("mod", l))
                    n = 2 * second + i
                    if not second and a > 0 and i == 0:
                        act.wait_ge(pe_ring, use("v", a - 1, 1))
                    if second and i == 0:
                        act.wait_ge(pe_ring, use("proj", a, 1))
                        if a > 0:
                            act.wait_ge(pe_ring, use("fc1", a - 1, MT - 1))
                    dst = postT if second else hT
                    act.activation(dst[:, i, :], bank(kind, a, i)[:, :], ACT.Identity,
                                   bias=modb[:, l % 2, n, b:b + 1], scale=mods[:, l % 2, n, b:b + 1]
                                   ).then_inc(done[kind], 1)
                elif kind == "v":
                    act.wait_ge(pe_ring, use(kind, a, i))
                    if i == 0 and a >= 2:
                        if multi(a - 2):
                            act.wait_ge(pe_av, nth("av", UNITS * (a - 1) - 1, TT - 1))
                        else:
                            act.wait_ge(pe_ring, use("av0", a - 2, 1))
                    src = bank(kind, a, i)
                    if multi(a):
                        if layer(a) == 1 and batch(a) < 2 and i == 0:
                            act.wait_ge(done["vones"], batch(a) + 1)
                        for t in range(2):
                            dst = V[a % 2][:, 2 * i + t, 0:VW].rearrange("p (h e) -> p h e", e=HD + 1)[:, :, 0:HD]
                            ins = act.activation(dst, src[:, t * DIM:(t + 1) * DIM].rearrange("p (h d) -> p h d", d=HD),
                                                 ACT.Copy)
                        ins.then_inc(done["v"], 1)
                    else:
                        act.activation(V[a % 2][:, 2 * i:2 * i + 2, 0:DIM],
                                       src[:, :].rearrange("p (t d) -> p t d", t=2), ACT.Copy).then_inc(done["v"], 1)
                elif kind == "qktok":
                    t = nth(kind, a, i) - 1
                    act.wait_ge(done["qktok"], t + 1)
                    if t >= 1:
                        act.wait_ge(ss_ready, t)
                    act.activation(sq[:, :], qk[:, i, :], ACT.Square).then_inc(sq_ready, 1)
                elif kind in ("q", "k"):
                    l = layer(a)
                    act.wait_ge(pe_ring, use(kind, a, i))
                    col = (C_Q if kind == "q" else C_K) + i
                    if l == 0:
                        if a > 0:
                            act.wait_ge(pe_s0, nth("scores0", a - 1, TT - 1))
                        act.activation(qk[:, 2 * (kind == "k") + i, :], bank(kind, a, i)[:, :], ACT.Identity,
                                       bias=colv[:, l, col:col + 1]).then_inc(done[kind], 1)
                    else:
                        if a > BATCH:
                            for g in range(UNITS):
                                act.wait_ge(stacked[g], STACK_IN(UNITS * (a - 1) + g))
                        hi = qh if kind == "q" else kh
                        if l == 1:
                            act.activation(hi[:, i, :], bank(kind, a, i)[:, :], ACT.Copy).then_inc(hi_ready, 1)
                        else:
                            act.activation(hi[:, i, :], bank(kind, a, i)[:, :], ACT.Identity,
                                           bias=colv[:, l, col:col + 1]).then_inc(hi_ready, 1)
                elif kind == "scores":
                    n = nth("scores", a, i) - 1
                    act.wait_ge(pe_scores, n + 1)
                    if n >= 4:
                        act.wait_ge(pe_av, n // 2 - 1)
                    elif n == 0:
                        act.wait_ge(pe_ring, use("pT0", BATCH - 1, TT - 1))
                    act.activation(probs[:, n % 4, :], ST[n % 2][:, :], ACT.Exp,
                                   scale=SCALE[layer(unit_job(a))]).then_inc(done["scores"], 1)
                elif kind == "scores0":
                    t = nth("scores0", a, i) - 1
                    act.wait_ge(nb_ready, t + 1)
                    if t >= TT:
                        act.wait_ge(pe_ring, use("pT0", a - 1, i))
                    act.activation(probs[:, i, 0:TOK], ST[t % 2][:, 0:TOK], ACT.Exp, bias=nb0[:, i:i + 1],
                                   scale=SCALE[0], accum_out=sum0[:, i:i + 1]).then_inc(exp0, 1)
                elif kind == "pT0":
                    act.wait_ge(pe_ring, use(kind, a, i))
                    if a > 1:
                        act.wait_ge(pe_ring, use("fc2", a - 2, 1))
                    if a > 0:
                        act.wait_ge(pe_ring, use("av0", a - 1, 1))
                    act.activation(gT[:, 0:TT, i * P:(i + 1) * P],
                                   bank(kind, a, i)[:, :].rearrange("p (k q) -> p k q", k=TT),
                                   ACT.Copy).then_inc(done[kind], 1)
                elif kind == "av0":
                    act.wait_ge(pe_ring, use(kind, a, i))
                    if a > 0:
                        act.wait_ge(pe_ring, use("proj", a - 1, 1))
                    act.activation(oU[:, 2 + i, :], bank(kind, a, i)[:, :], ACT.Identity,
                                   bias=colv[:, 0, C_V + i:C_V + i + 1]).then_inc(done[kind], 1)
                elif kind == "av" and i == TT - 1:
                    act.wait_ge(pe_av, nth("av", a, i))
                    j, g = divmod(a, UNITS)
                    if g == 0 and j > BATCH:
                        act.wait_ge(pe_ring, use("oT1", j - 1, TT - 1))
                    if g == 2 and j == BATCH:
                        act.wait_ge(pe_ring, use("proj", j - 1, 1))
                    act.activation(oU[:, g, :], AVB[:, :], ACT.Copy).then_inc(unit_out, 1)
                elif kind == "oT2":
                    l = layer(a)
                    act.wait_ge(pe_ring, use(kind, a, i))
                    if i == 0 and layer(a - 1) < LAYERS - 1:
                        act.wait_ge(pe_ring, use("fc1", a - 1, MT - 1))
                    elif i == 0:
                        act.wait_ge(pe_ring, use("proj", a - 1, 1))
                    act.activation(postT[:, i, :], bank(kind, a, i)[:, :], ACT.Identity,
                                   bias=colv[:, l, C_V + i:C_V + i + 1],
                                   scale=(1.0 if l < LAYERS - 1 else DIM ** -0.5)).then_inc(done[kind], 1)
                elif kind == "fc1":
                    act.wait_ge(pe_ring, use(kind, a, i))
                    if i == 0:
                        if a > 0:
                            act.wait_ge(pe_ring, use("fc2", a - 1, 1))
                        if a + 1 < BATCH:
                            act.wait_ge(pe_ring, use("av0", a + 1, 1))
                    act.activation(gT[:, i, :], bank(kind, a, i)[:, :], ACT.Gelu,
                                   bias=colv[:, layer(a), C_B1 + i:C_B1 + i + 1]).then_inc(done[kind], 1)

        @block.vector
        def _(dve):
            n_seq = [0]

            def link(ins):
                n_seq[0] += 1
                ins.then_inc(dve_seq, 1)
                dve.wait_ge(dve_seq, n_seq[0])

            for i in range(4):
                nc.vector.memset(SK[i][:, :, :].bitcast(F32), 1.0)
            link(nc.vector.memset(mhalf[:, :], -0.5))
            dve.wait_ge(e_ready, 1)
            link(nc.vector.tensor_scalar(condR[:, :, :], condE[:, :, :], 1.0, None, ALU.add))
            link(nc.vector.reciprocal(condE[:, :, :], condR[:, :, :]))
            nc.vector.tensor_tensor(condS[:, :, :], condT[:, :, :], condE[:, :, :], ALU.mult)
            nc.vector.tensor_scalar(smrow[:, :], rowv[:, R_SM:R_SM + HEADS], LOG100, None, ALU.min)
            nc.vector.tensor_scalar(colv[:, LAYERS - 1, C_V:C_V + 2], colv[:, LAYERS - 1, C_V:C_V + 2],
                                    DIM ** -0.5, None, ALU.mult).then_inc(cond_ready, 1)

            for kind, a, i in PLAN:
                if kind == "mod":
                    l, q = a, a % 2
                    n = 8 if l < LAYERS - 1 else 4
                    dve.wait_ge(pe_ring, use(kind, a))
                    if l >= 2:
                        dve.wait_ge(done["hT2"], nth("hT2", (l - 1) * BATCH - 1, CH - 1))
                    mb = colv[:, l, C_MB:C_MB + n].unsqueeze(2).to_broadcast([P, n, BATCH])
                    link(nc.vector.tensor_tensor(modr[:, 0:n, :], bank(kind, a)[:, 0:n * BATCH].rearrange(
                        "p (m b) -> p m b", b=BATCH), mb, ALU.add))
                    for s in range(n // 4):
                        sc, sh = modr[:, 4 * s:4 * s + 2, :], modr[:, 4 * s + 2:4 * s + 4, :]
                        g = colv[:, l, C_G + 2 * s:C_G + 2 * s + 2].unsqueeze(2).to_broadcast([P, 2, BATCH])
                        be = colv[:, l, C_BE + 2 * s:C_BE + 2 * s + 2].unsqueeze(2).to_broadcast([P, 2, BATCH])
                        if l < LAYERS - 1:
                            link(nc.vector.tensor_scalar(sc, sc, 1.0, None, ALU.add))
                        nc.vector.tensor_tensor(mods[:, q, 2 * s:2 * s + 2, :], sc, g, ALU.mult)
                        link(nc.vector.tensor_tensor(sc, sc, be, ALU.mult))
                        ins = nc.vector.tensor_tensor(modb[:, q, 2 * s:2 * s + 2, :], sc, sh, ALU.add)
                    ins.then_inc(done["mod"], 1)
                elif kind == "vones":
                    dve.wait_ge(pe_ring, use("av0", a - 2, 1))
                    nc.vector.memset(V[a % 2][:, :, :], 1.0).then_inc(done[kind], 1)
                elif kind == "gate":
                    l, b = layer(a), batch(a)
                    dve.wait_ge(pe_ring, use(kind, a))
                    if l >= 2:
                        dve.wait_ge(done["fc2"], nth("fc2", a - BATCH, 1))
                    nc.vector.tensor_tensor(gates[:, b, :], bank(kind, a)[:, :],
                                            rowv[:, R_GB + 512 * (l - 1):R_GB + 512 * l], ALU.add
                                            ).then_inc(done["gate"], 1)
                elif kind in ("stat1", "stat2"):
                    w = int(kind == "stat2")
                    l, b = layer(a), batch(a)
                    if w:
                        dve.wait_ge(done["proj"], nth("proj", a, 1))
                    elif l == 0:
                        dve.wait_ge(x_in[b], 16)
                    else:
                        dve.wait_ge(done["fc2"], nth("fc2", a - BATCH, 1))
                    for t in range(TT):
                        ins = nc.vector.bn_stats(stats[:, w, t, :], X[:, TT * b + t, :])
                    link(ins)
                    for t in range(TT):
                        ins = nc.vector.bn_aggr(mv[:, w, t, :], stats[:, w, t, :])
                    if l == 0:
                        link(ins)
                        link(nc.vector.tensor_tensor(var[:, w, :], mv[:, w, :, 0], mv[:, w, :, 0], ALU.mult))
                        ins = nc.vector.tensor_tensor(var[:, w, :], var[:, w, :], mv[:, w, :, 1], ALU.add)
                    ins.then_inc(done[kind], 1)
                elif kind in ("norm1", "norm2"):
                    w = int(kind == "norm2")
                    l, b = layer(a), batch(a)
                    dst = tok2 if w else tok1
                    dve.wait_ge(rstd2 if w else rstd1, nth(kind, a))
                    if w:
                        if multi(a):
                            dve.wait_ge(pe_ring, use("oT2", a, CH - 1))
                        if a > 0 and not multi(a):
                            dve.wait_ge(pe_ring, use("hT2", a - 1, CH - 1))
                    elif a > 0:
                        dve.wait_ge(pe_ring, use("hT1", a - 1, CH - 1))
                    for t in range(TT):
                        if l == 0:
                            ins = nc.vector.tensor_scalar(dst[:, t, :], X[:, TT * b + t, :], rstd[:, w, t:t + 1],
                                                          None, ALU.mult)
                        else:
                            ins = nc.vector.tensor_scalar(dst[:, t, :], X[:, TT * b + t, :], mv[:, w, t, 0:1],
                                                          rstd[:, w, t:t + 1], ALU.subtract, ALU.mult)
                    ins.then_inc(done[kind], 1)
                elif kind == "qktok":
                    dve.wait_ge(pe_ring, use(kind, a, i))
                    if a == BATCH:
                        dve.wait_ge(pe_s0, nth("scores0", BATCH - 1, TT - 1))
                    else:
                        dve.wait_ge(pe_ring, use("k", a - 1, 1))
                    nc.vector.tensor_tensor(qk[:, i, :], bank(kind, a, i)[:, :], rowv[:, R_QK:R_QK + TOK],
                                            ALU.add).then_inc(done[kind], 1)
                    t = nth(kind, a, i) - 1
                    dve.wait_ge(sq_ready, t + 1)
                    if a > BATCH and i == 0:
                        dve.wait_ge(done["qkss"], nth("qkss", a - 1, TT - 1))
                    nc.vector.tensor_reduce(ss[:, i, :], sq[:, :].rearrange("p (h d) -> p h d", d=HD),
                                            AX_X, ALU.add).then_inc(ss_ready, 1)
                elif kind == "qknorm":
                    dve.wait_ge(done["qkss"], nth("qkss", a, i))
                    r = rs[:, i, :].unsqueeze(2).to_broadcast([P, 2 * HEADS, HD])
                    v = qk[:, i, :].rearrange("p (h d) -> p h d", d=HD)
                    nc.vector.tensor_tensor(v, v, r, ALU.mult).then_inc(done[kind], 1)
                elif kind in ("q", "k"):
                    if not multi(a):
                        continue
                    l = layer(a)
                    col = (C_Q if kind == "q" else C_K) + i
                    hi, lo = (qh, ql) if kind == "q" else (kh, kl)
                    dve.wait_ge(hi_ready, (nth(kind, a, i) - nth(kind, BATCH, 0)) * 2 + 1 + (kind == "k"))
                    if l == 1:
                        nc.vector.tensor_tensor(lo[:, i, :], bank(kind, a, i)[:, :], hi[:, i, :].bitcast(F32),
                                                ALU.subtract).then_inc(done[kind], 1)
                    else:
                        nc.vector.scalar_tensor_tensor(out=lo[:, i, :], in0=bank(kind, a, i)[:, :],
                                                       scalar=colv[:, l, col:col + 1], in1=hi[:, i, :].bitcast(F32),
                                                       op0=ALU.add, op1=ALU.subtract).then_inc(done[kind], 1)
                elif kind == "max":
                    n, c = i % 4, i // 4
                    col = ((n % 2) * 2 + n // 2) * TT + c
                    dve.wait_ge(pe_ring, use(kind, a, i))
                    if i == 0 and a - 2 >= UNITS * BATCH:
                        dve.wait_ge(pe_ring, use("shift", a - 2))
                    nc.vector.tensor_reduce(m16[:, a % 2, col:col + 1], bank(kind, a, i)[:, :], AX_X, ALU.max,
                                            negate=True).then_inc(done["max"], 1)
                elif kind == "shift":
                    dve.wait_ge(pe_ring, use(kind, a))
                    if a - 2 >= UNITS * BATCH:
                        dve.wait_ge(shifted[a % 2], SHIFT_IN(a - 2))
                    nc.vector.tensor_copy(cT[:, a % 2, :], bank(kind, a)[0:16, 0:P]).then_inc(done["shift"], 1)
                elif kind == "scores0":
                    t = nth(kind, a, i) - 1
                    dve.wait_ge(pe_s0, t + 1)
                    if t >= TT:
                        dve.wait_ge(exp0, t + 1 - TT)
                    link(nc.vector.tensor_reduce(nm0[:, i:i + 1], ST[t % 2][:, 0:TOK], AX_X, ALU.max, negate=True))
                    nc.vector.tensor_scalar(nb0[:, i:i + 1], nm0[:, i:i + 1], SCALE[0], None, ALU.mult
                                            ).then_inc(nb_ready, 1)
                    dve.wait_ge(exp0, t + 1)
                    link(nc.vector.reciprocal(rc0[:, i:i + 1], sum0[:, i:i + 1]))
                    nc.vector.tensor_scalar(probs[:, i, 0:TOK], probs[:, i, 0:TOK], rc0[:, i:i + 1], None,
                                            ALU.mult).then_inc(done["scores0"], 1)
                elif kind == "oT1":
                    dve.wait_ge(pe_ring, use(kind, a, i))
                    if i == 0 and layer(a - 1) < LAYERS - 1:
                        dve.wait_ge(pe_ring, use("hT2", a - 1, CH - 1))
                    elif i == 0:
                        dve.wait_ge(out_sem, 16 * nth("final", a - 1, TT - 1))
                    b = bank(kind, a, i)[:, :].rearrange("p (h e) -> p h e", e=32)
                    link(nc.vector.reciprocal(rcp[:, i % 2, :], b[:, :, HD]))
                    nc.vector.tensor_tensor(tok2[:, i, :].rearrange("p (h d) -> p h d", d=HD), b[:, :, 0:HD],
                                            rcp[:, i % 2, :].unsqueeze(2).to_broadcast([P, HEADS, HD]), ALU.mult
                                            ).then_inc(done[kind], 1)
                elif kind in ("proj", "fc2"):
                    l = layer(a)
                    dve.wait_ge(pe_ring, use(kind, a, i))
                    if kind == "fc2":
                        dve.wait_ge(done["proj"], nth("proj", a, i))
                    elif a > 0 and layer(a - 1) < LAYERS - 1:
                        dve.wait_ge(done["fc2"], nth("fc2", a - 1, i))
                    elif a > 0:
                        dve.wait_ge(done["proj"], nth("proj", a - 1, i))
                    off = (R_PB if kind == "proj" else R_FB) + DIM * l
                    nc.vector.tensor_tensor(tmp[:, i, :, :], bank(kind, a, i)[:, :].rearrange("p (t d) -> p t d", t=2),
                                            rowv[:, off:off + DIM].unsqueeze(1).to_broadcast([P, 2, DIM]), ALU.add
                                            ).then_inc(y1 if kind == "proj" else y2, 1)

        @block.gpsimd
        def _(pool):
            n_seq = [0]

            def link(ins):
                n_seq[0] += 1
                ins.then_inc(pool_seq, 1)
                pool.wait_ge(pool_seq, n_seq[0])

            link(nc.gpsimd.memset(ident[:, :], 0.0))
            pool.wait_ge(dve_seq, 1)
            nc.gpsimd.affine_select(out=ident[:, :], in_=ident[:, :], compare_op=ALU.not_equal, fill=1.0, base=0,
                                    pattern=[[-1, P]], channel_multiplier=1).then_inc(const_ready, 1)
            for kind, a, i in PLAN:
                if kind in ("stat1", "stat2"):
                    w, l = int(kind == "stat2"), layer(a)
                    pool.wait_ge(done[kind], nth(kind, a))
                    src = var[:, w, :] if l == 0 else mv[:, w, :, 1]
                    if a > 0:
                        pool.wait_ge(done["norm2" if w else "norm1"], nth("norm2" if w else "norm1", a - 1))
                    link(nc.gpsimd.tensor_scalar(rstd[:, w, :], src, EPS[l], None, ALU.add))
                    nc.gpsimd.tensor_tensor(rstd[:, w, :], rstd[:, w, :], mhalf[:, 0:TT], ALU.pow
                                            ).then_inc(rstd2 if w else rstd1, 1)
                elif kind == "qkss":
                    pool.wait_ge(ss_ready, nth(kind, a, i))
                    pool.wait_ge(e_ready, 2)
                    if a > BATCH:
                        pool.wait_ge(done["qknorm"], nth("qknorm", a - 1, i))
                    link(nc.gpsimd.tensor_scalar(ss[:, i, :], ss[:, i, :], 1e-24, None, ALU.max))
                    link(nc.gpsimd.tensor_tensor(rs[:, i, :], ss[:, i, :], mhalf[:, :], ALU.pow))
                    nc.gpsimd.tensor_tensor(rs[:, i, 0:HEADS], rs[:, i, 0:HEADS], smrow[:, :], ALU.mult
                                            ).then_inc(done[kind], 1)
                elif kind in ("proj", "fc2"):
                    l, b = layer(a), batch(a)
                    pool.wait_ge(y1 if kind == "proj" else y2, nth(kind, a, i))
                    if l in (1, 2):
                        pool.wait_ge(done["gate"], nth("gate", a))
                        off = 0 if kind == "proj" else DIM
                        g = gates[:, b, off:off + DIM].unsqueeze(1).to_broadcast([P, 2, DIM])
                        link(nc.gpsimd.tensor_tensor(tmp[:, i, :, :], tmp[:, i, :, :], g, ALU.mult))
                    xs = X[:, TT * b + 2 * i:TT * b + 2 * i + 2, :]
                    if kind == "proj":
                        pool.wait_ge(done["norm1"], nth("norm1", a))
                    else:
                        pool.wait_ge(done["norm2"], nth("norm2", a))
                    nc.gpsimd.tensor_tensor(xs, xs, tmp[:, i, :, :], ALU.add).then_inc(done[kind], 1)
                    if l == LAYERS - 1 and i == 0:
                        pool.wait_ge(done["gate"], nth("gate", a))
                        gm, bt = gates[:, b, 0:DIM], gates[:, b, DIM:2 * DIM]
                        if True:
                            link(nc.gpsimd.tensor_tensor(sq[:, 0:DIM], gm, rowv[:, R_LB:R_LB + DIM], ALU.mult))
                            nc.gpsimd.tensor_tensor(gm, gm, rowv[:, R_LG:R_LG + DIM], ALU.mult)
                            link(nc.gpsimd.tensor_tensor(bt, bt, sq[:, 0:DIM], ALU.add))
                elif kind == "final":
                    l, b = layer(a), batch(a)
                    pool.wait_ge(done["norm2"], nth("norm2", a))
                    t = tok2[:, i, :]
                    link(nc.gpsimd.tensor_tensor(t, t, gates[:, b, 0:DIM], ALU.mult))
                    link(nc.gpsimd.tensor_tensor(t, t, gates[:, b, DIM:2 * DIM], ALU.add))
                    nc.gpsimd.tensor_tensor(t, t, X[:, TT * b + i, :], ALU.add).then_inc(done["final"], 1)


LOG100 = 4.605170185988092


def kernel(**inputs):
    import numpy as np
    import concourse.bacc as bacc
    from concourse.bass_utils import run_bass_kernel_spmd

    g = {k: np.asarray(v) for k, v in inputs.items()}
    one, zero = np.ones(DIM, np.float32), np.zeros(DIM, np.float32)

    def regroup(w):
        return w.reshape(HEADS, HD, 3, -1).transpose(2, 0, 1, 3).reshape(3 * DIM, -1)

    def parts(w, order):
        return np.concatenate([w[..., DIM * n:DIM * (n + 1)] for n in order], axis=-1)

    def by_unit(w, blocks):
        out = [w[..., DIM * n:DIM * (n + 1)] for n in range(w.shape[-1] // DIM)]
        for n in range(blocks):
            v = out[n].reshape(-1, UNITS, 2, 2, HD).transpose(0, 2, 1, 3, 4)
            out[n] = v.reshape(w.shape[:-1] + (DIM,))
        return np.concatenate(out, axis=-1)

    wqkv = np.stack([
        np.concatenate([g["L0_cond_q_w"], g["L0_cond_k_w"], g["L0_cond_v_w"]], axis=1),
        by_unit(g["L1_cond_mat_qkv_w"].T, 2), by_unit(g["L2_cond_Wqkv"], 2), by_unit(regroup(g["L3_cond_Wqkv"]).T, 2)])
    wp = np.stack([g["L0_cond_proj_w"], g["L1_cond_proj_w"].T, g["L2_cond_Wproj"], g["L3_cond_Wp"].T])
    w1 = np.stack([g["L0_cond_mlp_w1"], g["L1_cond_fc1_w"].T, g["L2_cond_W1"]])
    w2 = np.stack([g["L0_cond_mlp_w2"], g["L1_cond_fc2_w"].T, g["L2_cond_W2"]])
    ada1, adab1 = g["L1_cond_ada_w"].T, g["L1_cond_ada_b"]
    ada2, adab2 = g["L2_cond_Wt"], g["L2_cond_bt"]
    film3 = np.concatenate([g["L3_cond_Wg"].T, g["L3_cond_Wb"].T], axis=1)
    filmb3 = np.concatenate([g["L3_cond_bg"], g["L3_cond_bb"]])
    film0 = np.concatenate([g["L0_cond_film1_w"], g["L0_cond_film2_w"]], axis=1)
    filmb0 = np.concatenate([g["L0_cond_film1_b"], g["L0_cond_film2_b"]])
    wmod = np.stack([film0, parts(ada1, (2, 4, 3, 5)), parts(ada2, (1, 0, 4, 3)),
                     np.concatenate([film3, film3], axis=1)])
    modbias = [filmb0, parts(adab1, (2, 4, 3, 5)), parts(adab2, (1, 0, 4, 3)), np.concatenate([filmb3, filmb3])]
    wgate = np.stack([parts(ada1, (0, 1)), parts(ada2, (2, 5)), film3])
    gatebias = [parts(adab1, (0, 1)), parts(adab2, (2, 5)), filmb3]
    b3 = regroup(g["L3_cond_bqkv"])[:, 0]
    bqkv = [np.concatenate([g["L0_cond_q_b"], g["L0_cond_k_b"], g["L0_cond_v_b"]]),
            np.concatenate([g["L1_cond_q_bias"], zero, g["L1_cond_v_bias"]]), by_unit(g["L2_cond_bqkv"], 2), by_unit(b3, 2)]
    b1 = [g["L0_cond_mlp_b1"], g["L1_cond_fc1_b"], g["L2_cond_b1"], np.zeros(HID, np.float32)]
    ga = [(g["L0_cond_norm1_w"], g["L0_cond_norm2_w"], zero, zero), (one, one, zero, zero),
          (g["L2_cond_g1"], g["L2_cond_g2"], g["L2_cond_be1"], g["L2_cond_be2"]),
          (g["L3_cond_ln_g"], g["L3_cond_ln_g"], g["L3_cond_ln_b"], g["L3_cond_ln_b"])]
    cols = np.stack([np.concatenate([bqkv[l], b1[l], modbias[l], *ga[l]]).reshape(N_COL, P).T
                     for l in range(LAYERS)], axis=1)
    rows = np.concatenate([
        g["L0_cond_proj_b"], g["L1_cond_proj_b"], g["L2_cond_bproj"], g["L3_cond_bp"],
        g["L0_cond_mlp_b2"], g["L1_cond_fc2_b"], g["L2_cond_b2"], *gatebias,
        by_unit(g["L1_cond_q_bias"], 1), zero,
        g["L1_cond_scale_mul"].reshape(UNITS, 2, 2).transpose(1, 0, 2).reshape(-1), g["L3_cond_ln_g"], g["L3_cond_ln_b"]])
    host = {"x": g["x"], "cond": g["cond_1024"].T, "cols": cols, "rows": rows, "wqkv": wqkv, "wp": wp,
            "w1": w1, "w2": w2, "wmod": wmod, "wgate": wgate}

    nc = bacc.Bacc("TRN2", target_bir_lowering=False, num_devices=1, dynamic_dma_scratch_size=4096)
    arrays, args = {}, []
    for name, a in host.items():
        a = np.ascontiguousarray(a)
        arrays[f"in_{name}"] = a
        args.append(nc.dram_tensor(f"in_{name}", a.shape, mybir.dt.from_np(a.dtype), kind="ExternalInput").ap())
    out = nc.dram_tensor("out", (BATCH, TOK, DIM), F32, kind="ExternalOutput").ap()
    cond_blocks_kernel(nc, *args, out)
    r = run_bass_kernel_spmd(nc, [arrays], core_ids=[0])
    return r.results[0]["out"]
```

```python
from contextlib import ExitStack

import concourse.bass as bass
from concourse import mybir

F32 = mybir.dt.float32
F32R = mybir.dt.float32r
ALU = mybir.AluOpType
ACT = mybir.ActivationFunctionType
AX_X = mybir.AxisListType.X

LAYERS, BATCH, TOK, DIM, HID = 4, 4, 512, 256, 1024
HEADS, HD = 16, 16
P = 128
CH = DIM // P
TT = TOK // P
MT = HID // P
UNITS = HEADS // 4
JOBS = LAYERS * BATCH
TICKS = UNITS * TT
LEAD = 6
RING = 4
SBANKS = 3
PROBS = 8
BLK = 64
KS = 3 * HD
EPS = (1e-6, 1e-6, 1e-5, 1e-5)
SCALE = (DIM ** -0.5, 1.0, HD ** -0.5, 1.0)
C_Q, C_K, C_V, C_B1, C_MB, C_G, C_BE, N_COL = 0, 2, 4, 6, 14, 22, 26, 30
R_PB, R_FB, R_GB, R_QK, R_SM, R_LG, R_LB = 0, 1024, 1792, 3328, 3840, 3856, 4112
N_ROW = 4368


def layer(j):
    return j // BATCH


def batch(j):
    return j % BATCH


def multi(j):
    return layer(j) > 0


def prep(j):
    at = {t: [] for t in range(TICKS)}
    if j >= JOBS:
        return at
    at[0] += [("stat1", j, 0)]
    at[1] += [("norm1", j, 0)]
    at[2] += [("hT1", j, c) for c in range(CH)]
    if layer(j) == 1:
        at[3] += [("qktok", j, 0), ("qktok", j, 1)]
        at[4] += [("qkss", j, 0), ("qktok", j, 2), ("qkss", j, 1), ("qktok", j, 3)]
        at[5] += [("v", j, 0), ("qkss", j, 2)]
        at[6] += [("v", j, 1), ("qkss", j, 3)]
        at[7] += [("qknorm", j, t) for t in range(TT)]
        at[8] += [(x, j, i) for i in range(2) for x in "qk"]
        at[8] += [("stack", UNITS * j, 0)]
    else:
        at[3] += [("q", j, 0), ("k", j, 0)]
        at[4] += [("q", j, 1)]
        at[5] += [("k", j, 1)]
        at[6] += [("v", j, 0)]
        at[7] += [("v", j, 1)]
        at[6] += [("stack", UNITS * j, 0)]
    at[9] += [("stack", UNITS * j + 1, 0)]
    at[12] += [("stack", UNITS * j + 2, 0)]
    return at


def post(j):
    at = {t: [] for t in range(TICKS)}
    if multi(j):
        at[1] += [("oT1", j, c) for c in range(TT)]
        at[3] += [("oT2", j, c) for c in range(CH)]
    at[3] += [("proj", j, 0)]
    at[4] += [("proj", j, 1)]
    at[5] += [("stat2", j, 0)]
    at[6] += [("norm2", j, 0)]
    if layer(j) < LAYERS - 1:
        at[8] += [("hT2", j, c) for c in range(CH)]
        for m, t in enumerate((8, 8, 9, 9, 10, 10, 11, 11)):
            at[t] += [("fc1", j, m)]
        at[10] += [("gelu", j, 0)]
        at[12] += [("gelu", j, 1)]
        for t in range(TT):
            at[12 + t] += [("fc2", j, t)]
    else:
        for t in range(TT):
            at[7 + t] += [("final", j, t)]
    return at


def spread(main, rest):
    out, n = [], 0
    for i, step in enumerate(main):
        out.append(step)
        upto = len(rest) * (i + 1) // len(main)
        out += rest[n:upto]
        n = upto
    return out + rest[n:]


def single_window(w):
    j, n = w - 1, w + 1
    steps = [("scores0", w, 0), ("scores0", w, 1)]
    hT = [("hT1", n, c) for c in range(CH)]
    proj = [("proj", j, 0), ("proj", j, 1)] if j >= 0 else []
    steps += proj[:1] + [("soft0", w, 0), ("scores0", w, 2)] + proj[1:] + [("soft0", w, 1), ("scores0", w, 3)]
    steps += hT[:1] + [("soft0", w, 2)] + hT[1:] + [("soft0", w, 3)]
    if j >= 0:
        steps += [("stat2", j, 0)]
    pT = [("pT0", w, t) for t in range(TT)]
    if layer(n) == 0:
        steps += spread(pT, [("q", n, 0), ("k", n, 0), ("q", n, 1), ("k", n, 1)])
        if j >= 0:
            steps += [("norm2", j, 0)]
        steps += [("v", n, 0), ("v", n, 1)]
    else:
        steps += spread(pT, [("qktok", n, 0), ("qktok", n, 1), ("qkss", n, 0), ("qktok", n, 2)])
        steps += [("vones", n, 0), ("norm2", j, 0), ("qkss", n, 1), ("qktok", n, 3), ("qkss", n, 2)]
        steps += [("v", n, 0), ("qkss", n, 3), ("v", n, 1)]
    steps += [("av0", w, 0), ("av0", w, 1)]
    fc1, fc2, stat = [], [], []
    if j >= 0:
        steps += [("hT2", j, c) for c in range(CH)]
        fc1 = [("fc1", j, m) for m in range(MT)]
        fc1[6:6] = [("gelu", j, 0)]
        fc1 += [("gelu", j, 1)]
        fc2 = [("fc2", j, t) for t in range(TT)]
    if n + 1 < BATCH + 1:
        stat = [("stat1", n + 1, 0), ("norm1", n + 1, 0)]
    if layer(n) == 0:
        steps += fc1[:4] + stat[:1] + fc1[4:] + stat[1:] + fc2
        return steps
    u = UNITS * n
    steps += fc1[:2] + [("qknorm", n, t) for t in range(TT)] + fc1[2:4]
    steps += [(x, n, i) for i in range(2) for x in "qk"] + [("stack", u, 0), ("stack", u + 1, 0), ("stack", u + 2, 0)]
    steps += fc1[4:]
    steps += spread(fc2, [("max", u, i) for i in range(16)])
    steps += [("shift", u, 0)] + [("max", u + 1, i) for i in range(8)]
    return steps


def multi_window(w):
    before, after = post(w - 1), prep(w + 1)
    plan, last = [], layer(w) == LAYERS - 1
    for t in range(TICKS):
        g, c = divmod(t, TT)
        rest = before[t] + after[t]
        if t == 0:
            rest = [("stack", UNITS * w + 3, 0)] + rest
        if t == 3 and w == BATCH:
            rest = [("vones", w + 1, 0)] + rest
        if t == 12:
            rest = [("gate", w, 0)] + rest
        if batch(w) == 2 and not last:
            if t == 13:
                rest += [("modrow", layer(w) + 1, i) for i in range(mod_rows(layer(w) + 1))]
            if t == 14:
                rest += [("mod", layer(w) + 1, 0)]
        v = t + LEAD
        u = UNITS * w + v // TT
        maxima = [("max", u, 4 * (v % TT) + n) for n in range(4)] if u < UNITS * JOBS else []
        if v % TT == 0 and UNITS * w + v // TT - 1 < UNITS * JOBS:
            rest = [("shift", u - 1, 0)] + rest
        s = [("scores", UNITS * w + g, 4 * c + n) for n in range(4)]
        if t > 0:
            av = [("av", UNITS * w + (t - 1) // TT, (t - 1) % TT)]
        else:
            av = [("av", UNITS * w - 1, TT - 1)] if w > BATCH else []
        m = maxima
        if any(step[0] == "gelu" for step in rest):
            n = rest.index(next(step for step in rest if step[0] == "gelu")) + 1
            plan += s[:2] + m[:1] + s[2:] + m[1:2] + rest[:n] + m[2:3] + av + m[3:] + rest[n:]
        else:
            plan += spread(m[:1] + s[:2] + m[1:2] + av + m[2:3] + s[2:] + m[3:], rest)
        if t == 7 and batch(w) == 2 and not last:
            plan.append(("load_qkv", layer(w) + 1, 0))
        if t == 15 and batch(w) == 0:
            plan.append(("load_post", layer(w), 0))
        if t == 15 and batch(w) == 2 and layer(w) < LAYERS - 2:
            plan.append(("load_mod", layer(w) + 2, 0))
        if t == 15 and batch(w) == 3 and not last:
            plan.append(("load_gate", layer(w) + 1, 0))
    return plan


def mod_rows(l):
    return 2 if l < LAYERS - 1 else 1


def plan_steps():
    plan = [("load_mod", 0, 0), ("load_qkv", 0, 0), ("load_post", 0, 0), ("stat1", 0, 0), ("norm1", 0, 0),
            ("modrow", 0, 0), ("modrow", 0, 1), ("mod", 0, 0), ("load_mod", 1, 0), ("load_gate", 1, 0)]
    plan += [s for t in range(2, TICKS) for s in prep(0)[t] if s[0] != "stack"]
    plan += [("stat1", 1, 0), ("norm1", 1, 0)]
    for w in range(BATCH):
        plan += single_window(w)
        if w == 0:
            plan.append(("headscale", 1, 0))
        if w == 2:
            plan += [("load_qkv", 1, 0), ("modrow", 1, 0), ("modrow", 1, 1), ("mod", 1, 0), ("load_mod", 2, 0)]
    for w in range(BATCH, JOBS):
        plan += multi_window(w)
    plan.append(("av", UNITS * JOBS - 1, TT - 1))
    for steps in post(JOBS - 1).values():
        plan += steps
    return plan


PLAN = plan_steps()
RINGED = ("hT1", "v", "qktok", "q", "k", "max", "shift", "oT1", "oT2", "proj", "hT2", "fc1",
          "fc2", "gate", "modrow", "mod", "pT0", "av0")
NTH, USE, USES = {}, {}, []
_count = {}
for _s in PLAN:
    _count[_s[0]] = _count.get(_s[0], 0) + 1
    NTH[_s] = _count[_s[0]]
    if _s[0] in RINGED:
        USE[_s] = len(USES)
        USES.append(_s)


def nth(kind, a, i=0):
    return NTH[(kind, a, i)]


def use(kind, a, i=0):
    return USE[(kind, a, i)] + 1


def cond_blocks_kernel(nc, x, cond, cols, rows, wqkv, wp, w1, w2, wmod, wgate, out):
    x_v = x.rearrange("b (t p) d -> p b t d", p=P)
    out_v = out.rearrange("b (t p) d -> p b t d", p=P)

    with ExitStack() as ctx:
        def sb(name, shape, dt=F32):
            return ctx.enter_context(nc.sbuf_tensor(name, shape, dt))

        def sem(name):
            return ctx.enter_context(nc.semaphore(name))

        X = sb("X", [P, BATCH * TT, DIM])
        ident = sb("ident", [P, P])
        colv = sb("colv", [P, LAYERS, N_COL])
        rowv = sb("rowv", [P, N_ROW])
        condT = sb("condT", [P, CH, BATCH])
        condS = sb("condS", [P, CH, BATCH])
        condE = sb("condE", [P, CH, BATCH])
        condR = sb("condR", [P, CH, BATCH])
        smrow = sb("smrow", [P, HEADS])
        wqkv_s = sb("wqkv_s", [P, CH, 3 * DIM])
        wp_s = sb("wp_s", [P, CH, DIM])
        w1_s = sb("w1_s", [P, CH, HID])
        w2_s = sb("w2_s", [P, MT, DIM])
        wmod_s = sb("wmod_s", [P, CH, 4 * DIM])
        wgate_s = sb("wgate_s", [P, CH, 2 * DIM])
        modr = sb("modr", [P, 8, BATCH])
        mods = sb("mods", [P, 2, 4, BATCH])
        modb = sb("modb", [P, 2, 4, BATCH])
        mrow = sb("mrow", [BATCH, 4 * DIM])
        gates = sb("gates", [P, 2, 2 * DIM])
        tok1 = sb("tok1", [P, TT, DIM])
        tok2 = sb("tok2", [P, TT, DIM])
        hT = sb("hT", [P, CH, TOK])
        postT = sb("postT", [P, CH, TOK])
        qk = sb("qk", [P, 4, TOK])
        sq = sb("sq", [P, TOK])
        qh = sb("qh", [P, 2, TOK], F32R)
        ql = sb("ql", [P, 2, TOK], F32R)
        kh = sb("kh", [P, 2, TOK], F32R)
        kl = sb("kl", [P, 2, TOK], F32R)
        SQ = [sb(f"SQ{i}", [P, 2, TOK], F32R) for i in range(4)]
        SK = [sb(f"SK{i}", [P, 2, TOK], F32R) for i in range(4)]
        VW = HEADS * (HD + 1)
        V = [sb(f"V{i}", [P, TT, VW + 16]) for i in range(2)]
        probs = sb("probs", [P, PROBS, TOK])
        oU = sb("oU", [P, UNITS, TOK])
        gT = sb("gT", [P, MT, TOK])
        tmp = sb("tmp", [P, TT, DIM])
        m16 = sb("m16", [P, 2, 16])
        cT = sb("cT", [16, 2, P], F32R)
        stats = sb("stats", [P, 2, TT, 6])
        mv = sb("mv", [P, 2, TT, 2])
        var = sb("var", [P, 2, TT])
        rstd = sb("rstd", [P, 2, TT])
        mhalf = sb("mhalf", [P, 2 * HEADS])
        ss = sb("ss", [P, TT, 2 * HEADS])
        rs = sb("rs", [P, TT, 2 * HEADS])
        rcp = sb("rcp", [P, 2, HEADS])
        nm0 = sb("nm0", [P, TT])
        nb0 = sb("nb0", [P, TT])
        sum0 = sb("sum0", [P, TT])
        rc0 = sb("rc0", [P, TT])

        ST = [ctx.enter_context(nc.psum_tensor(f"ST{i}", [P, TOK], F32)) for i in range(SBANKS)]
        AVB = ctx.enter_context(nc.psum_tensor("AVB", [P, TOK], F32))
        ring = [ctx.enter_context(nc.psum_tensor(f"ring{i}", [P, TOK], F32)) for i in range(RING)]

        def bank(kind, a, i=0):
            return ring[USE[(kind, a, i)] % RING]

        kinds = sorted({s[0] for s in PLAN if not s[0].startswith("load") and s[0] != "stack"})
        done = {k: sem("done_" + k) for k in kinds}
        pe_ring = sem("pe_ring")
        pe_scores = sem("pe_scores")
        pe_av = sem("pe_av")
        pe_s0 = sem("pe_s0")
        unit_out = sem("unit_out")
        hi_ready = sem("hi_ready")
        sq_ready = sem("sq_ready")
        var1, var2 = sem("var1"), sem("var2")
        rstd1, rstd2 = sem("rstd1"), sem("rstd2")
        ss_ready = sem("ss_ready")
        nb_ready = sem("nb_ready")
        exp0 = sem("exp0")
        y1, y2 = sem("y1"), sem("y2")
        stacked = [sem(f"stacked{i}") for i in range(4)]
        shifted = [sem(f"shifted{i}") for i in range(2)]
        x_in = [sem(f"x_in{b}") for b in range(BATCH)]
        cond_in, cols_in, rows_in = sem("cond_in"), sem("cols_in"), sem("rows_in")
        in_qkv, in_post, in_mod, in_gate = sem("in_qkv"), sem("in_post"), sem("in_mod"), sem("in_gate")
        out_sem = sem("out_sem")
        dve_seq, act_seq, pool_seq = sem("dve_seq"), sem("act_seq"), sem("pool_seq")
        const_ready = sem("const_ready")
        cond_ready = sem("cond_ready")
        e_ready = sem("e_ready")
        clip_ready = sem("clip_ready")

        def post_loads(l):
            return 3 if l < LAYERS - 1 else 1

        POST_IN = [16 * sum(post_loads(i) for i in range(l + 1)) for l in range(LAYERS)]

        def STACK_IN(u):
            return 16 * 12 * ((u - UNITS * BATCH) // 4 + 1)

        def SHIFT_IN(u):
            return 16 * 2 * ((u - UNITS * BATCH) // 2 + 1)

        def slot_free(eng, u):
            if u - 4 >= UNITS * BATCH:
                eng.wait_ge(pe_scores, nth("scores", u - 4, 4 * TT - 1))

        def unit_job(u):
            return u // UNITS

        def wcond(l):
            return condS if l in (1, 2) else condT

        block = ctx.enter_context(nc.Block())

        @block.sync
        def _(sp):
            sp.dma_start(condT[:, :, :], cond.rearrange("(c p) b -> p c b", p=P)).then_inc(cond_in, 16)
            sp.dma_start(colv[:, :, :], cols).then_inc(cols_in, 16)
            sp.dma_start(X[:, 0:TT, :], x_v[:, 0]).then_inc(x_in[0], 16)
            for kind, a, i in PLAN:
                if kind == "load_qkv":
                    if a > 0:
                        j = (a - 1) * BATCH + 3
                        sp.wait_ge(pe_ring, use("v", j, 1))
                    sp.dma_start(wqkv_s[:, :, :], wqkv[a].rearrange("(c p) n -> p c n", p=P)).then_inc(in_qkv, 16)
                    if a == 0:
                        sp.dma_start(rowv[:, :], rows.partition_broadcast(P)).then_inc(rows_in, 16)
                        for b in range(1, BATCH):
                            sp.dma_start(X[:, b * TT:(b + 1) * TT, :], x_v[:, b]).then_inc(x_in[b], 16)
                elif kind == "load_post":
                    if a > 0:
                        sp.wait_ge(pe_ring, use("fc2", a * BATCH - 1, TT - 1))
                    sp.dma_start(wp_s[:, :, :], wp[a].rearrange("(c p) n -> p c n", p=P)).then_inc(in_post, 16)
                    if a < LAYERS - 1:
                        sp.dma_start(w1_s[:, :, :], w1[a].rearrange("(c p) n -> p c n", p=P)).then_inc(in_post, 16)
                        sp.dma_start(w2_s[:, :, :], w2[a].rearrange("(m p) n -> p m n", p=P)).then_inc(in_post, 16)
                elif kind == "load_mod":
                    if a > 0:
                        sp.wait_ge(pe_ring, use("modrow", a - 1, mod_rows(a - 1) - 1))
                    sp.dma_start(wmod_s[:, :, :], wmod[a].rearrange("(c p) n -> p c n", p=P)).then_inc(in_mod, 16)
                elif kind == "load_gate":
                    if a > 1:
                        sp.wait_ge(pe_ring, use("gate", a * BATCH - 1))
                    sp.dma_start(wgate_s[:, :, :], wgate[a - 1].rearrange("(c p) n -> p c n", p=P)).then_inc(in_gate, 16)
                elif kind == "stack":
                    j, g = divmod(a, UNITS)
                    sp.wait_ge(done["k"], nth("k", j, 1))
                    sp.wait_ge(done["q"], nth("q", j, 1))
                    slot_free(sp, a)
                    sp.wait_ge(const_ready, 1)
                    for stack, parts in ((SQ[a % 4], (qh, ql, qh)), (SK[a % 4], (kh, kh, kl))):
                        for r, part in enumerate(parts):
                            for par in range(2):
                                src = part[2 * HD * g + HD * par:2 * HD * g + HD * par + HD, :, :]
                                dst = stack[BLK * par + HD * r:BLK * par + HD * r + HD, :, :]
                                sp.dma_start(dst.bitcast(F32), src.bitcast(F32)).then_inc(stacked[a % 4], 16)
                elif kind == "shift":
                    sp.wait_ge(done["shift"], nth("shift", a))
                    for par in range(2):
                        d = SQ[a % 4][BLK * par + KS:BLK * par + KS + 1, :, :]
                        dst = bass.AP(d.tensor, d.offset, [[2 * TOK, 1], [P, 8], [1, P]]).bitcast(F32)
                        s = cT[8 * par:8 * par + 8, a % 2, :]
                        src = bass.AP(s.tensor, s.offset, [[2 * P, 8], [P, 1], [1, P]]).bitcast(F32)
                        sp.dma_start(dst, s.bitcast(F32)).then_inc(shifted[a % 2], 16)
                elif kind == "final":
                    sp.wait_ge(done["final"], nth("final", a, i))
                    sp.dma_start(out_v[:, batch(a), i], tok2[:, i, :]).then_inc(out_sem, 16)
            sp.wait_ge(out_sem, 16 * BATCH * TT)

        @block.tensor
        def _(pe):
            def claim(kind, a, i):
                n = USE[(kind, a, i)]
                if n >= RING:
                    k, b, m = USES[n - RING]
                    pe.wait_ge({"proj": y1, "fc2": y2}.get(k, done[k]), nth(k, b, m))
                return ring[n % RING]

            pe.wait_ge(const_ready, 1)
            for kind, a, i in PLAN:
                o = claim(kind, a, i) if kind in RINGED else None
                mm = None
                if kind in ("q", "k", "qktok", "v"):
                    pe.wait_ge(done["hT1"], nth("hT1", a, CH - 1))
                    pe.wait_ge(in_qkv, 16 * (layer(a) + 1))
                if kind == "modrow":
                    pe.wait_ge(in_mod, 16 * (a + 1))
                    pe.wait_ge(cond_ready, 1)
                    for c in range(CH):
                        mm = pe.matmul(o[0:BATCH, :], wcond(a)[:, c, :], wmod_s[:, c, i * TOK:(i + 1) * TOK],
                                       start=(c == 0), stop=(c == CH - 1))
                elif kind == "mod":
                    pe.wait_ge(done["modrow"], nth("modrow", a, mod_rows(a) - 1))
                    for m in range(4 * mod_rows(a)):
                        mm = pe.transpose(o[:, BATCH * m:BATCH * (m + 1)], mrow[:, m * P:(m + 1) * P],
                                          ident[0:BATCH, 0:BATCH])
                elif kind == "gate":
                    pe.wait_ge(in_gate, 16 * layer(a))
                    pe.wait_ge(cond_ready, 1)
                    for c in range(CH):
                        mm = pe.matmul(o[:, :], wcond(layer(a))[:, c, batch(a):batch(a) + 1].to_broadcast([P, P]),
                                       wgate_s[:, c, :], start=(c == 0), stop=(c == CH - 1))
                elif kind in ("hT1", "hT2"):
                    src = tok1 if kind == "hT1" else tok2
                    norm = "norm1" if kind == "hT1" else "norm2"
                    pe.wait_ge(done[norm], nth(norm, a))
                    for t in range(TT):
                        mm = pe.transpose(o[:, t * P:(t + 1) * P], src[:, t, i * P:(i + 1) * P], ident[:, :])
                elif kind == "v":
                    for t in range(2):
                        for c in range(CH):
                            tok = (2 * i + t) * P
                            mm = pe.matmul(o[:, t * DIM:(t + 1) * DIM], hT[:, c, tok:tok + P],
                                           wqkv_s[:, c, 2 * DIM:3 * DIM], start=(c == 0), stop=(c == CH - 1))
                elif kind == "qktok":
                    for c in range(CH):
                        mm = pe.matmul(o[:, :], hT[:, c, i * P:(i + 1) * P], wqkv_s[:, c, 0:2 * DIM],
                                       start=(c == 0), stop=(c == CH - 1))
                elif kind in ("q", "k"):
                    off = DIM * (kind == "k") + i * P
                    if layer(a) == 1:
                        pe.wait_ge(done["qknorm"], nth("qknorm", a, TT - 1))
                        for t in range(TT):
                            mm = pe.transpose(o[:, t * P:(t + 1) * P], qk[:, t, off:off + P], ident[:, :])
                    else:
                        for c in range(CH):
                            mm = pe.matmul(o[:, :], wqkv_s[:, c, off:off + P], hT[:, c, :],
                                           start=(c == 0), stop=(c == CH - 1))
                elif kind == "max":
                    if i == 0:
                        pe.wait_ge(stacked[a % 4], STACK_IN(a))
                    n, c = i % 4, i // 4
                    r = BLK * (n % 2)
                    mm = pe.matmul(o[:, :], SQ[a % 4][r:r + KS, n // 2, c * P:(c + 1) * P],
                                   SK[a % 4][r:r + KS, n // 2, :], start=True, stop=True)
                elif kind == "shift":
                    pe.wait_ge(done["max"], nth("max", a, 15))
                    mm = pe.transpose(o[0:16, 0:P], m16[:, a % 2, :], ident[:, :])
                elif kind == "scores":
                    t, c, n = nth("scores", a, i) - 1, i // 4, i % 4
                    if i == 0:
                        pe.wait_ge(shifted[a % 2], SHIFT_IN(a))
                    if t >= SBANKS:
                        pe.wait_ge(done["scores"], t + 1 - SBANKS)
                    else:
                        pe.wait_ge(exp0, BATCH * TT)
                    r = BLK * (n % 2)
                    mm = pe.matmul(ST[t % SBANKS][:, :], SK[a % 4][r:r + KS + 1, n // 2, c * P:(c + 1) * P],
                                   SQ[a % 4][r:r + KS + 1, n // 2, :], start=True, stop=True)
                    mm.then_inc(pe_scores, 1)
                    continue
                elif kind == "av":
                    j, g = divmod(a, UNITS)
                    t = nth("av", a, i) - 1
                    if i == 0:
                        pe.wait_ge(done["v"], nth("v", j, 1))
                        if t > 0:
                            pe.wait_ge(unit_out, t // TT)
                    for n in range(4):
                        pe.wait_ge(done["scores"], 4 * t + n + 1)
                        h = 4 * g + n
                        mm = pe.matmul(AVB[32 * n:32 * n + 32, :], V[j % 2][:, i, (HD + 1) * h:(HD + 1) * h + 32],
                                       probs[:, (4 * t + n) % PROBS, :],
                                       start=(i == 0), stop=(i == TT - 1))
                    mm.then_inc(pe_av, 1)
                    continue
                elif kind == "scores0":
                    t = nth("scores0", a, i) - 1
                    if i == 0:
                        pe.wait_ge(done["q"], nth("q", a, 1))
                        pe.wait_ge(done["k"], nth("k", a, 1))
                    if t >= SBANKS:
                        pe.wait_ge(exp0, t + 1 - SBANKS)
                    for c in range(CH):
                        mm = pe.matmul(ST[t % SBANKS][:, :], qk[:, c, i * P:(i + 1) * P], qk[:, 2 + c, :],
                                       start=(c == 0), stop=(c == CH - 1))
                    mm.then_inc(pe_s0, 1)
                    continue
                elif kind == "pT0":
                    pe.wait_ge(done["soft0"], nth("soft0", a, i))
                    for t in range(TT):
                        mm = pe.transpose(o[:, t * P:(t + 1) * P], probs[:, i, t * P:(t + 1) * P], ident[:, :])
                elif kind == "av0":
                    pe.wait_ge(done["pT0"], nth("pT0", a, TT - 1))
                    pe.wait_ge(done["v"], nth("v", a, 1))
                    for t in range(TT):
                        mm = pe.matmul(o[:, :], V[a % 2][:, t, i * P:(i + 1) * P], gT[:, t, :],
                                       start=(t == 0), stop=(t == TT - 1))
                elif kind == "oT1":
                    pe.wait_ge(unit_out, UNITS * (a + 1 - BATCH))
                    for g in range(UNITS):
                        mm = pe.transpose(o[:, g * P:(g + 1) * P], oU[:, g, i * P:(i + 1) * P], ident[:, :])
                elif kind == "oT2":
                    pe.wait_ge(done["oT1"], nth("oT1", a, TT - 1))
                    for t in range(TT):
                        mm = pe.transpose(o[:, t * P:(t + 1) * P], tok2[:, t, i * P:(i + 1) * P], ident[:, :])
                elif kind == "proj":
                    if multi(a):
                        pe.wait_ge(done["oT2"], nth("oT2", a, CH - 1))
                    else:
                        pe.wait_ge(done["av0"], nth("av0", a, 1))
                    pe.wait_ge(in_post, POST_IN[layer(a)])
                    for t in range(2):
                        tok = (2 * i + t) * P
                        for c in range(CH):
                            src = postT[:, c, tok:tok + P] if multi(a) else oU[:, 2 + c, tok:tok + P]
                            mm = pe.matmul(o[:, t * DIM:(t + 1) * DIM], src, wp_s[:, c, :],
                                           start=(c == 0), stop=(c == CH - 1))
                elif kind == "fc1":
                    pe.wait_ge(done["hT2"], nth("hT2", a, CH - 1))
                    for c in range(CH):
                        mm = pe.matmul(o[:, :], w1_s[:, c, i * P:(i + 1) * P], postT[:, c, :],
                                       start=(c == 0), stop=(c == CH - 1))
                elif kind == "fc2":
                    for m in range(MT):
                        if m % (MT // 2) == 0:
                            pe.wait_ge(done["gelu"], nth("gelu", a, m // (MT // 2)))
                        mm = pe.matmul(o[:, 0:DIM], gT[:, m, i * P:(i + 1) * P], w2_s[:, m, :],
                                       start=(m == 0), stop=(m == MT - 1))
                if mm is not None:
                    mm.then_inc(pe_ring, 1)

        @block.scalar
        def _(act):
            act.wait_ge(cond_in, 16)
            act.activation(condE[:, :, :], condT[:, :, :], ACT.Exp, scale=-1.0).then_inc(e_ready, 1)
            act.wait_ge(cols_in, 16)
            for kind, a, i in PLAN:
                if kind == "headscale":
                    act.wait_ge(clip_ready, 1)
                    act.activation(smrow[:, :], smrow[:, :], ACT.Exp).then_inc(done[kind], 1)
                elif kind == "modrow":
                    act.wait_ge(pe_ring, use(kind, a, i))
                    if a > 0:
                        act.wait_ge(pe_ring, use("mod", a - 1))
                    act.activation(mrow[:, i * TOK:(i + 1) * TOK], bank(kind, a, i)[0:BATCH, :], ACT.Copy
                                   ).then_inc(done[kind], 1)
                elif kind in ("hT1", "hT2"):
                    l, b, second = layer(a), batch(a), kind == "hT2"
                    act.wait_ge(pe_ring, use(kind, a, i))
                    act.wait_ge(done["mod"], nth("mod", l))
                    n = 2 * second + i
                    if not second and a > 0 and i == 0:
                        act.wait_ge(pe_ring, use("v", a - 1, 1))
                    if second and i == 0:
                        act.wait_ge(pe_ring, use("proj", a, 1))
                        if a > 0:
                            act.wait_ge(pe_ring, use("fc1", a - 1, MT - 1))
                    dst = postT if second else hT
                    act.activation(dst[:, i, :], bank(kind, a, i)[:, :], ACT.Identity,
                                   bias=modb[:, l % 2, n, b:b + 1], scale=mods[:, l % 2, n, b:b + 1]
                                   ).then_inc(done[kind], 1)
                elif kind == "v":
                    act.wait_ge(pe_ring, use(kind, a, i))
                    if i == 0 and a >= 2:
                        if multi(a - 2):
                            act.wait_ge(pe_av, nth("av", UNITS * (a - 1) - 1, TT - 1))
                        else:
                            act.wait_ge(pe_ring, use("av0", a - 2, 1))
                    src = bank(kind, a, i)
                    if multi(a):
                        if layer(a) == 1 and batch(a) < 2 and i == 0:
                            act.wait_ge(done["vones"], batch(a) + 1)
                        for t in range(2):
                            dst = V[a % 2][:, 2 * i + t, 0:VW].rearrange("p (h e) -> p h e", e=HD + 1)[:, :, 0:HD]
                            ins = act.activation(dst, src[:, t * DIM:(t + 1) * DIM].rearrange("p (h d) -> p h d", d=HD),
                                                 ACT.Copy)
                        ins.then_inc(done["v"], 1)
                    else:
                        act.activation(V[a % 2][:, 2 * i:2 * i + 2, 0:DIM],
                                       src[:, :].rearrange("p (t d) -> p t d", t=2), ACT.Copy).then_inc(done["v"], 1)
                elif kind == "qkss":
                    t = nth(kind, a, i) - 1
                    act.wait_ge(done["qktok"], t + 1)
                    if t >= 1:
                        act.wait_ge(ss_ready, t)
                    act.activation(sq[:, :], qk[:, i, :], ACT.Square).then_inc(sq_ready, 1)
                elif kind in ("q", "k"):
                    l = layer(a)
                    act.wait_ge(pe_ring, use(kind, a, i))
                    col = (C_Q if kind == "q" else C_K) + i
                    if l == 0:
                        if a > 0:
                            act.wait_ge(pe_s0, nth("scores0", a - 1, TT - 1))
                        act.activation(qk[:, 2 * (kind == "k") + i, :], bank(kind, a, i)[:, :], ACT.Identity,
                                       bias=colv[:, l, col:col + 1]).then_inc(done[kind], 1)
                    else:
                        if a > BATCH:
                            for g in range(UNITS):
                                act.wait_ge(stacked[g], STACK_IN(UNITS * (a - 1) + g))
                        hi = qh if kind == "q" else kh
                        if l == 1:
                            act.activation(hi[:, i, :], bank(kind, a, i)[:, :], ACT.Copy).then_inc(hi_ready, 1)
                        else:
                            act.activation(hi[:, i, :], bank(kind, a, i)[:, :], ACT.Identity,
                                           bias=colv[:, l, col:col + 1]).then_inc(hi_ready, 1)
                elif kind == "scores":
                    n = nth("scores", a, i) - 1
                    act.wait_ge(pe_scores, n + 1)
                    if n >= PROBS:
                        act.wait_ge(pe_av, (n - PROBS) // 4 + 1)
                    elif n == 0:
                        act.wait_ge(pe_ring, use("pT0", BATCH - 1, TT - 1))
                    act.activation(probs[:, n % PROBS, :], ST[n % SBANKS][:, :], ACT.Exp,
                                   scale=SCALE[layer(unit_job(a))]).then_inc(done["scores"], 1)
                elif kind == "scores0":
                    t = nth("scores0", a, i) - 1
                    act.wait_ge(nb_ready, t + 1)
                    if t >= TT:
                        act.wait_ge(pe_ring, use("pT0", a - 1, i))
                        act.wait_ge(done["soft0"], nth("soft0", a - 1, i))
                    act.activation(probs[:, i, :], ST[t % SBANKS][:, :], ACT.Exp, bias=nb0[:, i:i + 1],
                                   scale=SCALE[0], accum_out=sum0[:, i:i + 1]).then_inc(exp0, 1)
                elif kind == "pT0":
                    act.wait_ge(pe_ring, use(kind, a, i))
                    if a > 1:
                        act.wait_ge(pe_ring, use("fc2", a - 2, TT - 1))
                    if a > 0:
                        act.wait_ge(pe_ring, use("av0", a - 1, 1))
                    act.activation(gT[:, 0:TT, i * P:(i + 1) * P],
                                   bank(kind, a, i)[:, :].rearrange("p (k q) -> p k q", k=TT),
                                   ACT.Copy).then_inc(done[kind], 1)
                elif kind == "av0":
                    act.wait_ge(pe_ring, use(kind, a, i))
                    if a > 0:
                        act.wait_ge(pe_ring, use("proj", a - 1, 1))
                    act.activation(oU[:, 2 + i, :], bank(kind, a, i)[:, :], ACT.Identity,
                                   bias=colv[:, 0, C_V + i:C_V + i + 1]).then_inc(done[kind], 1)
                elif kind == "av" and i == TT - 1:
                    act.wait_ge(pe_av, nth("av", a, i))
                    j, g = divmod(a, UNITS)
                    if g == 0 and j > BATCH:
                        act.wait_ge(pe_ring, use("oT1", j - 1, TT - 1))
                    if g == 2 and j == BATCH:
                        act.wait_ge(pe_ring, use("proj", j - 1, 1))
                    act.activation(oU[:, g, :], AVB[:, :], ACT.Copy).then_inc(unit_out, 1)
                elif kind == "oT2":
                    l = layer(a)
                    act.wait_ge(pe_ring, use(kind, a, i))
                    if i == 0 and layer(a - 1) < LAYERS - 1:
                        act.wait_ge(pe_ring, use("fc1", a - 1, MT - 1))
                    elif i == 0:
                        act.wait_ge(pe_ring, use("proj", a - 1, 1))
                    act.activation(postT[:, i, :], bank(kind, a, i)[:, :], ACT.Identity,
                                   bias=colv[:, l, C_V + i:C_V + i + 1],
                                   scale=(1.0 if l < LAYERS - 1 else DIM ** -0.5)).then_inc(done[kind], 1)
                elif kind == "gelu":
                    half = gT[:, i * MT // 2:(i + 1) * MT // 2, :]
                    act.wait_ge(done["fc1"], nth("fc1", a, (i + 1) * MT // 2 - 1))
                    act.activation(half, half, ACT.Gelu).then_inc(done[kind], 1)

        @block.vector
        def _(dve):
            n_seq = [0]

            def link(ins):
                n_seq[0] += 1
                ins.then_inc(dve_seq, 1)
                dve.wait_ge(dve_seq, n_seq[0])

            for i in range(4):
                nc.vector.memset(SK[i][:, :, :].bitcast(F32), 1.0)
            link(nc.vector.memset(mhalf[:, :], -0.5))
            dve.wait_ge(e_ready, 1)
            link(nc.vector.tensor_scalar(condR[:, :, :], condE[:, :, :], 1.0, None, ALU.add))
            link(nc.vector.reciprocal(condE[:, :, :], condR[:, :, :]))
            nc.vector.tensor_tensor(condS[:, :, :], condT[:, :, :], condE[:, :, :], ALU.mult).then_inc(cond_ready, 1)
            dve.wait_ge(cols_in, 16)

            for kind, a, i in PLAN:
                if kind == "headscale":
                    nc.vector.tensor_scalar(colv[:, LAYERS - 1, C_V:C_V + 2], colv[:, LAYERS - 1, C_V:C_V + 2],
                                            DIM ** -0.5, None, ALU.mult)
                    dve.wait_ge(rows_in, 16)
                    nc.vector.tensor_scalar(smrow[:, :], rowv[:, R_SM:R_SM + HEADS], LOG100, None, ALU.min
                                            ).then_inc(clip_ready, 1)
                elif kind == "mod":
                    l, q = a, a % 2
                    n = 8 if l < LAYERS - 1 else 4
                    dve.wait_ge(pe_ring, use(kind, a))
                    if l >= 2:
                        dve.wait_ge(done["hT2"], nth("hT2", (l - 1) * BATCH - 1, CH - 1))
                    mb = colv[:, l, C_MB:C_MB + n].unsqueeze(2).to_broadcast([P, n, BATCH])
                    link(nc.vector.tensor_tensor(modr[:, 0:n, :], bank(kind, a)[:, 0:n * BATCH].rearrange(
                        "p (m b) -> p m b", b=BATCH), mb, ALU.add))
                    for s in range(n // 4):
                        sc, sh = modr[:, 4 * s:4 * s + 2, :], modr[:, 4 * s + 2:4 * s + 4, :]
                        g = colv[:, l, C_G + 2 * s:C_G + 2 * s + 2].unsqueeze(2).to_broadcast([P, 2, BATCH])
                        be = colv[:, l, C_BE + 2 * s:C_BE + 2 * s + 2].unsqueeze(2).to_broadcast([P, 2, BATCH])
                        if l < LAYERS - 1:
                            link(nc.vector.tensor_scalar(sc, sc, 1.0, None, ALU.add))
                        nc.vector.tensor_tensor(mods[:, q, 2 * s:2 * s + 2, :], sc, g, ALU.mult)
                        link(nc.vector.tensor_tensor(sc, sc, be, ALU.mult))
                        ins = nc.vector.tensor_tensor(modb[:, q, 2 * s:2 * s + 2, :], sc, sh, ALU.add)
                    ins.then_inc(done["mod"], 1)
                elif kind == "fc1":
                    dve.wait_ge(pe_ring, use(kind, a, i))
                    if i == 0:
                        if a > 0:
                            dve.wait_ge(pe_ring, use("fc2", a - 1, TT - 1))
                        if a + 1 < BATCH:
                            dve.wait_ge(pe_ring, use("av0", a + 1, 1))
                    col = C_B1 + i
                    nc.vector.tensor_scalar(gT[:, i, :], bank(kind, a, i)[:, :], colv[:, layer(a), col:col + 1],
                                            None, ALU.add).then_inc(done[kind], 1)
                elif kind == "vones":
                    dve.wait_ge(pe_ring, use("av0", a - 2, 1))
                    nc.vector.memset(V[a % 2][:, :, :], 1.0).then_inc(done[kind], 1)
                elif kind == "gate":
                    l, b = layer(a), batch(a)
                    dve.wait_ge(pe_ring, use(kind, a))
                    if a - 2 >= BATCH and layer(a - 2) < LAYERS - 1:
                        dve.wait_ge(done["fc2"], nth("fc2", a - 2, TT - 1))
                    elif a - 2 >= BATCH:
                        dve.wait_ge(done["final"], nth("final", a - 2, TT - 1))
                    nc.vector.tensor_tensor(gates[:, a % 2, :], bank(kind, a)[:, :],
                                            rowv[:, R_GB + 512 * (l - 1):R_GB + 512 * l], ALU.add
                                            ).then_inc(done["gate"], 1)
                elif kind in ("stat1", "stat2"):
                    w = int(kind == "stat2")
                    l, b = layer(a), batch(a)
                    if w:
                        dve.wait_ge(done["proj"], nth("proj", a, 1))
                    elif l == 0:
                        dve.wait_ge(x_in[b], 16)
                    else:
                        dve.wait_ge(done["fc2"], nth("fc2", a - BATCH, TT - 1))
                    for t in range(TT):
                        ins = nc.vector.bn_stats(stats[:, w, t, :], X[:, TT * b + t, :])
                    link(ins)
                    for t in range(TT):
                        ins = nc.vector.bn_aggr(mv[:, w, t, :], stats[:, w, t, :])
                    if l == 0:
                        link(ins)
                        link(nc.vector.tensor_tensor(var[:, w, :], mv[:, w, :, 0], mv[:, w, :, 0], ALU.mult))
                        ins = nc.vector.tensor_tensor(var[:, w, :], var[:, w, :], mv[:, w, :, 1], ALU.add)
                    ins.then_inc(done[kind], 1)
                elif kind in ("norm1", "norm2"):
                    w = int(kind == "norm2")
                    l, b = layer(a), batch(a)
                    dst = tok2 if w else tok1
                    dve.wait_ge(rstd2 if w else rstd1, nth(kind, a))
                    if w:
                        if multi(a):
                            dve.wait_ge(pe_ring, use("oT2", a, CH - 1))
                        if a > 0 and not multi(a):
                            dve.wait_ge(pe_ring, use("hT2", a - 1, CH - 1))
                    elif a > 0:
                        dve.wait_ge(pe_ring, use("hT1", a - 1, CH - 1))
                    for t in range(TT):
                        if l == 0:
                            ins = nc.vector.tensor_scalar(dst[:, t, :], X[:, TT * b + t, :], rstd[:, w, t:t + 1],
                                                          None, ALU.mult)
                        else:
                            ins = nc.vector.tensor_scalar(dst[:, t, :], X[:, TT * b + t, :], mv[:, w, t, 0:1],
                                                          rstd[:, w, t:t + 1], ALU.subtract, ALU.mult)
                    ins.then_inc(done[kind], 1)
                elif kind == "qktok":
                    dve.wait_ge(pe_ring, use(kind, a, i))
                    if a == BATCH:
                        dve.wait_ge(pe_s0, nth("scores0", BATCH - 1, TT - 1))
                    else:
                        dve.wait_ge(pe_ring, use("k", a - 1, 1))
                    nc.vector.tensor_tensor(qk[:, i, :], bank(kind, a, i)[:, :], rowv[:, R_QK:R_QK + TOK],
                                            ALU.add).then_inc(done[kind], 1)
                elif kind == "qkss":
                    t = nth(kind, a, i) - 1
                    dve.wait_ge(sq_ready, t + 1)
                    if a > BATCH and i == 0:
                        dve.wait_ge(done["qkss"], nth("qkss", a - 1, TT - 1))
                    nc.vector.tensor_reduce(ss[:, i, :], sq[:, :].rearrange("p (h d) -> p h d", d=HD),
                                            AX_X, ALU.add).then_inc(ss_ready, 1)
                elif kind == "qknorm":
                    dve.wait_ge(done["qkss"], nth("qkss", a, i))
                    r = rs[:, i, :].unsqueeze(2).to_broadcast([P, 2 * HEADS, HD])
                    v = qk[:, i, :].rearrange("p (h d) -> p h d", d=HD)
                    nc.vector.tensor_tensor(v, v, r, ALU.mult).then_inc(done[kind], 1)
                elif kind in ("q", "k"):
                    if not multi(a):
                        continue
                    l = layer(a)
                    col = (C_Q if kind == "q" else C_K) + i
                    hi, lo = (qh, ql) if kind == "q" else (kh, kl)
                    dve.wait_ge(hi_ready, (nth(kind, a, i) - nth(kind, BATCH, 0)) * 2 + 1 + (kind == "k"))
                    if l == 1:
                        nc.vector.tensor_tensor(lo[:, i, :], bank(kind, a, i)[:, :], hi[:, i, :].bitcast(F32),
                                                ALU.subtract).then_inc(done[kind], 1)
                    else:
                        nc.vector.scalar_tensor_tensor(out=lo[:, i, :], in0=bank(kind, a, i)[:, :],
                                                       scalar=colv[:, l, col:col + 1], in1=hi[:, i, :].bitcast(F32),
                                                       op0=ALU.add, op1=ALU.subtract).then_inc(done[kind], 1)
                elif kind == "max":
                    n, c = i % 4, i // 4
                    col = ((n % 2) * 2 + n // 2) * TT + c
                    dve.wait_ge(pe_ring, use(kind, a, i))
                    if i == 0 and a - 2 >= UNITS * BATCH:
                        dve.wait_ge(pe_ring, use("shift", a - 2))
                    nc.vector.tensor_reduce(m16[:, a % 2, col:col + 1], bank(kind, a, i)[:, :], AX_X, ALU.max,
                                            negate=True).then_inc(done["max"], 1)
                elif kind == "shift":
                    dve.wait_ge(pe_ring, use(kind, a))
                    if a - 2 >= UNITS * BATCH:
                        dve.wait_ge(shifted[a % 2], SHIFT_IN(a - 2))
                    nc.vector.tensor_copy(cT[:, a % 2, :], bank(kind, a)[0:16, 0:P]).then_inc(done["shift"], 1)
                elif kind == "scores0":
                    t = nth(kind, a, i) - 1
                    dve.wait_ge(pe_s0, t + 1)
                    if t >= TT:
                        dve.wait_ge(exp0, t + 1 - TT)
                    link(nc.vector.tensor_reduce(nm0[:, i:i + 1], ST[t % SBANKS][:, :], AX_X, ALU.max, negate=True))
                    nc.vector.tensor_scalar(nb0[:, i:i + 1], nm0[:, i:i + 1], SCALE[0], None, ALU.mult
                                            ).then_inc(nb_ready, 1)
                elif kind == "soft0":
                    dve.wait_ge(exp0, nth(kind, a, i))
                    link(nc.vector.reciprocal(rc0[:, i:i + 1], sum0[:, i:i + 1]))
                    nc.vector.tensor_scalar(probs[:, i, :], probs[:, i, :], rc0[:, i:i + 1], None,
                                            ALU.mult).then_inc(done["soft0"], 1)
                elif kind == "oT1":
                    dve.wait_ge(pe_ring, use(kind, a, i))
                    if i == 0 and layer(a - 1) < LAYERS - 1:
                        dve.wait_ge(pe_ring, use("hT2", a - 1, CH - 1))
                    elif i == 0:
                        dve.wait_ge(out_sem, 16 * nth("final", a - 1, TT - 1))
                    b = bank(kind, a, i)[:, :].rearrange("p (h e) -> p h e", e=32)
                    link(nc.vector.reciprocal(rcp[:, i % 2, :], b[:, :, HD]))
                    nc.vector.tensor_tensor(tok2[:, i, :].rearrange("p (h d) -> p h d", d=HD), b[:, :, 0:HD],
                                            rcp[:, i % 2, :].unsqueeze(2).to_broadcast([P, HEADS, HD]), ALU.mult
                                            ).then_inc(done[kind], 1)
                elif kind in ("proj", "fc2"):
                    l = layer(a)
                    dve.wait_ge(pe_ring, use(kind, a, i))
                    if kind == "fc2":
                        dve.wait_ge(done["proj"], nth("proj", a, i // 2))
                    elif a > 0 and layer(a - 1) < LAYERS - 1:
                        dve.wait_ge(done["fc2"], nth("fc2", a - 1, 2 * i + 1))
                    elif a > 0:
                        dve.wait_ge(done["proj"], nth("proj", a - 1, i))
                    off = (R_PB if kind == "proj" else R_FB) + DIM * l
                    if kind == "proj":
                        nc.vector.tensor_tensor(tmp[:, 2 * i:2 * i + 2, :],
                                                bank(kind, a, i)[:, :].rearrange("p (t d) -> p t d", t=2),
                                                rowv[:, off:off + DIM].unsqueeze(1).to_broadcast([P, 2, DIM]), ALU.add
                                                ).then_inc(y1, 1)
                    else:
                        nc.vector.tensor_tensor(tmp[:, i, :], bank(kind, a, i)[:, 0:DIM], rowv[:, off:off + DIM],
                                                ALU.add).then_inc(y2, 1)

        @block.gpsimd
        def _(pool):
            n_seq = [0]

            def link(ins):
                n_seq[0] += 1
                ins.then_inc(pool_seq, 1)
                pool.wait_ge(pool_seq, n_seq[0])

            link(nc.gpsimd.memset(ident[:, :], 0.0))
            pool.wait_ge(dve_seq, 1)
            nc.gpsimd.affine_select(out=ident[:, :], in_=ident[:, :], compare_op=ALU.not_equal, fill=1.0, base=0,
                                    pattern=[[-1, P]], channel_multiplier=1).then_inc(const_ready, 1)
            for kind, a, i in PLAN:
                if kind in ("stat1", "stat2"):
                    w, l = int(kind == "stat2"), layer(a)
                    pool.wait_ge(done[kind], nth(kind, a))
                    src = var[:, w, :] if l == 0 else mv[:, w, :, 1]
                    if a > 0:
                        pool.wait_ge(done["norm2" if w else "norm1"], nth("norm2" if w else "norm1", a - 1))
                    link(nc.gpsimd.tensor_scalar(rstd[:, w, :], src, EPS[l], None, ALU.add))
                    nc.gpsimd.tensor_tensor(rstd[:, w, :], rstd[:, w, :], mhalf[:, 0:TT], ALU.pow
                                            ).then_inc(rstd2 if w else rstd1, 1)
                elif kind == "qkss":
                    pool.wait_ge(ss_ready, nth(kind, a, i))
                    pool.wait_ge(done["headscale"], 1)
                    if a > BATCH:
                        pool.wait_ge(done["qknorm"], nth("qknorm", a - 1, i))
                    link(nc.gpsimd.tensor_scalar(ss[:, i, :], ss[:, i, :], 1e-24, None, ALU.max))
                    link(nc.gpsimd.tensor_tensor(rs[:, i, :], ss[:, i, :], mhalf[:, :], ALU.pow))
                    nc.gpsimd.tensor_tensor(rs[:, i, 0:HEADS], rs[:, i, 0:HEADS], smrow[:, :], ALU.mult
                                            ).then_inc(done[kind], 1)
                elif kind in ("proj", "fc2"):
                    l, b = layer(a), batch(a)
                    n, t = (2, 2 * i) if kind == "proj" else (1, i)
                    pool.wait_ge(y1 if kind == "proj" else y2, nth(kind, a, i))
                    y = tmp[:, t:t + n, :]
                    if l in (1, 2):
                        pool.wait_ge(done["gate"], nth("gate", a))
                        off = 0 if kind == "proj" else DIM
                        g = gates[:, a % 2, off:off + DIM].unsqueeze(1).to_broadcast([P, n, DIM])
                        link(nc.gpsimd.tensor_tensor(y, y, g, ALU.mult))
                    xs = X[:, TT * b + t:TT * b + t + n, :]
                    if kind == "proj":
                        pool.wait_ge(done["norm1"], nth("norm1", a))
                    else:
                        pool.wait_ge(done["norm2"], nth("norm2", a))
                    nc.gpsimd.tensor_tensor(xs, xs, y, ALU.add).then_inc(done[kind], 1)
                    if l == LAYERS - 1 and i == 0:
                        pool.wait_ge(done["gate"], nth("gate", a))
                        gm, bt = gates[:, a % 2, 0:DIM], gates[:, a % 2, DIM:2 * DIM]
                        link(nc.gpsimd.tensor_tensor(sq[:, 0:DIM], gm, rowv[:, R_LB:R_LB + DIM], ALU.mult))
                        nc.gpsimd.tensor_tensor(gm, gm, rowv[:, R_LG:R_LG + DIM], ALU.mult)
                        link(nc.gpsimd.tensor_tensor(bt, bt, sq[:, 0:DIM], ALU.add))
                elif kind == "final":
                    l, b = layer(a), batch(a)
                    pool.wait_ge(done["norm2"], nth("norm2", a))
                    t = tok2[:, i, :]
                    link(nc.gpsimd.tensor_tensor(t, t, gates[:, a % 2, 0:DIM], ALU.mult))
                    link(nc.gpsimd.tensor_tensor(t, t, gates[:, a % 2, DIM:2 * DIM], ALU.add))
                    nc.gpsimd.tensor_tensor(t, t, X[:, TT * b + i, :], ALU.add).then_inc(done["final"], 1)


LOG100 = 4.605170185988092


def kernel(**inputs):
    import numpy as np
    import concourse.bacc as bacc
    from concourse.bass_utils import run_bass_kernel_spmd

    g = {k: np.asarray(v) for k, v in inputs.items()}
    one, zero = np.ones(DIM, np.float32), np.zeros(DIM, np.float32)

    def regroup(w):
        return w.reshape(HEADS, HD, 3, -1).transpose(2, 0, 1, 3).reshape(3 * DIM, -1)

    def parts(w, order):
        return np.concatenate([w[..., DIM * n:DIM * (n + 1)] for n in order], axis=-1)

    def by_unit(w, blocks):
        out = [w[..., DIM * n:DIM * (n + 1)] for n in range(w.shape[-1] // DIM)]
        for n in range(blocks):
            v = out[n].reshape(-1, UNITS, 2, 2, HD).transpose(0, 2, 1, 3, 4)
            out[n] = v.reshape(w.shape[:-1] + (DIM,))
        return np.concatenate(out, axis=-1)

    wqkv = np.stack([
        np.concatenate([g["L0_cond_q_w"], g["L0_cond_k_w"], g["L0_cond_v_w"]], axis=1),
        by_unit(g["L1_cond_mat_qkv_w"].T, 2), by_unit(g["L2_cond_Wqkv"], 2), by_unit(regroup(g["L3_cond_Wqkv"]).T, 2)])
    wp = np.stack([g["L0_cond_proj_w"], g["L1_cond_proj_w"].T, g["L2_cond_Wproj"], g["L3_cond_Wp"].T])
    w1 = np.stack([g["L0_cond_mlp_w1"], g["L1_cond_fc1_w"].T, g["L2_cond_W1"]])
    w2 = np.stack([g["L0_cond_mlp_w2"], g["L1_cond_fc2_w"].T, g["L2_cond_W2"]])
    ada1, adab1 = g["L1_cond_ada_w"].T, g["L1_cond_ada_b"]
    ada2, adab2 = g["L2_cond_Wt"], g["L2_cond_bt"]
    film3 = np.concatenate([g["L3_cond_Wg"].T, g["L3_cond_Wb"].T], axis=1)
    filmb3 = np.concatenate([g["L3_cond_bg"], g["L3_cond_bb"]])
    film0 = np.concatenate([g["L0_cond_film1_w"], g["L0_cond_film2_w"]], axis=1)
    filmb0 = np.concatenate([g["L0_cond_film1_b"], g["L0_cond_film2_b"]])
    wmod = np.stack([film0, parts(ada1, (2, 4, 3, 5)), parts(ada2, (1, 0, 4, 3)),
                     np.concatenate([film3, film3], axis=1)])
    modbias = [filmb0, parts(adab1, (2, 4, 3, 5)), parts(adab2, (1, 0, 4, 3)), np.concatenate([filmb3, filmb3])]
    wgate = np.stack([parts(ada1, (0, 1)), parts(ada2, (2, 5)), film3])
    gatebias = [parts(adab1, (0, 1)), parts(adab2, (2, 5)), filmb3]
    b3 = regroup(g["L3_cond_bqkv"])[:, 0]
    bqkv = [np.concatenate([g["L0_cond_q_b"], g["L0_cond_k_b"], g["L0_cond_v_b"]]),
            np.concatenate([g["L1_cond_q_bias"], zero, g["L1_cond_v_bias"]]), by_unit(g["L2_cond_bqkv"], 2), by_unit(b3, 2)]
    b1 = [g["L0_cond_mlp_b1"], g["L1_cond_fc1_b"], g["L2_cond_b1"], np.zeros(HID, np.float32)]
    ga = [(g["L0_cond_norm1_w"], g["L0_cond_norm2_w"], zero, zero), (one, one, zero, zero),
          (g["L2_cond_g1"], g["L2_cond_g2"], g["L2_cond_be1"], g["L2_cond_be2"]),
          (g["L3_cond_ln_g"], g["L3_cond_ln_g"], g["L3_cond_ln_b"], g["L3_cond_ln_b"])]
    cols = np.stack([np.concatenate([bqkv[l], b1[l], modbias[l], *ga[l]]).reshape(N_COL, P).T
                     for l in range(LAYERS)], axis=1)
    rows = np.concatenate([
        g["L0_cond_proj_b"], g["L1_cond_proj_b"], g["L2_cond_bproj"], g["L3_cond_bp"],
        g["L0_cond_mlp_b2"], g["L1_cond_fc2_b"], g["L2_cond_b2"], *gatebias,
        by_unit(g["L1_cond_q_bias"], 1), zero,
        g["L1_cond_scale_mul"].reshape(UNITS, 2, 2).transpose(1, 0, 2).reshape(-1), g["L3_cond_ln_g"], g["L3_cond_ln_b"]])
    host = {"x": g["x"], "cond": g["cond_1024"].T, "cols": cols, "rows": rows, "wqkv": wqkv, "wp": wp,
            "w1": w1, "w2": w2, "wmod": wmod, "wgate": wgate}

    nc = bacc.Bacc("TRN2", target_bir_lowering=False, num_devices=1, dynamic_dma_scratch_size=4096)
    arrays, args = {}, []
    for name, a in host.items():
        a = np.ascontiguousarray(a)
        arrays[f"in_{name}"] = a
        args.append(nc.dram_tensor(f"in_{name}", a.shape, mybir.dt.from_np(a.dtype), kind="ExternalInput").ap())
    out = nc.dram_tensor("out", (BATCH, TOK, DIM), F32, kind="ExternalOutput").ap()
    cond_blocks_kernel(nc, *args, out)
    r = run_bass_kernel_spmd(nc, [arrays], core_ids=[0])
    return r.results[0]["out"]
```

```python
from contextlib import ExitStack

import concourse.bass as bass
from concourse import mybir

F32 = mybir.dt.float32
F32R = mybir.dt.float32r
ALU = mybir.AluOpType
ACT = mybir.ActivationFunctionType
AX_X = mybir.AxisListType.X

LAYERS, BATCH, TOK, DIM, HID = 4, 4, 512, 256, 1024
HEADS, HD = 16, 16
P = 128
CH = DIM // P
TT = TOK // P
MT = HID // P
UNITS = HEADS // 4
JOBS = LAYERS * BATCH
TICKS = UNITS * TT
STAT, NORM = 6, 8
LEAD = 6
RING = 4
SBANKS = 3
PROBS = 8
BLK = 64
KS = 3 * HD
EPS = (1e-6, 1e-6, 1e-5, 1e-5)
SCALE = (DIM ** -0.5, 1.0, HD ** -0.5, 1.0)
C_Q, C_K, C_V, C_B1, C_MB, C_G, C_BE, N_COL = 0, 2, 4, 6, 14, 22, 26, 30
R_PB, R_FB, R_LB, POST_ROWS = 0, DIM, 2 * DIM, 3 * DIM
GATE_ROWS = 2 * DIM
LAYER_ROWS = POST_ROWS + GATE_ROWS
R_QK, R_SM, HEAD_ROWS = 0, 2 * DIM, 2 * DIM + HEADS


def layer(j):
    return j // BATCH


def batch(j):
    return j % BATCH


def multi(j):
    return layer(j) > 0


def prep(j):
    at = {t: [] for t in range(TICKS)}
    if j >= JOBS:
        return at
    at[0] += [("hT1", j, c) for c in range(CH)]
    if layer(j) == 1:
        at[2] += [("qktok", j, 0), ("qktok", j, 1)]
        at[3] += [("qkss", j, 0), ("qktok", j, 2), ("qkss", j, 1)]
        at[4] += [("qktok", j, 3), ("qkss", j, 2)]
        at[5] += [("qkss", j, 3), ("qkroot", j, 0), ("v", j, 0)]
        at[6] += [("qkrs", j, 0), ("qknorm", j, 0), ("qknorm", j, 1), ("v", j, 1)]
        at[6] += [("qknorm", j, 2), ("qknorm", j, 3)]
        at[7] += [(x, j, i) for i in range(2) for x in "qk"] + [("stack", UNITS * j, 0)]
    else:
        at[2] += [("q", j, 0)]
        at[3] += [("k", j, 0)]
        at[4] += [("q", j, 1)]
        at[5] += [("k", j, 1)]
        at[6] += [("v", j, 0), ("stack", UNITS * j, 0)]
        at[7] += [("v", j, 1)]
    at[9] += [("stack", UNITS * j + 1, 0)]
    at[12] += [("stack", UNITS * j + 2, 0)]
    return at


def post(j):
    at = {t: [] for t in range(TICKS)}
    if multi(j):
        at[1] += [("oT1", j, c) for c in range(TT)]
        at[2] += [("oT2", j, c) for c in range(CH)]
        at[3] += [("proj", j, 0)]
        at[4] += [("proj", j, 1)]
        at[5] += [("stat2", j, 0)]
        at[6] += [("norm2", j, 0)]
    if layer(j) < LAYERS - 1:
        at[7] += [("hT2", j, c) for c in range(CH)]
        for m, t in enumerate((8, 8, 9, 9, 10, 10, 11, 11)):
            at[t] += [("fc1", j, m)]
        at[10] += [("gelu", j, 0)]
        at[12] += [("gelu", j, 1)]
        for t in range(TT):
            at[12 + t] += [("fc2", j, t)]
    else:
        for t in range(TT):
            at[7 + t] += [("final", j, t)]
            at[10 + t] += [("store", j, t)]
    return at


def spread(main, rest):
    out, n = [], 0
    for i, step in enumerate(main):
        out.append(step)
        upto = len(rest) * (i + 1) // len(main)
        out += rest[n:upto]
        n = upto
    return out + rest[n:]


def single_window(w):
    j, n = w - 1, w + 1
    hT2, fc1, fc2 = [], [], []
    if j >= 0:
        hT2 = [("hT2", j, c) for c in range(CH)]
        fc1 = [("fc1", j, m) for m in range(MT)]
        fc2 = [("fc2", j, t) for t in range(TT)]
    else:
        fc1 = [("v", 0, 0), ("v", 0, 1), ("modrow", 0, 1), ("mod", 0, 1)]
    steps = hT2[:1] + [("scores0", w, 0)] + hT2[1:] + [("scores0", w, 1)] + fc1[:1]
    steps += [("soft0", w, 0), ("scores0", w, 2)] + fc1[1:2] + [("soft0", w, 1), ("scores0", w, 3)] + fc1[2:3]
    steps += [("soft0", w, 2)] + [("hT1", n, c) for c in range(CH)] + fc1[3:4] + [("soft0", w, 3)]
    if j >= 0:
        steps.append(("gelu", j, 0))
    pT = [("pT0", w, t) for t in range(TT)]
    av = [("av0", w, 0), ("av0", w, 1)]
    proj = [("proj", w, 0), ("proj", w, 1)]
    steps += spread(pT, fc1[4:])
    if j >= 0:
        steps.append(("gelu", j, 1))
    else:
        steps += [("split_wp", 0, 0)] + [("split_w1", 0, i) for i in range(4)]
    stats = [("stat2", w, 0)]
    norms = [("norm2", w, 0)]
    if n + 1 <= BATCH + 1:
        stats += [("stat1", n + 1, 0)]
        norms += [("norm1", n + 1, 0)]
    if layer(n) == 0:
        if j < 0:
            steps += av + [("q", n, 0), ("k", n, 0)] + proj + stats + [("q", n, 1), ("k", n, 1)]
            return steps + [("v", n, 0)] + norms + [("v", n, 1)]
        steps += [("q", n, 0), ("k", n, 0)] + av + [("q", n, 1), ("k", n, 1)] + proj[:1] + [("v", n, 0)] + proj[1:]
        return steps + fc2[:1] + stats + [("v", n, 1)] + fc2[1:3] + norms + fc2[3:]
    u = UNITS * n
    split = [("split_qkv", 1, i) for i in range(3)]
    load = [("load_qkv", 1, i) for i in range(3)]
    i = steps.index(("soft0", w, 1))
    steps[i:i] = [split[0], load[1]]
    i = steps.index(("pT0", w, 0))
    steps[i:i] = [split[1], load[2]]
    steps += [split[2], ("vones", n, 0)] + av + [("qktok", n, 0), ("qktok", n, 1)] + proj
    steps += [("qkss", n, 0), ("qktok", n, 2), ("qkss", n, 1), ("qktok", n, 3), ("qkss", n, 2), ("qkss", n, 3)]
    steps += [("qkroot", n, 0), ("v", n, 0)] + stats + [("qkrs", n, 0), ("v", n, 1)] + fc2[:1]
    steps += [("qknorm", n, t) for t in range(TT)] + norms + [(x, n, i) for i in range(2) for x in "qk"]
    steps += [("stack", u, 0), ("stack", u + 1, 0), ("stack", u + 2, 0)] + fc2[1:]
    steps += [("max", u, i) for i in range(16)]
    steps += [("max", u + 1, i) for i in range(4)] + [("shift", u, 0)] + [("max", u + 1, i) for i in range(4, 8)]
    return steps


def multi_window(w):
    before, after = post(w - 1), prep(w + 1)
    plan, last = [], layer(w) == LAYERS - 1
    for t in range(TICKS):
        g, c = divmod(t, TT)
        rest = after[t] + before[t] if t in (2, 3) else before[t] + after[t]
        if w + 2 < JOBS and t in (STAT, NORM):
            rest.append(("stat1" if t == STAT else "norm1", w + 2, 0))
        if t == 0:
            rest = [("stack", UNITS * w + 3, 0)] + rest
        if t == 3 and w == BATCH:
            rest = [("vones", w + 1, 0)] + rest
        if t == 12:
            rest = [("gate", w, 0)] + rest
        n = layer(w) + 1
        if not last:
            i = batch(w) - 1
            if i in range(mod_rows(n)) and t in (13, 14):
                rest.append(("modrow" if t == 13 else "mod", n, i))
            if batch(w) == 2 and t in (10, 12, 14):
                rest.append(("split_qkv", n, (t - 10) // 2))
        if batch(w) == 1:
            if t == 1:
                rest.append(("split_wp", layer(w), 0))
            if t in (3, 5, 7, 9) and not last:
                rest.append(("split_w1", layer(w), (t - 3) // 2))
        v = t + LEAD
        u = UNITS * w + v // TT
        maxima = [("max", u, 4 * (v % TT) + n) for n in range(4)] if u < UNITS * JOBS else []
        shift = []
        if v % TT == 0 and UNITS * w + v // TT - 1 < UNITS * JOBS:
            if last:
                shift = [("shift", u - 1, 0)]
            else:
                rest = rest[:len(rest) // 2] + [("shift", u - 1, 0)] + rest[len(rest) // 2:]
        s = [("scores", UNITS * w + g, 4 * c + n) for n in range(4)]
        if t > 0:
            av = [("av", UNITS * w + (t - 1) // TT, (t - 1) % TT)]
        else:
            av = [("av", UNITS * w - 1, TT - 1)] if w > BATCH else []
        m = maxima
        if any(step[0] == "gelu" for step in rest):
            n = rest.index(next(step for step in rest if step[0] == "gelu")) + 1
            plan += s[:2] + m[:1] + shift + s[2:] + m[1:2] + rest[:n] + m[2:3] + av + m[3:] + rest[n:]
        else:
            plan += spread(m[:1] + s[:2] + shift + m[1:2] + av + m[2:3] + s[2:] + m[3:], rest)
        if t in (8, 10, 12) and batch(w) == 2 and not last:
            plan.append(("load_qkv", layer(w) + 1, (t - 8) // 2))
        if t == 15 and batch(w) == 0:
            plan.append(("load_wp", layer(w), 0))
            if not last:
                plan.append(("load_w2", layer(w), 0))
        if t in (1, 3, 5, 7) and batch(w) == 1 and not last:
            plan.append(("load_w1", layer(w), t // 2))
        if t == 15 and batch(w) == 1 and not last and mod_rows(layer(w) + 1) > 1:
            plan.append(("load_mod", layer(w) + 1, 1))
        if t == 15 and batch(w) == 2 and layer(w) < LAYERS - 2:
            plan.append(("load_mod", layer(w) + 2, 0))
        if t == 15 and batch(w) == 3 and not last:
            plan.append(("load_gate", layer(w) + 1, 0))
    return plan


def mod_rows(l):
    return 2 if l < LAYERS - 1 else 1


def plan_steps():
    plan = [("load_mod", 0, 0)] + [("load_qkv", 0, n) for n in range(3)] + [("load_mod", 0, 1), ("load_wp", 0, 0)]
    plan += [("load_w1", 0, n) for n in range(4)] + [("load_w2", 0, 0), ("stat1", 0, 0), ("norm1", 0, 0)]
    plan += [("modrow", 0, 0), ("mod", 0, 0)] + [("split_qkv", 0, n) for n in range(3)]
    plan += [s for t in range(TICKS) for s in prep(0)[t] if s[0] not in ("stack", "v")]
    plan += [("load_mod", 1, 0), ("stat1", 1, 0), ("norm1", 1, 0)]
    for w in range(BATCH):
        steps = single_window(w)
        if w == 0:
            i = steps.index(("mod", 0, 1))
            steps[i:i] = [("headscale", 1, 0), ("load_gate", 1, 0)]
        if w in (1, 2):
            steps = [("modrow", 1, w - 1)] + steps + [("mod", 1, w - 1), ("load_mod", w, 2 - w)]
        plan += steps
        if w == 2:
            plan.append(("load_qkv", 1, 0))
    for w in range(BATCH, JOBS):
        plan += multi_window(w)
    plan.append(("av", UNITS * JOBS - 1, TT - 1))
    for steps in post(JOBS - 1).values():
        plan += steps
    return plan


PLAN = plan_steps()
RINGED = ("hT1", "v", "qktok", "q", "k", "max", "shift", "oT1", "oT2", "proj", "hT2", "fc1",
          "fc2", "gate", "modrow", "mod", "pT0", "av0")
NTH, USE, USES = {}, {}, []
_count = {}
for _s in PLAN:
    _count[_s[0]] = _count.get(_s[0], 0) + 1
    NTH[_s] = _count[_s[0]]
    if _s[0] in RINGED:
        USE[_s] = len(USES)
        USES.append(_s)

TMP_BEFORE, _last = {}, {}
for _s in PLAN:
    if _s[0] in ("proj", "fc2"):
        _tiles = (2 * _s[2], 2 * _s[2] + 1) if _s[0] == "proj" else (_s[2],)
        TMP_BEFORE[_s] = sorted({_last[t] for t in _tiles if t in _last})
        _last.update({t: _s for t in _tiles})
PIECES = [s for s in PLAN if s[0].startswith("split")]
CUTS = [s for s in PLAN if s[0] in ("hT1", "hT2", "oT2", "av0")]


def nth(kind, a, i=0):
    return NTH[(kind, a, i)]


def use(kind, a, i=0):
    return USE[(kind, a, i)] + 1


def cond_blocks_kernel(nc, x, cond, cols, rows, wqkv, wp, w1, w2, wmod, wgate, out):
    x_v = x.rearrange("b (t p) d -> p b t d", p=P)
    out_v = out.rearrange("b (t p) d -> p b t d", p=P)

    with ExitStack() as ctx:
        def sb(name, shape, dt=F32):
            return ctx.enter_context(nc.sbuf_tensor(name, shape, dt))

        def sem(name):
            return ctx.enter_context(nc.semaphore(name))

        X = sb("X", [P, BATCH * TT, DIM])
        ident = sb("ident", [P, P])
        colv = sb("colv", [P, LAYERS, N_COL])
        rowp = sb("rowp", [P, POST_ROWS])
        rowg = sb("rowg", [P, GATE_ROWS])
        rowh = sb("rowh", [P, HEAD_ROWS])
        condT = sb("condT", [P, CH, BATCH])
        condS = sb("condS", [P, CH, BATCH])
        condE = sb("condE", [P, CH, BATCH])
        condR = sb("condR", [P, CH, BATCH])
        smrow = sb("smrow", [P, HEADS])
        wqkv_h = sb("wqkv_h", [P, CH, 3 * DIM], F32R)
        wqkv_l = sb("wqkv_l", [P, CH, 3 * DIM], F32R)
        wp_h = sb("wp_h", [P, CH, DIM], F32R)
        wp_l = sb("wp_l", [P, CH, DIM], F32R)
        w1_h = sb("w1_h", [P, CH, HID], F32R)
        w1_l = sb("w1_l", [P, CH, HID], F32R)
        w2_s = sb("w2_s", [P, MT, DIM])
        wmod_s = sb("wmod_s", [P, CH, 2 * DIM])
        wgate_s = sb("wgate_s", [P, CH, 2 * DIM])
        modr = sb("modr", [P, 4, BATCH])
        mods = sb("mods", [P, 2, 4, BATCH])
        modb = sb("modb", [P, 2, 4, BATCH])
        raw = sb("raw", [P, CH, DIM])
        gates = sb("gates", [P, 2, 2 * DIM])
        tok1 = sb("tok1", [P, TT, DIM])
        tok2 = sb("tok2", [P, TT, DIM])
        hT_h = sb("hT_h", [P, CH, TOK], F32R)
        hT_l = sb("hT_l", [P, CH, TOK], F32R)
        full = sb("full", [P, 2, TOK])
        postT_h = sb("postT_h", [P, CH, TOK], F32R)
        postT_l = sb("postT_l", [P, CH, TOK], F32R)
        qk = sb("qk", [P, 4, TOK])
        sq = sb("sq", [P, TOK])
        mrow = sq[0:BATCH, :]
        qh = sb("qh", [P, 2, TOK], F32R)
        ql = sb("ql", [P, 2, TOK], F32R)
        kh = sb("kh", [P, 2, TOK], F32R)
        kl = sb("kl", [P, 2, TOK], F32R)
        SQ = [sb(f"SQ{i}", [P, 2, TOK], F32R) for i in range(4)]
        SK = [sb(f"SK{i}", [P, 2, TOK], F32R) for i in range(4)]
        VW = HEADS * (HD + 1)
        V = [sb(f"V{i}", [P, TT, VW + 16]) for i in range(2)]
        probs = sb("probs", [P, PROBS, TOK])
        oU = sb("oU", [P, UNITS, TOK])
        gT = sb("gT", [P, MT, TOK])
        tmp = sb("tmp", [P, TT, DIM])
        m16 = sb("m16", [P, 2, 16])
        cT = sb("cT", [48, P], F32R)
        stats = sb("stats", [P, 2, TT, 6])
        mv = sb("mv", [P, 2, TT, 2])
        var = sb("var", [P, 2, TT])
        rstd = sb("rstd", [P, 2, TT])
        mhalf = sb("mhalf", [P, TT])
        ss = sb("ss", [P, TT, 2 * HEADS])
        rs = sb("rs", [P, TT, 2 * HEADS])
        rcp = sb("rcp", [P, 2, HEADS])
        nm0 = sb("nm0", [P, TT])
        nb0 = sb("nb0", [P, TT])
        sum0 = sb("sum0", [P, TT])
        rc0 = sb("rc0", [P, TT])

        ST = [ctx.enter_context(nc.psum_tensor(f"ST{i}", [P, TOK], F32)) for i in range(SBANKS)]
        AVB = ctx.enter_context(nc.psum_tensor("AVB", [P, TOK], F32))
        ring = [ctx.enter_context(nc.psum_tensor(f"ring{i}", [P, TOK], F32)) for i in range(RING)]

        def bank(kind, a, i=0):
            return ring[USE[(kind, a, i)] % RING]

        kinds = sorted({s[0] for s in PLAN if not s[0].startswith("load") and s[0] not in ("stack", "store")})
        done = {k: sem("done_" + k) for k in kinds}
        pe_ring = sem("pe_ring")
        pe_scores = sem("pe_scores")
        pe_av = sem("pe_av")
        pe_s0 = sem("pe_s0")
        unit_out = sem("unit_out")
        hi_ready = sem("hi_ready")
        sq_ready = sem("sq_ready")
        hi_in = {k: sem("hi_" + k) for k in ("hT1", "hT2", "oT2", "av0")}
        w_hi = sem("w_hi")
        rstd1, rstd2 = sem("rstd1"), sem("rstd2")
        ss_ready = sem("ss_ready")
        nb_ready = sem("nb_ready")
        exp0 = sem("exp0")
        y1, y2 = sem("y1"), sem("y2")
        stacked = [sem(f"stacked{i}") for i in range(4)]
        shifted = [sem(f"shifted{i}") for i in range(2)]
        x_in = [sem(f"x_in{b}") for b in range(BATCH)]
        cond_in, cols_in, rows_in = sem("cond_in"), sem("cols_in"), sem("rows_in")
        raw_in, in_w2 = sem("raw_in"), sem("in_w2")
        in_mod = [sem(f"in_mod{i}") for i in range(2)]
        in_gate, in_rowp, in_rowg = sem("in_gate"), sem("in_rowp"), sem("in_rowg")
        out_sem = sem("out_sem")
        dve_seq, pool_seq = sem("dve_seq"), sem("pool_seq")
        const_ready = sem("const_ready")
        cond_ready = sem("cond_ready")
        e_ready = sem("e_ready")
        clip_ready = sem("clip_ready")
        gates_ready = sem("gates_ready")
        final_dve = sem("final_dve")

        first_in = [sem(f"first_in{n}") for n in range(sum(s[1] == 0 for s in PIECES))]

        def STACK_IN(u):
            return 16 * 12 * ((u - UNITS * BATCH) // 4 + 1)

        def SHIFT_IN(u):
            return 16 * 2 * ((u - UNITS * BATCH) // 2 + 1)

        def slot_free(eng, u):
            if u - 4 >= UNITS * BATCH:
                eng.wait_ge(pe_scores, nth("scores", u - 4, 4 * TT - 1))

        def unit_job(u):
            return u // UNITS

        def wcond(l):
            return condS if l in (1, 2) else condT

        parts_of = {"split_qkv": (wqkv_h, wqkv_l), "split_wp": (wp_h, wp_l), "split_w1": (w1_h, w1_l)}

        def piece(kind, a, i):
            if a == 0:
                return gT[:, PIECES.index((kind, a, i)), :].rearrange("p (c n) -> p c n", c=CH)
            return raw[:, :, :]

        def whole(act, kind, a, i):
            n = CUTS.index((kind, a, i))
            if n >= 2:
                act.wait_ge(done[CUTS[n - 2][0]], nth(*CUTS[n - 2]))
            return full[:, n % 2, :]

        block = ctx.enter_context(nc.Block())

        @block.sync
        def _(sp):
            sp.dma_start(condT[:, :, :], cond.rearrange("(c p) b -> p c b", p=P)).then_inc(cond_in, 16)
            sp.dma_start(colv[:, :, :], cols).then_inc(cols_in, 16)
            sp.dma_start(X[:, 0:TT, :], x_v[:, 0]).then_inc(x_in[0], 16)
            for kind, a, i in PLAN:
                if kind in ("load_qkv", "load_wp", "load_w1"):
                    step = ("split" + kind[4:], a, i)
                    n = PIECES.index(step)
                    if a > 0:
                        sp.wait_ge(done[PIECES[n - 1][0]], nth(*PIECES[n - 1]))
                    src = {"load_qkv": wqkv, "load_wp": wp, "load_w1": w1}[kind][a, :, DIM * i:DIM * (i + 1)]
                    got = raw_in if a > 0 else first_in[n]
                    sp.dma_start(piece(*step), src.rearrange("(c p) n -> p c n", p=P)).then_inc(got, 16)
                    if kind == "load_wp":
                        if a > 0:
                            sp.wait_ge(y2, nth("fc2", a * BATCH - 1, TT - 1))
                        r = a * LAYER_ROWS
                        sp.dma_start(rowp[:, :], rows[r:r + POST_ROWS].partition_broadcast(P)).then_inc(in_rowp, 16)
                    if (kind, a, i) == ("load_qkv", 0, 2):
                        sp.dma_start(X[:, TT:2 * TT, :], x_v[:, 1]).then_inc(x_in[1], 16)
                    if (kind, a, i) == ("load_w1", 0, 3):
                        for b in range(2, BATCH):
                            sp.dma_start(X[:, b * TT:(b + 1) * TT, :], x_v[:, b]).then_inc(x_in[b], 16)
                        sp.dma_start(rowh[:, :], rows[LAYERS * LAYER_ROWS:].partition_broadcast(P)).then_inc(rows_in, 16)
                elif kind == "load_w2":
                    if a > 0:
                        sp.wait_ge(pe_ring, use("fc2", a * BATCH - 1, TT - 1))
                    sp.dma_start(w2_s[:, :, :], w2[a].rearrange("(m p) n -> p m n", p=P)).then_inc(in_w2, 16)
                elif kind == "load_mod":
                    if a > 0 and i == 0:
                        sp.wait_ge(pe_ring, use("modrow", a - 1, mod_rows(a - 1) - 1 if a > 1 else 0))
                    elif a > 0:
                        sp.wait_ge(pe_ring, use("modrow", a, 0))
                    dst = wgate_s if (a, i) == (0, 1) else wmod_s
                    src = wmod[a, :, 2 * DIM * i:2 * DIM * (i + 1)]
                    sp.dma_start(dst[:, :, :], src.rearrange("(c p) n -> p c n", p=P)).then_inc(in_mod[i], 16)
                elif kind == "load_gate":
                    if a > 1:
                        sp.wait_ge(pe_ring, use("gate", a * BATCH - 1))
                        sp.wait_ge(done["gate"], nth("gate", a * BATCH - 1))
                    else:
                        sp.wait_ge(pe_ring, use("modrow", 0, 1))
                    sp.dma_start(wgate_s[:, :, :], wgate[a - 1].rearrange("(c p) n -> p c n", p=P)).then_inc(in_gate, 16)
                    r = a * LAYER_ROWS + POST_ROWS
                    sp.dma_start(rowg[:, :], rows[r:r + GATE_ROWS].partition_broadcast(P)).then_inc(in_rowg, 16)
                elif kind == "stack":
                    j, g = divmod(a, UNITS)
                    sp.wait_ge(done["k"], nth("k", j, 1))
                    sp.wait_ge(done["q"], nth("q", j, 1))
                    slot_free(sp, a)
                    sp.wait_ge(const_ready, 1)
                    for stack, parts in ((SQ[a % 4], (qh, ql, qh)), (SK[a % 4], (kh, kh, kl))):
                        for r, part in enumerate(parts):
                            for par in range(2):
                                src = part[2 * HD * g + HD * par:2 * HD * g + HD * par + HD, :, :]
                                dst = stack[BLK * par + HD * r:BLK * par + HD * r + HD, :, :]
                                sp.dma_start(dst.bitcast(F32), src.bitcast(F32)).then_inc(stacked[a % 4], 16)
                elif kind == "shift":
                    sp.wait_ge(done["shift"], nth("shift", a))
                    for par in range(2):
                        d = SQ[a % 4][BLK * par + KS:BLK * par + KS + 1, :, :]
                        dst = bass.AP(d.tensor, d.offset, [[2 * TOK, 1], [P, 8], [1, P]]).bitcast(F32)
                        r = 32 * (a % 2) + 8 * par
                        s = cT[r:r + 8, :]
                        src = bass.AP(s.tensor, s.offset, [[P, 8], [P, 1], [1, P]]).bitcast(F32)
                        sp.dma_start(dst, s.bitcast(F32)).then_inc(shifted[a % 2], 16)
                elif kind == "store":
                    if a < JOBS - 1:
                        sp.wait_ge(done["final"], nth("final", a, i))
                    elif i % 2:
                        sp.wait_ge(final_dve, i // 2 + 1)
                    else:
                        sp.wait_ge(done["final"], nth("final", a, 0) + i // 2)
                    sp.dma_start(out_v[:, batch(a), i], tok2[:, i, :]).then_inc(out_sem, 16)
            sp.wait_ge(out_sem, 16 * BATCH * TT)

        @block.tensor
        def _(pe):
            def claim(kind, a, i):
                n = USE[(kind, a, i)]
                if n >= RING:
                    k, b, m = USES[n - RING]
                    pe.wait_ge({"proj": y1, "fc2": y2}.get(k, hi_in.get(k, done[k])), nth(k, b, m))
                return ring[n % RING]

            def product(out, stationary, moving, first, last):
                (sh, sl), (mh, ml) = stationary, moving
                pe.matmul(out, sh, mh, start=first, stop=False)
                pe.matmul(out, sh, ml, start=False, stop=False)
                return pe.matmul(out, sl, mh, start=False, stop=last)

            pe.wait_ge(const_ready, 1)
            for kind, a, i in PLAN:
                o = claim(kind, a, i) if kind in RINGED else None
                mm = None
                if kind in ("q", "k", "qktok", "v"):
                    pe.wait_ge(done["hT1"], nth("hT1", a, CH - 1))
                    part = {"q": 0, "k": 1, "qktok": 1, "v": 2}[kind]
                    pe.wait_ge(done["split_qkv"], nth("split_qkv", layer(a), part))
                if kind == "modrow":
                    pe.wait_ge(in_mod[i], 16 * (a + 1))
                    pe.wait_ge(cond_ready, 1)
                    src = wgate_s if (a, i) == (0, 1) else wmod_s
                    for c in range(CH):
                        mm = pe.matmul(o[0:BATCH, :], wcond(a)[:, c, :], src[:, c, :],
                                       start=(c == 0), stop=(c == CH - 1))
                elif kind == "mod":
                    pe.wait_ge(done["modrow"], nth("modrow", a, i))
                    for m in range(4):
                        mm = pe.transpose(o[:, BATCH * m:BATCH * (m + 1)], mrow[:, m * P:(m + 1) * P],
                                          ident[0:BATCH, 0:BATCH])
                elif kind == "gate":
                    pe.wait_ge(in_gate, 16 * layer(a))
                    pe.wait_ge(cond_ready, 1)
                    for c in range(CH):
                        mm = pe.matmul(o[:, :], wcond(layer(a))[:, c, batch(a):batch(a) + 1].to_broadcast([P, P]),
                                       wgate_s[:, c, :], start=(c == 0), stop=(c == CH - 1))
                elif kind in ("hT1", "hT2"):
                    src = tok1 if kind == "hT1" else tok2
                    norm = "norm1" if kind == "hT1" else "norm2"
                    pe.wait_ge(done[norm], nth(norm, a))
                    for t in range(TT):
                        mm = pe.transpose(o[:, t * P:(t + 1) * P], src[:, t, i * P:(i + 1) * P], ident[:, :])
                elif kind == "v":
                    for t in range(2):
                        for c in range(CH):
                            tok = (2 * i + t) * P
                            mm = product(o[:, t * DIM:(t + 1) * DIM], [h[:, c, tok:tok + P] for h in (hT_h, hT_l)],
                                         [w[:, c, 2 * DIM:3 * DIM] for w in (wqkv_h, wqkv_l)], c == 0, c == CH - 1)
                elif kind == "qktok":
                    for c in range(CH):
                        mm = product(o[:, :], [h[:, c, i * P:(i + 1) * P] for h in (hT_h, hT_l)],
                                     [w[:, c, 0:2 * DIM] for w in (wqkv_h, wqkv_l)], c == 0, c == CH - 1)
                elif kind in ("q", "k"):
                    off = DIM * (kind == "k") + i * P
                    if layer(a) == 1:
                        pe.wait_ge(done["qknorm"], nth("qknorm", a, TT - 1))
                        for t in range(TT):
                            mm = pe.transpose(o[:, t * P:(t + 1) * P], qk[:, t, off:off + P], ident[:, :])
                    else:
                        for c in range(CH):
                            mm = product(o[:, :], [w[:, c, off:off + P] for w in (wqkv_h, wqkv_l)],
                                         [h[:, c, :] for h in (hT_h, hT_l)], c == 0, c == CH - 1)
                elif kind == "max":
                    if i == 0:
                        pe.wait_ge(stacked[a % 4], STACK_IN(a))
                    n, c = i % 4, i // 4
                    r = BLK * (n % 2)
                    mm = pe.matmul(o[:, :], SQ[a % 4][r:r + KS, n // 2, c * P:(c + 1) * P],
                                   SK[a % 4][r:r + KS, n // 2, :], start=True, stop=True)
                elif kind == "shift":
                    pe.wait_ge(done["max"], nth("max", a, 15))
                    mm = pe.transpose(o[0:16, 0:P], m16[:, a % 2, :], ident[:, :])
                elif kind == "scores":
                    t, c, n = nth("scores", a, i) - 1, i // 4, i % 4
                    if i == 0:
                        pe.wait_ge(shifted[a % 2], SHIFT_IN(a))
                    if t >= SBANKS:
                        pe.wait_ge(done["scores"], t + 1 - SBANKS)
                    else:
                        pe.wait_ge(exp0, BATCH * TT)
                    r = BLK * (n % 2)
                    mm = pe.matmul(ST[t % SBANKS][:, :], SK[a % 4][r:r + KS + 1, n // 2, c * P:(c + 1) * P],
                                   SQ[a % 4][r:r + KS + 1, n // 2, :], start=True, stop=True)
                    mm.then_inc(pe_scores, 1)
                    continue
                elif kind == "av":
                    j, g = divmod(a, UNITS)
                    t = nth("av", a, i) - 1
                    if i == 0:
                        pe.wait_ge(done["v"], nth("v", j, 1))
                        if t > 0:
                            pe.wait_ge(unit_out, t // TT)
                    for n in range(4):
                        pe.wait_ge(done["scores"], 4 * t + n + 1)
                        h = 4 * g + n
                        mm = pe.matmul(AVB[32 * n:32 * n + 32, :], V[j % 2][:, i, (HD + 1) * h:(HD + 1) * h + 32],
                                       probs[:, (4 * t + n) % PROBS, :],
                                       start=(i == 0), stop=(i == TT - 1))
                    mm.then_inc(pe_av, 1)
                    continue
                elif kind == "scores0":
                    t = nth("scores0", a, i) - 1
                    if i == 0:
                        pe.wait_ge(done["q"], nth("q", a, 1))
                        pe.wait_ge(done["k"], nth("k", a, 1))
                    if t >= SBANKS:
                        pe.wait_ge(exp0, t + 1 - SBANKS)
                    for c in range(CH):
                        mm = product(ST[t % SBANKS][:, :], [x[:, c, i * P:(i + 1) * P] for x in (qh, ql)],
                                     [x[:, c, :] for x in (kh, kl)], c == 0, c == CH - 1)
                    mm.then_inc(pe_s0, 1)
                    continue
                elif kind == "pT0":
                    pe.wait_ge(done["soft0"], nth("soft0", a, i))
                    for t in range(TT):
                        mm = pe.transpose(o[:, t * P:(t + 1) * P], probs[:, i, t * P:(t + 1) * P], ident[:, :])
                elif kind == "av0":
                    pe.wait_ge(done["pT0"], nth("pT0", a, TT - 1))
                    pe.wait_ge(done["v"], nth("v", a, 1))
                    for t in range(TT):
                        mm = pe.matmul(o[:, :], V[a % 2][:, t, i * P:(i + 1) * P], oU[:, t, :],
                                       start=(t == 0), stop=(t == TT - 1))
                elif kind == "oT1":
                    pe.wait_ge(unit_out, UNITS * (a + 1 - BATCH))
                    for g in range(UNITS):
                        mm = pe.transpose(o[:, g * P:(g + 1) * P], oU[:, g, i * P:(i + 1) * P], ident[:, :])
                elif kind == "oT2":
                    pe.wait_ge(done["oT1"], nth("oT1", a, TT - 1))
                    for t in range(TT):
                        mm = pe.transpose(o[:, t * P:(t + 1) * P], tok2[:, t, i * P:(i + 1) * P], ident[:, :])
                elif kind == "proj":
                    if multi(a):
                        pe.wait_ge(done["oT2"], nth("oT2", a, CH - 1))
                    else:
                        pe.wait_ge(done["av0"], nth("av0", a, 1))
                    pe.wait_ge(done["split_wp"], nth("split_wp", layer(a)))
                    for t in range(2):
                        tok = (2 * i + t) * P
                        for c in range(CH):
                            src = [h[:, c, tok:tok + P] for h in (postT_h, postT_l)]
                            mm = product(o[:, t * DIM:(t + 1) * DIM], src, [w[:, c, :] for w in (wp_h, wp_l)],
                                         c == 0, c == CH - 1)
                elif kind == "fc1":
                    pe.wait_ge(done["hT2"], nth("hT2", a, CH - 1))
                    pe.wait_ge(done["split_w1"], nth("split_w1", layer(a), i // 2))
                    for c in range(CH):
                        mm = product(o[:, :], [w[:, c, i * P:(i + 1) * P] for w in (w1_h, w1_l)],
                                     [h[:, c, :] for h in (postT_h, postT_l)], c == 0, c == CH - 1)
                elif kind == "fc2":
                    pe.wait_ge(in_w2, 16 * (layer(a) + 1))
                    for m in range(MT):
                        if m % (MT // 2) == 0:
                            pe.wait_ge(done["gelu"], nth("gelu", a, m // (MT // 2)))
                        mm = pe.matmul(o[:, 0:DIM], gT[:, m, i * P:(i + 1) * P], w2_s[:, m, :],
                                       start=(m == 0), stop=(m == MT - 1))
                if mm is not None:
                    mm.then_inc(pe_ring, 1)

        @block.scalar
        def _(act):
            act.wait_ge(cond_in, 16)
            act.activation(condE[:, :, :], condT[:, :, :], ACT.Exp, scale=-1.0).then_inc(e_ready, 1)
            act.wait_ge(cols_in, 16)
            for kind, a, i in PLAN:
                if kind.startswith("split"):
                    hi = parts_of[kind][0]
                    n = PIECES.index((kind, a, i))
                    got = first_in[n] if a == 0 else raw_in
                    act.wait_ge(got, 16 if a == 0 else 16 * (n + 1 - len(first_in)))
                    if a > 0:
                        last = {"split_qkv": ("v", a * BATCH - 1, 1), "split_wp": ("proj", a * BATCH - 1, 1),
                                "split_w1": ("fc1", a * BATCH - 1, MT - 1)}[kind]
                        act.wait_ge(pe_ring, use(*last))
                    act.activation(hi[:, :, DIM * i:DIM * (i + 1)], piece(kind, a, i), ACT.Copy).then_inc(w_hi, 1)
                elif kind == "headscale":
                    act.wait_ge(clip_ready, 1)
                    act.activation(smrow[:, :], smrow[:, :], ACT.Exp).then_inc(done[kind], 1)
                elif kind == "modrow":
                    act.wait_ge(pe_ring, use(kind, a, i))
                    if i > 0 or a > 0:
                        act.wait_ge(pe_ring, use("mod", a, 0) if i > 0 else use("mod", a - 1, mod_rows(a - 1) - 1))
                    act.activation(mrow[:, :], bank(kind, a, i)[0:BATCH, :], ACT.Copy
                                   ).then_inc(done[kind], 1)
                elif kind in ("hT1", "hT2"):
                    l, b, second = layer(a), batch(a), kind == "hT2"
                    act.wait_ge(pe_ring, use(kind, a, i))
                    act.wait_ge(done["mod"], nth("mod", l, min(int(second), mod_rows(l) - 1)))
                    n = 2 * second + i
                    if not second and a > 0 and i == 0:
                        act.wait_ge(pe_ring, use("v", a - 1, 1))
                    if second and i == 0:
                        act.wait_ge(pe_ring, use("proj", a, 1))
                        if a > 0:
                            act.wait_ge(pe_ring, use("fc1", a - 1, MT - 1))
                    hi = postT_h if second else hT_h
                    for dst in (whole(act, kind, a, i), hi[:, i, :]):
                        ins = act.activation(dst, bank(kind, a, i)[:, :], ACT.Identity,
                                             bias=modb[:, l % 2, n, b:b + 1], scale=mods[:, l % 2, n, b:b + 1])
                    ins.then_inc(hi_in[kind], 1)
                elif kind == "v":
                    act.wait_ge(pe_ring, use(kind, a, i))
                    if i == 0 and a >= 2:
                        if multi(a - 2):
                            act.wait_ge(pe_av, nth("av", UNITS * (a - 1) - 1, TT - 1))
                        else:
                            act.wait_ge(pe_ring, use("av0", a - 2, 1))
                    src = bank(kind, a, i)
                    if multi(a):
                        if layer(a) == 1 and batch(a) < 2 and i == 0:
                            act.wait_ge(done["vones"], batch(a) + 1)
                        for t in range(2):
                            dst = V[a % 2][:, 2 * i + t, 0:VW].rearrange("p (h e) -> p h e", e=HD + 1)[:, :, 0:HD]
                            ins = act.activation(dst, src[:, t * DIM:(t + 1) * DIM].rearrange("p (h d) -> p h d", d=HD),
                                                 ACT.Copy)
                        ins.then_inc(done["v"], 1)
                    else:
                        act.activation(V[a % 2][:, 2 * i:2 * i + 2, 0:DIM],
                                       src[:, :].rearrange("p (t d) -> p t d", t=2), ACT.Copy).then_inc(done["v"], 1)
                elif kind == "qkss":
                    t = nth(kind, a, i) - 1
                    act.wait_ge(done["qktok"], t + 1)
                    if t >= 1:
                        act.wait_ge(done["qkss"], t)
                    act.activation(sq[:, :], qk[:, i, :], ACT.Square).then_inc(sq_ready, 1)
                elif kind == "qkroot":
                    act.wait_ge(ss_ready, nth(kind, a))
                    act.activation(rs[:, :, :], ss[:, :, :], ACT.Sqrt).then_inc(done[kind], 1)
                elif kind in ("q", "k"):
                    l = layer(a)
                    act.wait_ge(pe_ring, use(kind, a, i))
                    col = (C_Q if kind == "q" else C_K) + i
                    if a > BATCH:
                        for g in range(UNITS):
                            act.wait_ge(stacked[g], STACK_IN(UNITS * (a - 1) + g))
                    elif a > 0:
                        act.wait_ge(pe_s0, nth("scores0", a - 1, TT - 1))
                    hi = qh if kind == "q" else kh
                    if l == 1:
                        act.activation(hi[:, i, :], bank(kind, a, i)[:, :], ACT.Copy).then_inc(hi_ready, 1)
                    else:
                        act.activation(hi[:, i, :], bank(kind, a, i)[:, :], ACT.Identity,
                                       bias=colv[:, l, col:col + 1]).then_inc(hi_ready, 1)
                elif kind == "scores":
                    n = nth("scores", a, i) - 1
                    act.wait_ge(pe_scores, n + 1)
                    if n >= PROBS:
                        act.wait_ge(pe_av, (n - PROBS) // 4 + 1)
                    elif n == 0:
                        act.wait_ge(pe_ring, use("pT0", BATCH - 1, TT - 1))
                    act.activation(probs[:, n % PROBS, :], ST[n % SBANKS][:, :], ACT.Exp,
                                   scale=SCALE[layer(unit_job(a))]).then_inc(done["scores"], 1)
                elif kind == "scores0":
                    t = nth("scores0", a, i) - 1
                    act.wait_ge(nb_ready, t + 1)
                    if t >= TT:
                        act.wait_ge(pe_ring, use("pT0", a - 1, i))
                        act.wait_ge(done["soft0"], nth("soft0", a - 1, i))
                    act.activation(probs[:, i, :], ST[t % SBANKS][:, :], ACT.Exp, bias=nb0[:, i:i + 1],
                                   scale=SCALE[0], accum_out=sum0[:, i:i + 1]).then_inc(exp0, 1)
                elif kind == "pT0":
                    act.wait_ge(pe_ring, use(kind, a, i))
                    if a > 0:
                        act.wait_ge(pe_ring, use("av0", a - 1, 1))
                    act.activation(oU[:, :, i * P:(i + 1) * P],
                                   bank(kind, a, i)[:, :].rearrange("p (k q) -> p k q", k=TT),
                                   ACT.Copy).then_inc(done[kind], 1)
                elif kind == "av0":
                    act.wait_ge(pe_ring, use(kind, a, i))
                    if a > 0:
                        act.wait_ge(pe_ring, use("fc1", a - 1, MT - 1))
                    for dst in (whole(act, kind, a, i), postT_h[:, i, :]):
                        ins = act.activation(dst, bank(kind, a, i)[:, :], ACT.Identity,
                                             bias=colv[:, 0, C_V + i:C_V + i + 1])
                    ins.then_inc(hi_in[kind], 1)
                elif kind == "av" and i == TT - 1:
                    act.wait_ge(pe_av, nth("av", a, i))
                    j, g = divmod(a, UNITS)
                    if g == 0 and j > BATCH:
                        act.wait_ge(pe_ring, use("oT1", j - 1, TT - 1))
                    if g == 0 and j == BATCH:
                        act.wait_ge(pe_ring, use("av0", j - 1, 1))
                    act.activation(oU[:, g, :], AVB[:, :], ACT.Copy).then_inc(unit_out, 1)
                elif kind == "oT2":
                    l = layer(a)
                    act.wait_ge(pe_ring, use(kind, a, i))
                    if i == 0 and layer(a - 1) < LAYERS - 1:
                        act.wait_ge(pe_ring, use("fc1", a - 1, MT - 1))
                    elif i == 0:
                        act.wait_ge(pe_ring, use("proj", a - 1, 1))
                    for dst in (whole(act, kind, a, i), postT_h[:, i, :]):
                        ins = act.activation(dst, bank(kind, a, i)[:, :], ACT.Identity,
                                             bias=colv[:, l, C_V + i:C_V + i + 1],
                                             scale=(1.0 if l < LAYERS - 1 else DIM ** -0.5))
                    ins.then_inc(hi_in[kind], 1)
                elif kind == "gelu":
                    half = gT[:, i * MT // 2:(i + 1) * MT // 2, :]
                    act.wait_ge(done["fc1"], nth("fc1", a, (i + 1) * MT // 2 - 1))
                    act.activation(half, half, ACT.Gelu).then_inc(done[kind], 1)

        @block.vector
        def _(dve):
            n_seq = [0]

            def link(ins):
                n_seq[0] += 1
                ins.then_inc(dve_seq, 1)
                dve.wait_ge(dve_seq, n_seq[0])

            for i in range(4):
                nc.vector.memset(SK[i][:, :, :].bitcast(F32), 1.0)
            link(nc.vector.memset(mhalf[:, :], -0.5))
            dve.wait_ge(e_ready, 1)
            link(nc.vector.tensor_scalar(condR[:, :, :], condE[:, :, :], 1.0, None, ALU.add))
            link(nc.vector.reciprocal(condE[:, :, :], condR[:, :, :]))
            nc.vector.tensor_tensor(condS[:, :, :], condT[:, :, :], condE[:, :, :], ALU.mult).then_inc(cond_ready, 1)
            dve.wait_ge(cols_in, 16)

            for kind, a, i in PLAN:
                if kind == "headscale":
                    nc.vector.tensor_scalar(colv[:, LAYERS - 1, C_V:C_V + 2], colv[:, LAYERS - 1, C_V:C_V + 2],
                                            DIM ** -0.5, None, ALU.mult)
                    dve.wait_ge(rows_in, 16)
                    nc.vector.tensor_scalar(smrow[:, :], rowh[:, R_SM:R_SM + HEADS], LOG100, None, ALU.min
                                            ).then_inc(clip_ready, 1)
                elif kind == "mod":
                    l, q, n = a, a % 2, 2 * i
                    dve.wait_ge(pe_ring, use(kind, a, i))
                    if l >= 2:
                        dve.wait_ge(done["hT2"], nth("hT2", (l - 1) * BATCH - 1, CH - 1))
                    if nth(kind, a, i) > 1:
                        dve.wait_ge(done["mod"], nth(kind, a, i) - 1)
                    mb = colv[:, l, C_MB + 4 * i:C_MB + 4 * i + 4].unsqueeze(2).to_broadcast([P, 4, BATCH])
                    link(nc.vector.tensor_tensor(modr[:, :, :], bank(kind, a, i)[:, 0:4 * BATCH].rearrange(
                        "p (m b) -> p m b", b=BATCH), mb, ALU.add))
                    sc, sh = modr[:, 0:2, :], modr[:, 2:4, :]
                    g = colv[:, l, C_G + n:C_G + n + 2].unsqueeze(2).to_broadcast([P, 2, BATCH])
                    be = colv[:, l, C_BE + n:C_BE + n + 2].unsqueeze(2).to_broadcast([P, 2, BATCH])
                    if l < LAYERS - 1:
                        link(nc.vector.tensor_scalar(sc, sc, 1.0, None, ALU.add))
                    link(nc.vector.tensor_tensor(mods[:, q, n:n + 2, :], sc, g, ALU.mult))
                    link(nc.vector.tensor_tensor(sc, sc, be, ALU.mult))
                    nc.vector.tensor_tensor(modb[:, q, n:n + 2, :], sc, sh, ALU.add).then_inc(done["mod"], 1)
                elif kind == "fc1":
                    dve.wait_ge(pe_ring, use(kind, a, i))
                    if i == 0:
                        if a > 0:
                            dve.wait_ge(pe_ring, use("fc2", a - 1, TT - 1))
                        else:
                            dve.wait_ge(done["split_w1"], nth("split_w1", 0, 3))
                    col = C_B1 + i
                    nc.vector.tensor_scalar(gT[:, i, :], bank(kind, a, i)[:, :], colv[:, layer(a), col:col + 1],
                                            None, ALU.add).then_inc(done[kind], 1)
                elif kind in ("hT1", "hT2", "oT2", "av0"):
                    dve.wait_ge(hi_in[kind], nth(kind, a, i))
                    lo, hi = [x[:, i, :] for x in ((hT_l, hT_h) if kind == "hT1" else (postT_l, postT_h))]
                    nc.vector.tensor_tensor(lo, full[:, CUTS.index((kind, a, i)) % 2, :], hi.bitcast(F32),
                                            ALU.subtract).then_inc(done[kind], 1)
                elif kind == "vones":
                    dve.wait_ge(pe_ring, use("av0", a - 2, 1))
                    nc.vector.memset(V[a % 2][:, :, :], 1.0).then_inc(done[kind], 1)
                elif kind == "gate":
                    l, b = layer(a), batch(a)
                    dve.wait_ge(pe_ring, use(kind, a))
                    dve.wait_ge(in_rowg, 16 * l)
                    if a - 2 >= BATCH and layer(a - 2) < LAYERS - 1:
                        dve.wait_ge(done["fc2"], nth("fc2", a - 2, TT - 1))
                    elif a - 2 >= BATCH:
                        dve.wait_ge(done["final"], nth("final", a - 2, TT - 1))
                    nc.vector.tensor_tensor(gates[:, a % 2, :], bank(kind, a)[:, :],
                                            rowg[:, :], ALU.add
                                            ).then_inc(done["gate"], 1)
                elif kind in ("stat1", "stat2"):
                    w = int(kind == "stat2")
                    l, b = layer(a), batch(a)
                    if w:
                        dve.wait_ge(done["proj"], nth("proj", a, 1))
                    elif l == 0:
                        dve.wait_ge(x_in[b], 16)
                    else:
                        dve.wait_ge(done["fc2"], nth("fc2", a - BATCH, TT - 1))
                    for t in range(TT):
                        ins = nc.vector.bn_stats(stats[:, w, t, :], X[:, TT * b + t, :])
                    link(ins)
                    for t in range(TT):
                        ins = nc.vector.bn_aggr(mv[:, w, t, :], stats[:, w, t, :])
                    if l == 0:
                        link(ins)
                        link(nc.vector.tensor_tensor(var[:, w, :], mv[:, w, :, 0], mv[:, w, :, 0], ALU.mult))
                        ins = nc.vector.tensor_tensor(var[:, w, :], var[:, w, :], mv[:, w, :, 1], ALU.add)
                    ins.then_inc(done[kind], 1)
                elif kind == "norm1" and not multi(a):
                    dve.wait_ge(rstd1, nth(kind, a))
                    if a > 0:
                        dve.wait_ge(pe_ring, use("hT1", a - 1, CH - 1))
                    for t in range(TT):
                        ins = nc.vector.tensor_scalar(tok1[:, t, :], X[:, TT * batch(a) + t, :], rstd[:, 0, t:t + 1],
                                                      None, ALU.mult)
                    ins.then_inc(done[kind], 1)
                elif kind == "norm2":
                    l, b = layer(a), batch(a)
                    dve.wait_ge(rstd2, nth(kind, a))
                    if multi(a):
                        dve.wait_ge(pe_ring, use("oT2", a, CH - 1))
                    elif a > 0:
                        dve.wait_ge(pe_ring, use("hT2", a - 1, CH - 1))
                    for t in range(TT):
                        if l == 0:
                            ins = nc.vector.tensor_scalar(tok2[:, t, :], X[:, TT * b + t, :], rstd[:, 1, t:t + 1],
                                                          None, ALU.mult)
                        else:
                            ins = nc.vector.tensor_scalar(tok2[:, t, :], X[:, TT * b + t, :], mv[:, 1, t, 0:1],
                                                          rstd[:, 1, t:t + 1], ALU.subtract, ALU.mult)
                    ins.then_inc(done[kind], 1)
                elif kind == "final" and a == JOBS - 1 and i % 2:
                    b, t = batch(a), tok2[:, i, :]
                    if i == 1:
                        dve.wait_ge(done["norm2"], nth("norm2", a))
                        dve.wait_ge(gates_ready, 4)
                    link(nc.vector.tensor_tensor(t, t, gates[:, a % 2, 0:DIM], ALU.mult))
                    link(nc.vector.tensor_tensor(t, t, gates[:, a % 2, DIM:2 * DIM], ALU.add))
                    nc.vector.tensor_tensor(t, t, X[:, TT * b + i, :], ALU.add).then_inc(final_dve, 1)
                elif kind == "qktok":
                    dve.wait_ge(pe_ring, use(kind, a, i))
                    if a > BATCH:
                        dve.wait_ge(pe_ring, use("k", a - 1, 1))
                    nc.vector.tensor_tensor(qk[:, i, :], bank(kind, a, i)[:, :], rowh[:, R_QK:R_QK + TOK],
                                            ALU.add).then_inc(done[kind], 1)
                elif kind == "qkss":
                    t = nth(kind, a, i) - 1
                    dve.wait_ge(sq_ready, t + 1)
                    if a > BATCH and i == 0:
                        dve.wait_ge(done["qkroot"], nth("qkroot", a - 1))
                    nc.vector.tensor_reduce(ss[:, i, :], sq[:, :].rearrange("p (h d) -> p h d", d=HD),
                                            AX_X, ALU.add).then_inc(done[kind], 1)
                elif kind == "qkroot":
                    dve.wait_ge(done["qkss"], nth("qkss", a, TT - 1))
                    nc.vector.tensor_scalar(ss[:, :, :], ss[:, :, :], 1e-24, None, ALU.max).then_inc(ss_ready, 1)
                elif kind == "qkrs":
                    dve.wait_ge(done["qkroot"], nth("qkroot", a))
                    link(nc.vector.reciprocal(rs[:, :, :], rs[:, :, :]))
                    dve.wait_ge(done["headscale"], 1)
                    nc.vector.tensor_tensor(rs[:, :, 0:HEADS], rs[:, :, 0:HEADS],
                                            smrow[:, :].unsqueeze(1).to_broadcast([P, TT, HEADS]), ALU.mult
                                            ).then_inc(done[kind], 1)
                elif kind == "qknorm":
                    dve.wait_ge(done["qkrs"], nth("qkrs", a))
                    r = rs[:, i, :].unsqueeze(2).to_broadcast([P, 2 * HEADS, HD])
                    v = qk[:, i, :].rearrange("p (h d) -> p h d", d=HD)
                    nc.vector.tensor_tensor(v, v, r, ALU.mult).then_inc(done[kind], 1)
                elif kind in ("q", "k"):
                    l = layer(a)
                    col = (C_Q if kind == "q" else C_K) + i
                    hi, lo = (qh, ql) if kind == "q" else (kh, kl)
                    dve.wait_ge(hi_ready, (nth(kind, a, i) - 1) * 2 + 1 + (kind == "k"))
                    if l == 1:
                        nc.vector.tensor_tensor(lo[:, i, :], bank(kind, a, i)[:, :], hi[:, i, :].bitcast(F32),
                                                ALU.subtract).then_inc(done[kind], 1)
                    else:
                        nc.vector.scalar_tensor_tensor(out=lo[:, i, :], in0=bank(kind, a, i)[:, :],
                                                       scalar=colv[:, l, col:col + 1], in1=hi[:, i, :].bitcast(F32),
                                                       op0=ALU.add, op1=ALU.subtract).then_inc(done[kind], 1)
                elif kind == "max":
                    n, c = i % 4, i // 4
                    col = ((n % 2) * 2 + n // 2) * TT + c
                    dve.wait_ge(pe_ring, use(kind, a, i))
                    if i == 0 and a - 2 >= UNITS * BATCH:
                        dve.wait_ge(pe_ring, use("shift", a - 2))
                    nc.vector.tensor_reduce(m16[:, a % 2, col:col + 1], bank(kind, a, i)[:, :], AX_X, ALU.max,
                                            negate=True).then_inc(done["max"], 1)
                elif kind == "shift":
                    dve.wait_ge(pe_ring, use(kind, a))
                    if a - 2 >= UNITS * BATCH:
                        dve.wait_ge(shifted[a % 2], SHIFT_IN(a - 2))
                    r = 32 * (a % 2)
                    nc.vector.tensor_copy(cT[r:r + 16, :], bank(kind, a)[0:16, 0:P]).then_inc(done["shift"], 1)
                elif kind == "scores0":
                    t = nth(kind, a, i) - 1
                    dve.wait_ge(pe_s0, t + 1)
                    if t >= TT:
                        dve.wait_ge(exp0, t + 1 - TT)
                    link(nc.vector.tensor_reduce(nm0[:, i:i + 1], ST[t % SBANKS][:, :], AX_X, ALU.max, negate=True))
                    nc.vector.tensor_scalar(nb0[:, i:i + 1], nm0[:, i:i + 1], SCALE[0], None, ALU.mult
                                            ).then_inc(nb_ready, 1)
                elif kind == "soft0":
                    dve.wait_ge(exp0, nth(kind, a, i))
                    link(nc.vector.reciprocal(rc0[:, i:i + 1], sum0[:, i:i + 1]))
                    nc.vector.tensor_scalar(probs[:, i, :], probs[:, i, :], rc0[:, i:i + 1], None,
                                            ALU.mult).then_inc(done["soft0"], 1)
                elif kind == "oT1":
                    dve.wait_ge(pe_ring, use(kind, a, i))
                    if i == 0 and layer(a - 1) < LAYERS - 1:
                        dve.wait_ge(pe_ring, use("hT2", a - 1, CH - 1))
                    elif i == 0:
                        dve.wait_ge(out_sem, 16 * nth("final", a - 1, TT - 1))
                    b = bank(kind, a, i)[:, :].rearrange("p (h e) -> p h e", e=32)
                    link(nc.vector.reciprocal(rcp[:, i % 2, :], b[:, :, HD]))
                    nc.vector.tensor_tensor(tok2[:, i, :].rearrange("p (h d) -> p h d", d=HD), b[:, :, 0:HD],
                                            rcp[:, i % 2, :].unsqueeze(2).to_broadcast([P, HEADS, HD]), ALU.mult
                                            ).then_inc(done[kind], 1)
                elif kind in ("proj", "fc2"):
                    l = layer(a)
                    dve.wait_ge(pe_ring, use(kind, a, i))
                    for step in TMP_BEFORE[(kind, a, i)]:
                        dve.wait_ge(done[step[0]], nth(*step))
                    off = R_PB if kind == "proj" else R_FB
                    dve.wait_ge(in_rowp, 16 * (l + 1))
                    if kind == "proj":
                        nc.vector.tensor_tensor(tmp[:, 2 * i:2 * i + 2, :],
                                                bank(kind, a, i)[:, :].rearrange("p (t d) -> p t d", t=2),
                                                rowp[:, off:off + DIM].unsqueeze(1).to_broadcast([P, 2, DIM]), ALU.add
                                                ).then_inc(y1, 1)
                    else:
                        nc.vector.tensor_tensor(tmp[:, i, :], bank(kind, a, i)[:, 0:DIM], rowp[:, off:off + DIM],
                                                ALU.add).then_inc(y2, 1)

        @block.gpsimd
        def _(pool):
            n_seq = [0]

            def link(ins):
                n_seq[0] += 1
                ins.then_inc(pool_seq, 1)
                pool.wait_ge(pool_seq, n_seq[0])

            link(nc.gpsimd.memset(ident[:, :], 0.0))
            pool.wait_ge(dve_seq, 1)
            nc.gpsimd.affine_select(out=ident[:, :], in_=ident[:, :], compare_op=ALU.not_equal, fill=1.0, base=0,
                                    pattern=[[-1, P]], channel_multiplier=1).then_inc(const_ready, 1)
            for kind, a, i in PLAN:
                if kind.startswith("split"):
                    hi, lo = [w[:, :, DIM * i:DIM * (i + 1)] for w in parts_of[kind]]
                    pool.wait_ge(w_hi, PIECES.index((kind, a, i)) + 1)
                    nc.gpsimd.tensor_tensor(lo, piece(kind, a, i), hi.bitcast(F32), ALU.subtract
                                            ).then_inc(done[kind], 1)
                elif kind in ("stat1", "stat2"):
                    w, l = int(kind == "stat2"), layer(a)
                    pool.wait_ge(done[kind], nth(kind, a))
                    src = var[:, w, :] if l == 0 else mv[:, w, :, 1]
                    if a > 0:
                        pool.wait_ge(done["norm2" if w else "norm1"], nth("norm2" if w else "norm1", a - 1))
                    link(nc.gpsimd.tensor_scalar(rstd[:, w, :], src, EPS[l], None, ALU.add))
                    nc.gpsimd.tensor_tensor(rstd[:, w, :], rstd[:, w, :], mhalf[:, 0:TT], ALU.pow
                                            ).then_inc(rstd2 if w else rstd1, 1)
                elif kind == "norm1" and multi(a):
                    pool.wait_ge(rstd1, nth(kind, a))
                    pool.wait_ge(pe_ring, use("hT1", a - 1, CH - 1))
                    pool.wait_ge(done[kind], nth(kind, a) - 1)
                    for t in range(TT):
                        ins = nc.gpsimd.tensor_scalar(tok1[:, t, :], X[:, TT * batch(a) + t, :], mv[:, 0, t, 0:1],
                                                      rstd[:, 0, t:t + 1], ALU.subtract, ALU.mult)
                    ins.then_inc(done[kind], 1)
                elif kind in ("proj", "fc2"):
                    l, b = layer(a), batch(a)
                    n, t = (2, 2 * i) if kind == "proj" else (1, i)
                    pool.wait_ge(y1 if kind == "proj" else y2, nth(kind, a, i))
                    y = tmp[:, t:t + n, :]
                    if l in (1, 2):
                        pool.wait_ge(done["gate"], nth("gate", a))
                        off = 0 if kind == "proj" else DIM
                        g = gates[:, a % 2, off:off + DIM].unsqueeze(1).to_broadcast([P, n, DIM])
                        link(nc.gpsimd.tensor_tensor(y, y, g, ALU.mult))
                    xs = X[:, TT * b + t:TT * b + t + n, :]
                    if kind == "proj":
                        pool.wait_ge(done["norm1"], nth("norm1", a))
                    else:
                        pool.wait_ge(done["norm2"], nth("norm2", a))
                    nc.gpsimd.tensor_tensor(xs, xs, y, ALU.add).then_inc(done[kind], 1)
                elif kind == "gate" and layer(a) == LAYERS - 1:
                    pool.wait_ge(done["gate"], nth("gate", a))
                    gm, bt = gates[:, a % 2, 0:DIM], gates[:, a % 2, DIM:2 * DIM]
                    if batch(a) > 0:
                        pool.wait_ge(gates_ready, batch(a))
                    else:
                        pool.wait_ge(in_rowp, 16 * LAYERS)
                    link(nc.gpsimd.tensor_tensor(sq[:, 0:DIM], gm, rowp[:, R_LB:R_LB + DIM], ALU.mult))
                    nc.gpsimd.tensor_tensor(gm, gm, rowp[:, R_FB:R_FB + DIM], ALU.mult)
                    nc.gpsimd.tensor_tensor(bt, bt, sq[:, 0:DIM], ALU.add).then_inc(gates_ready, 1)
                elif kind == "final":
                    if a == JOBS - 1 and i % 2:
                        continue
                    l, b = layer(a), batch(a)
                    pool.wait_ge(done["norm2"], nth("norm2", a))
                    t = tok2[:, i, :]
                    pool.wait_ge(gates_ready, b + 1)
                    link(nc.gpsimd.tensor_tensor(t, t, gates[:, a % 2, 0:DIM], ALU.mult))
                    link(nc.gpsimd.tensor_tensor(t, t, gates[:, a % 2, DIM:2 * DIM], ALU.add))
                    nc.gpsimd.tensor_tensor(t, t, X[:, TT * b + i, :], ALU.add).then_inc(done["final"], 1)


LOG100 = 4.605170185988092


def kernel(**inputs):
    import numpy as np
    import concourse.bacc as bacc
    from concourse.bass_utils import run_bass_kernel_spmd

    g = {k: np.asarray(v) for k, v in inputs.items()}
    one, zero = np.ones(DIM, np.float32), np.zeros(DIM, np.float32)

    def regroup(w):
        return w.reshape(HEADS, HD, 3, -1).transpose(2, 0, 1, 3).reshape(3 * DIM, -1)

    def parts(w, order):
        return np.concatenate([w[..., DIM * n:DIM * (n + 1)] for n in order], axis=-1)

    def by_unit(w, blocks):
        out = [w[..., DIM * n:DIM * (n + 1)] for n in range(w.shape[-1] // DIM)]
        for n in range(blocks):
            v = out[n].reshape(-1, UNITS, 2, 2, HD).transpose(0, 2, 1, 3, 4)
            out[n] = v.reshape(w.shape[:-1] + (DIM,))
        return np.concatenate(out, axis=-1)

    wqkv = np.stack([
        np.concatenate([g["L0_cond_q_w"], g["L0_cond_k_w"], g["L0_cond_v_w"]], axis=1),
        by_unit(g["L1_cond_mat_qkv_w"].T, 2), by_unit(g["L2_cond_Wqkv"], 2), by_unit(regroup(g["L3_cond_Wqkv"]).T, 2)])
    wp = np.stack([g["L0_cond_proj_w"], g["L1_cond_proj_w"].T, g["L2_cond_Wproj"], g["L3_cond_Wp"].T])
    w1 = np.stack([g["L0_cond_mlp_w1"], g["L1_cond_fc1_w"].T, g["L2_cond_W1"]])
    w2 = np.stack([g["L0_cond_mlp_w2"], g["L1_cond_fc2_w"].T, g["L2_cond_W2"]])
    ada1, adab1 = g["L1_cond_ada_w"].T, g["L1_cond_ada_b"]
    ada2, adab2 = g["L2_cond_Wt"], g["L2_cond_bt"]
    film3 = np.concatenate([g["L3_cond_Wg"].T, g["L3_cond_Wb"].T], axis=1)
    filmb3 = np.concatenate([g["L3_cond_bg"], g["L3_cond_bb"]])
    film0 = np.concatenate([g["L0_cond_film1_w"], g["L0_cond_film2_w"]], axis=1)
    filmb0 = np.concatenate([g["L0_cond_film1_b"], g["L0_cond_film2_b"]])
    wmod = np.stack([film0, parts(ada1, (2, 4, 3, 5)), parts(ada2, (1, 0, 4, 3)),
                     np.concatenate([film3, film3], axis=1)])
    modbias = [filmb0, parts(adab1, (2, 4, 3, 5)), parts(adab2, (1, 0, 4, 3)), np.concatenate([filmb3, filmb3])]
    wgate = np.stack([parts(ada1, (0, 1)), parts(ada2, (2, 5)), film3])
    gatebias = [parts(adab1, (0, 1)), parts(adab2, (2, 5)), filmb3]
    b3 = regroup(g["L3_cond_bqkv"])[:, 0]
    bqkv = [np.concatenate([g["L0_cond_q_b"], g["L0_cond_k_b"], g["L0_cond_v_b"]]),
            np.concatenate([g["L1_cond_q_bias"], zero, g["L1_cond_v_bias"]]), by_unit(g["L2_cond_bqkv"], 2), by_unit(b3, 2)]
    b1 = [g["L0_cond_mlp_b1"], g["L1_cond_fc1_b"], g["L2_cond_b1"], np.zeros(HID, np.float32)]
    ga = [(g["L0_cond_norm1_w"], g["L0_cond_norm2_w"], zero, zero), (one, one, zero, zero),
          (g["L2_cond_g1"], g["L2_cond_g2"], g["L2_cond_be1"], g["L2_cond_be2"]),
          (g["L3_cond_ln_g"], g["L3_cond_ln_g"], g["L3_cond_ln_b"], g["L3_cond_ln_b"])]
    cols = np.stack([np.concatenate([bqkv[l], b1[l], modbias[l], *ga[l]]).reshape(N_COL, P).T
                     for l in range(LAYERS)], axis=1)
    lb = [zero, zero, zero, g["L3_cond_ln_b"]]
    pb = [g["L0_cond_proj_b"], g["L1_cond_proj_b"], g["L2_cond_bproj"], g["L3_cond_bp"]]
    fb = [g["L0_cond_mlp_b2"], g["L1_cond_fc2_b"], g["L2_cond_b2"], g["L3_cond_ln_g"]]
    gb = [np.concatenate([zero, zero]), *gatebias]
    rows = np.concatenate([v for l in range(LAYERS) for v in (pb[l], fb[l], lb[l], gb[l])] + [
        by_unit(g["L1_cond_q_bias"], 1), zero,
        g["L1_cond_scale_mul"].reshape(UNITS, 2, 2).transpose(1, 0, 2).reshape(-1)])
    host = {"x": g["x"], "cond": g["cond_1024"].T, "cols": cols, "rows": rows, "wqkv": wqkv, "wp": wp,
            "w1": w1, "w2": w2, "wmod": wmod, "wgate": wgate}

    nc = bacc.Bacc("TRN2", target_bir_lowering=False, num_devices=1, dynamic_dma_scratch_size=4096)
    arrays, args = {}, []
    for name, a in host.items():
        a = np.ascontiguousarray(a)
        arrays[f"in_{name}"] = a
        args.append(nc.dram_tensor(f"in_{name}", a.shape, mybir.dt.from_np(a.dtype), kind="ExternalInput").ap())
    out = nc.dram_tensor("out", (BATCH, TOK, DIM), F32, kind="ExternalOutput").ap()
    cond_blocks_kernel(nc, *args, out)
    r = run_bass_kernel_spmd(nc, [arrays], core_ids=[0])
    return r.results[0]["out"]
```
